# Optimizing a Trainium2 kernel written in Bass

```python
import numpy as np
import jax
import jax.numpy as jnp

def _softmax(x, axis=-1):
    return jax.nn.softmax(x, axis=axis)

def _gelu(x):
    return jax.nn.gelu(x, approximate=True)

def _silu(x):
    return jax.nn.silu(x)

def _sigmoid(x):
    return jax.nn.sigmoid(x)

def _layernorm(x, axis=-1, eps=1e-05):
    m = jnp.mean(x, axis=axis, keepdims=True)
    v = jnp.var(x, axis=axis, keepdims=True)
    return (x - m) / jnp.sqrt(v + eps)

def _scatter_add(tgt, idx, src, axis=0):
    return tgt.at[idx].add(src)

def _segment_sum(src, seg, n):
    return jax.ops.segment_sum(src, seg, n)
kernel_name = 'mk_macaron_d1_jaxref_r4_fe6fb5'

def setup_inputs(seed: int=0):
    np.random.seed(seed)
    _w = jnp.asarray

    def _L0_attn_setup():
        import jax, jax.numpy as jnp
        from jax import lax
        import numpy as np
        D_MODEL = 512
        D_STATE = 128
        D_CONV = 4
        EXPAND = 2
        HEADDIM = 64
        NGROUPS = 1
        D_INNER = EXPAND * D_MODEL
        D_SSM = D_INNER
        NHEADS = D_SSM // HEADDIM
        CONV_DIM = D_SSM + 2 * NGROUPS * D_STATE
        D_IN_PROJ = 2 * D_INNER + 2 * NGROUPS * D_STATE + NHEADS
        BATCH = 2
        SEQLEN = 512
        EPS = 1e-05

        def _silu(x):
            return x * jax.nn.sigmoid(x)
        key = jax.random.key(seed)
        ks = jax.random.split(key, 8)
        u = jax.random.normal(ks[0], (BATCH, SEQLEN, D_MODEL), jnp.float32)
        W_in = jax.random.normal(ks[1], (D_IN_PROJ, D_MODEL), jnp.float32) * 0.02
        conv_w = jax.random.normal(ks[2], (CONV_DIM, 1, D_CONV), jnp.float32) * 0.2
        conv_b = jax.random.normal(ks[3], (CONV_DIM,), jnp.float32) * 0.02
        dt = jnp.exp(jax.random.uniform(ks[4], (NHEADS,)) * (jnp.log(0.1) - jnp.log(0.001)) + jnp.log(0.001))
        dt_bias = dt + jnp.log(-jnp.expm1(-dt))
        A_log = jnp.log(jax.random.uniform(ks[5], (NHEADS,), minval=1.0, maxval=16.0))
        D = jnp.ones((NHEADS,), jnp.float32)
        norm_w = jnp.ones((D_SSM,), jnp.float32)
        W_out = jax.random.normal(ks[6], (D_MODEL, D_INNER), jnp.float32) * 0.02
        return dict(u=u, W_in=W_in, conv_w=conv_w, conv_b=conv_b, dt_bias=dt_bias, A_log=A_log, D=D, norm_w=norm_w, W_out=W_out)
    _L0_attn_in = _L0_attn_setup()

    def _L0_ffn_setup():
        import jax, jax.numpy as jnp
        import numpy as np
        E = 8
        TOP_K = 2
        D = 512
        DE = 352
        DS = 704
        B, S = (2, 512)
        key = jax.random.key(seed)
        ks = jax.random.split(key, 8)
        std = 0.02
        return {'x': jax.random.normal(ks[0], (B, S, D), jnp.float32), 'W_router': jax.random.normal(ks[1], (D, E), jnp.float32) * std, 'We_gate': jax.random.normal(ks[2], (E, D, DE), jnp.float32) * std, 'We_up': jax.random.normal(ks[3], (E, D, DE), jnp.float32) * std, 'We_down': jax.random.normal(ks[4], (E, DE, D), jnp.float32) * std, 'Ws_gate': jax.random.normal(ks[5], (D, DS), jnp.float32) * std, 'Ws_up': jax.random.normal(ks[6], (D, DS), jnp.float32) * std, 'Ws_down': jax.random.normal(ks[7], (DS, D), jnp.float32) * std}
    _L0_ffn_in = _L0_ffn_setup()
    _d = {'L0_attn_u': _L0_attn_in['u'], 'L0_attn_W_in': _L0_attn_in['W_in'], 'L0_attn_conv_w': _L0_attn_in['conv_w'], 'L0_attn_conv_b': _L0_attn_in['conv_b'], 'L0_attn_dt_bias': _L0_attn_in['dt_bias'], 'L0_attn_A_log': _L0_attn_in['A_log'], 'L0_attn_D': _L0_attn_in['D'], 'L0_attn_norm_w': _L0_attn_in['norm_w'], 'L0_attn_W_out': _L0_attn_in['W_out'], 'L0_ffn_W_router': _L0_ffn_in['W_router'], 'L0_ffn_We_gate': _L0_ffn_in['We_gate'], 'L0_ffn_We_up': _L0_ffn_in['We_up'], 'L0_ffn_We_down': _L0_ffn_in['We_down'], 'L0_ffn_Ws_gate': _L0_ffn_in['Ws_gate'], 'L0_ffn_Ws_up': _L0_ffn_in['Ws_up'], 'L0_ffn_Ws_down': _L0_ffn_in['Ws_down']}
    _x0 = _d['L0_attn_u']
    _d['L0_attn_u'] = jax.random.normal(jax.random.fold_in(jax.random.key(seed), 1), (2, 1024, 512), dtype=_x0.dtype)
    del _x0
    return _d

def reference(L0_attn_u, L0_attn_W_in, L0_attn_conv_w, L0_attn_conv_b, L0_attn_dt_bias, L0_attn_A_log, L0_attn_D, L0_attn_norm_w, L0_attn_W_out, L0_ffn_W_router, L0_ffn_We_gate, L0_ffn_We_up, L0_ffn_We_down, L0_ffn_Ws_gate, L0_ffn_Ws_up, L0_ffn_Ws_down):

    def _L0_attn_ref(u, W_in, conv_w, conv_b, dt_bias, A_log, D, norm_w, W_out):
        import jax, jax.numpy as jnp
        from jax import lax
        import numpy as np
        D_MODEL = 512
        D_STATE = 128
        D_CONV = 4
        EXPAND = 2
        HEADDIM = 64
        NGROUPS = 1
        D_INNER = EXPAND * D_MODEL
        D_SSM = D_INNER
        NHEADS = D_SSM // HEADDIM
        CONV_DIM = D_SSM + 2 * NGROUPS * D_STATE
        D_IN_PROJ = 2 * D_INNER + 2 * NGROUPS * D_STATE + NHEADS
        BATCH = 2
        SEQLEN = 512
        EPS = 1e-05

        def _silu(x):
            return x * jax.nn.sigmoid(x)
        batch, seqlen, _ = u.shape
        zxbcdt = jnp.einsum('bld,ed->ble', u, W_in)
        z = zxbcdt[..., :D_SSM]
        xBC = zxbcdt[..., D_SSM:D_SSM + CONV_DIM]
        dt = zxbcdt[..., D_SSM + CONV_DIM:]
        xc = lax.conv_general_dilated(xBC.transpose(0, 2, 1), conv_w, window_strides=(1,), padding=[(D_CONV - 1, 0)], feature_group_count=CONV_DIM, dimension_numbers=('NCH', 'OIH', 'NCH'))
        xBC = _silu((xc + conv_b[None, :, None]).transpose(0, 2, 1))
        x = xBC[..., :D_SSM]
        Bm = xBC[..., D_SSM:D_SSM + NGROUPS * D_STATE]
        Cm = xBC[..., D_SSM + NGROUPS * D_STATE:]
        A = -jnp.exp(A_log)
        dt_s = jax.nn.softplus(dt + dt_bias)
        dA = jnp.exp(dt_s * A)
        xh = x.reshape(batch, seqlen, NHEADS, HEADDIM)

        def step(state, inp):
            dA_t, dt_t, B_t, C_t, x_t = inp
            dB = dt_t[:, :, None] * B_t[:, None, :]
            state = dA_t[:, :, None, None] * state + x_t[..., None] * dB[:, :, None, :]
            y = jnp.einsum('bn,bhpn->bhp', C_t, state)
            return (state, y)
        state0 = jnp.zeros((batch, NHEADS, HEADDIM, D_STATE), u.dtype)
        xs = (dA.transpose(1, 0, 2), dt_s.transpose(1, 0, 2), Bm.transpose(1, 0, 2), Cm.transpose(1, 0, 2), xh.transpose(1, 0, 2, 3))
        _, ys = lax.scan(step, state0, xs)
        y = ys.transpose(1, 0, 2, 3) + xh * D[None, None, :, None]
        y = y.reshape(batch, seqlen, D_SSM)
        yg = y * _silu(z)
        yn = yg * lax.rsqrt(jnp.mean(yg * yg, axis=-1, keepdims=True) + EPS) * norm_w
        return jnp.einsum('bld,ed->ble', yn, W_out)

    def _L0_ffn_ref(x, W_router, We_gate, We_up, We_down, Ws_gate, Ws_up, Ws_down):
        import jax, jax.numpy as jnp
        import numpy as np
        E = 8
        TOP_K = 2
        D = 512
        DE = 352
        DS = 704
        B, S = (2, 512)
        b, s, d = x.shape
        shared = jax.nn.silu(x @ Ws_gate) * (x @ Ws_up) @ Ws_down
        scores = jax.nn.softmax(x @ W_router, axis=-1)
        topk_vals, topk_idx = jax.lax.top_k(scores, TOP_K)
        onehot = jax.nn.one_hot(topk_idx, E, dtype=x.dtype)
        combine = jnp.einsum('bsk,bske->bse', topk_vals, onehot)
        combine = combine.reshape(b * s, E)
        xf = x.reshape(b * s, d)
        h = jax.nn.silu(jnp.einsum('td,edh->eth', xf, We_gate)) * jnp.einsum('td,edh->eth', xf, We_up)
        y_all = jnp.einsum('eth,ehd->etd', h, We_down)
        routed = jnp.einsum('etd,te->td', y_all, combine)
        return routed.reshape(b, s, d) + shared
    x = L0_attn_u
    x = x + 0.5 * _L0_ffn_ref(_layernorm(x, axis=-1), L0_ffn_W_router, L0_ffn_We_gate, L0_ffn_We_up, L0_ffn_We_down, L0_ffn_Ws_gate, L0_ffn_Ws_up, L0_ffn_Ws_down)
    x = x + _L0_attn_ref(_layernorm(x, axis=-1), L0_attn_W_in, L0_attn_conv_w, L0_attn_conv_b, L0_attn_dt_bias, L0_attn_A_log, L0_attn_D, L0_attn_norm_w, L0_attn_W_out)
    x = x + 0.5 * _L0_ffn_ref(_layernorm(x, axis=-1), L0_ffn_W_router, L0_ffn_We_gate, L0_ffn_We_up, L0_ffn_We_down, L0_ffn_Ws_gate, L0_ffn_Ws_up, L0_ffn_Ws_down)
    return x

_drawn_inputs = setup_inputs


def setup_inputs(seed=0):
    import zlib

    import numpy as np

    out = dict(_drawn_inputs(seed))
    spreads = {'L0_attn_D': (1.0, 0.2), 'L0_attn_norm_w': (1.0, 0.2)}
    factors = {'L0_attn_dt_bias': 8.0,
     'L0_attn_A_log': 8.0,
     'L0_ffn_W_router': 6.869,
     'L0_ffn_We_gate': 6.042,
     'L0_ffn_We_up': 5.897,
     'L0_ffn_We_down': 5.876}
    for name, (base, spread) in spreads.items():
        noise = np.random.default_rng([zlib.crc32(name.encode()), seed]).standard_normal(out[name].shape)
        drawn = base * np.exp(spread * noise) if base else spread * noise
        out[name] = jnp.asarray(drawn.astype(out[name].dtype))
    for name, factor in factors.items():
        out[name] = (out[name] * factor).astype(out[name].dtype)
    return out
```

```python
import concourse.bass as bass
from concourse import mybir


P = 128
D = 512
KD = D // P
TOK = 2048
NT = TOK // P
NB = 4
TB = NT // NB
BATCH = 2
BPB = NB // BATCH
TPB = NT // BATCH
NE = 8
FE = 352
NS = 2
NX = NE + NS
FCH = [(0, 128), (128, 128), (256, 96)]
NF = len(FCH)
HEADS = 16
HD = 64
DI = HEADS * HD
KI = DI // P
NCH = 10
TAPS = 4
WU = 256
NWU = 9
HG = 4
GH = HEADS // HG
EPS = 1e-5
ROUTE = 0.5
DECAY_FLOOR = -120.0
MASKED = -30000.0
HALVES = [(0, 0), (0, 1), (1, 0)]
LOG1P = [1.0 / (2 * k + 1) for k in range(1, 9)]
PLAN = ("ffn", "mixer", "ffn")


class Chain:

    def __init__(self, eng, sem):
        self.eng, self.sem, self.count, self.turn = eng, sem, 0, 0

    def mark(self, ins):
        ins.then_inc(self.sem, 1)
        self.count += 1

    def join(self):
        self.eng.wait_ge(self.sem, self.turn + self.count)

    def step(self, ins):
        self.mark(ins)
        self.join()

    def enter(self, i, per_turn):
        self.turn, self.start, self.per_turn = i * per_turn, self.count, per_turn

    def leave(self, turns):
        assert self.count - self.start == self.per_turn, self.count - self.start
        self.count += (turns - 1) * self.per_turn
        self.turn = 0


def program(nc, x, w_router, w_gate, w_up, w_down, w_in, w_dt, conv, heads, norm_w, w_out, out):
    F, R, B16, U32 = mybir.dt.float32, mybir.dt.float32r, mybir.dt.bfloat16, mybir.dt.uint32
    ACT, ALU, AX = mybir.ActivationFunctionType, mybir.AluOpType, mybir.AxisListType

    def sb(name, shape, dt=F):
        return nc.alloc_sbuf_tensor(name, shape, dt)

    def sem(name):
        return nc.alloc_semaphore(name)

    def each(ap, n):
        return ap.rearrange("p (a o) -> p a o", o=1).broadcast_to([P, ap.shape[1], n])

    def some(ap, n):
        return ap.rearrange("p (o a) -> p o a", o=1).broadcast_to([P, n, ap.shape[1]])

    X = sb("X", [P, NT, D])
    ident = sb("ident", [P, P])
    comb = sb("comb", [P, NT, NX])
    iota8 = sb("iota8", [P, NE])
    stats = sb("stats", [P, NT, 6])
    mv = sb("mv", [P, NT, 2])
    rstd = sb("rstd", [P, NT])
    mhalf = sb("mhalf", [P, NT])
    spare = sb("spare", [P, 1])
    spare2 = sb("spare2", [P, 3])
    zero = sb("zero", [P, 1])
    eps = sb("eps", [P, 1])
    by_di = sb("by_di", [P, 1])
    wr = sb("wr", [P, KD, NE])
    r_a = sb("r_a", [P, NT, NE])
    r_b = sb("r_b", [P, NT, NE])
    r_top = sb("r_top", [P, NT, NE])
    r_idx = sb("r_idx", [P, NT, NE], U32)
    r_1 = sb("r_1", [P, NT])
    r_2 = sb("r_2", [P, NT])
    cw = sb("cw", [P, NCH, TAPS + 1])
    hp = sb("hp", [P, 3 * HEADS])
    nw = sb("nw", [P, KI])
    negA = sb("negA", [P, HEADS])
    tri = sb("tri", [P, P])
    tri_b = sb("tri_b", [P, P], B16)
    ones_b = sb("ones_b", [P, P], B16)
    ident_b = sb("ident_b", [P, P], B16)
    mask_b = sb("mask_b", [P, P], B16)

    arena = nc.sbuf_base

    def placer():
        at = [(arena + 63) // 64 * 64]

        def place(name, shape, dt=F):
            size = {F: 4, R: 4, U32: 4, B16: 2}[dt]
            for n in shape[1:]:
                size *= n
            t = nc.alloc_sbuf_tensor_at(name, shape, dt, offset=at[0])
            at[0] += (size + 63) // 64 * 64
            return t
        return place

    ff = placer()
    xT = ff("xT", [P, 2, KD, TOK], R)
    g_raw = ff("g_raw", [P, KD, FE])
    u_raw = ff("u_raw", [P, KD, FE])
    d_raw = ff("d_raw", [P, NF, D])
    g_hl = ff("g_hl", [P, 2, 2, KD, FE], R)
    u_hl = ff("u_hl", [P, 2, 2, KD, FE], R)
    d_hl = ff("d_hl", [P, 2, 2, NF, D], R)
    gate = ff("gate", [P, 2, D])
    hT = ff("hT", [P, 2, NF, D], R)
    xn_f = gate

    mx = placer()
    xb = mx("xb", [P, 2, KD, D], R)
    w_raw = mx("w_raw", [P, 2, KD, WU])
    w_hl = mx("w_hl", [P, 2, 2, KD, WU], R)
    wdt = mx("wdt", [P, KD, HEADS])
    wo = mx("wo", [P, 2, KI, D], R)
    xn_m = mx("xn_m", [P, 2, D])
    pre = mx("pre", [P, 2, TAPS - 1 + D])
    halo = mx("halo", [P, NCH, TAPS - 1])
    acc = mx("acc", [P, 2, D])
    xc = mx("xc", [P, NCH, D])
    zs = mx("zs", [P, TB, DI])
    S = mx("S", [P, DI])
    L = mx("L", [P, HEADS, P])
    xdt = mx("xdt", [P, DI])
    xw = mx("xw", [P, DI])
    xD = mx("xD", [P, DI])
    GB = mx("GB", [P, 2 * P])
    Bt = GB[:, P:2 * P]
    y = mx("y", [P, 2, DI])
    ysq = mx("ysq", [P, DI])
    yT = mx("yT", [P, 2, KI, P], R)
    ssq = mx("ssq", [P, 2])
    rs = mx("rs", [P, 2])
    NQ = TB * HEADS
    d_x = mx("d_x", [P, NQ])
    d_e = mx("d_e", [P, NQ])
    d_z = mx("d_z", [P, NQ])
    d_q = mx("d_q", [P, NQ])
    d_p = mx("d_p", [P, NQ])
    dts = mx("dts", [P, NQ])
    d_a = mx("d_a", [P, NQ])
    aparts = mx("aparts", [P, 3, NQ], B16)
    ncs = mx("ncs", [P, NQ])
    ecs = mx("ecs", [P, NQ])
    dec = mx("dec", [P, NQ])
    wd = mx("wd", [P, NQ])

    bank = [nc.alloc_psum_tensor(f"bank{i}", [P, 512], F) for i in range(8)]

    s_x = [sem(f"s_x{b}") for b in range(NB)]
    s_const = sem("s_const")
    c_pool = sem("c_pool")
    c_dve = sem("c_dve")
    c_act = sem("c_act")
    s_ready = sem("s_ready")
    s_bf = sem("s_bf")
    s_out = sem("s_out")
    l_var = sem("l_var")
    l_rstd = sem("l_rstd")
    l_xn = sem("l_xn")
    l_tp = sem("l_tp")
    l_hi = sem("l_hi")
    l_lo = sem("l_lo")
    r_lg = sem("r_lg")
    r_sh = sem("r_sh")
    r_ex = sem("r_ex")
    f_graw, f_uraw, f_draw = sem("f_graw"), sem("f_uraw"), sem("f_draw")
    f_whi = sem("f_whi")
    f_wlo = sem("f_wlo")
    f_gu = sem("f_gu")
    f_silu = sem("f_silu")
    f_h = sem("f_h")
    f_hhi = sem("f_hhi")
    f_hlo = sem("f_hlo")
    f_dn = sem("f_dn")
    f_acc = sem("f_acc")
    m_wo_raw = [sem(f"m_wo_raw{p}") for p in range(4)]
    m_wdt = sem("m_wdt")
    m_wo_n = sem("m_wo_n")
    m_wo_hi = sem("m_wo_hi")
    m_wo_lo = sem("m_wo_lo")
    m_raw = [sem(f"m_raw{q}") for q in range(2)]
    m_whi = sem("m_whi")
    m_wlo = sem("m_wlo")
    m_cp = sem("m_cp")
    m_pre = sem("m_pre")
    m_pre2 = sem("m_pre2")
    m_hin = sem("m_hin")
    m_hout = sem("m_hout")
    m_conv = sem("m_conv")
    m_xc = sem("m_xc")
    m_dtp = sem("m_dtp")
    m_dx = sem("m_dx")
    m_de = sem("m_de")
    m_ap = sem("m_ap")
    m_cs = sem("m_cs")
    m_ncs = sem("m_ncs")
    m_dec = sem("m_dec")
    m_zp = sem("m_zp")
    m_z = sem("m_z")
    m_B = sem("m_B")
    m_L = sem("m_L")
    m_G = sem("m_G")
    m_xt = sem("m_xt")
    m_Bt = sem("m_Bt")
    m_xev = sem("m_xev")
    m_xw = sem("m_xw")
    m_C = sem("m_C")
    m_yc = sem("m_yc")
    m_yd = sem("m_yd")
    m_M = sem("m_M")
    m_D = sem("m_D")
    m_Sd = sem("m_Sd")
    m_S = sem("m_S")
    m_E = sem("m_E")
    m_yi = sem("m_yi")
    m_yg = sem("m_yg")
    m_sq = sem("m_sq")
    m_rs = sem("m_rs")
    m_F = sem("m_F")
    m_yhi = sem("m_yhi")
    m_ylo = sem("m_ylo")
    m_out = sem("m_out")
    m_res = sem("m_res")
    m_zero = sem("m_zero")

    UPE = NB
    PAIRS = NX // 2
    PAIR_U = 2 * UPE

    H0, LO0, DN0, ACC0 = 2, 2, TB, NT

    def phase_counts(k):
        return PLAN[:k].count("ffn"), PLAN[:k].count("mixer")

    def wait_residual(eng, k, tiles_before, batches_before=None):
        nf, nm = phase_counts(k)
        if k == 0:
            return
        if PLAN[k - 1] == "ffn":
            eng.wait_ge(f_acc, ACC0 + nf * NX * NT)
        else:
            eng.wait_ge(m_res, nm * NT)

    def loop_waits(eng, i):
        def after(s, n, each_turn, unit=1):
            if isinstance(n, int) and n <= 0:
                return
            eng.wait_ge(s, (i * each_turn + n) * unit)

        def settle(*sems):
            for s, each_turn in sems:
                eng.wait_ge(s, i * each_turn + each_turn)
        return after, settle

    block = nc.Block()
    with block:

        @block.sync
        def _(sp):
            for b in range(NB):
                sp.dma_start(X[:, b * TB:(b + 1) * TB, :], x[:, b * TB:(b + 1) * TB, :]).then_inc(s_x[b], 16)
                if b == 0:
                    sp.dma_start(wr[:], w_router).then_inc(s_const, 16)
                    sp.dma_start(cw[:], conv).then_inc(s_const, 16)
                    sp.dma_start(hp[:], heads).then_inc(s_const, 16)
                    sp.dma_start(nw[:], norm_w).then_inc(s_const, 16)

            def ffn(k):
                nf, nm = phase_counts(k)
                first = nf * NX
                if k:
                    wait_residual(sp, k, NT)

                def load(e, g):
                    sp.wait_ge(f_wlo, 3 * g - 2)
                    sp.dma_start(g_raw[:], w_gate[e]).then_inc(f_graw, 16)
                    sp.wait_ge(f_wlo, 3 * g - 1)
                    sp.dma_start(u_raw[:], w_up[e]).then_inc(f_uraw, 16)
                    sp.wait_ge(f_wlo, 3 * g)
                    sp.dma_start(d_raw[:, 0:2, :], w_down[e][0:2 * P, :].rearrange("(c p) n -> p c n", p=P))\
                        .then_inc(f_draw, 16)
                    sp.dma_start(d_raw[0:FE - 2 * P, 2, :], w_down[e][2 * P:FE, :]).then_inc(f_draw, 16)

                if first == 0:
                    sp.dma_start(g_raw[:], w_gate[0]).then_inc(f_graw, 16)
                    sp.dma_start(u_raw[:], w_up[0]).then_inc(f_uraw, 16)
                    sp.dma_start(d_raw[:, 0:2, :], w_down[0][0:2 * P, :].rearrange("(c p) n -> p c n", p=P))\
                        .then_inc(f_draw, 16)
                    sp.dma_start(d_raw[0:FE - 2 * P, 2, :], w_down[0][2 * P:FE, :]).then_inc(f_draw, 16)
                else:
                    load(0, first)
                with sp.Fori(1, NX) as e:
                    sp.wait_ge(f_wlo, 3 * (e + first) - 2)
                    sp.dma_start(g_raw[:], w_gate[bass.ds(e, 1), :, :, :].rearrange("o p c n -> p (o c) n"))\
                        .then_inc(f_graw, 16)
                    sp.wait_ge(f_wlo, 3 * (e + first) - 1)
                    sp.dma_start(u_raw[:], w_up[bass.ds(e, 1), :, :, :].rearrange("o p c n -> p (o c) n"))\
                        .then_inc(f_uraw, 16)
                    sp.wait_ge(f_wlo, 3 * (e + first))
                    sp.dma_start(d_raw[:, 0:2, :],
                                 w_down[bass.ds(e, 1), 0:2 * P, :].rearrange("o (c p) n -> p (o c) n", p=P))\
                        .then_inc(f_draw, 16)
                    sp.dma_start(d_raw[0:FE - 2 * P, 2, :],
                                 w_down[bass.ds(e, 1), 2 * P:FE, :].rearrange("o p n -> p (o n)"))\
                        .then_inc(f_draw, 16)

            def mixer(k):
                wait_residual(sp, k, NT)
                sp.dma_start(wdt[:], w_dt).then_inc(m_wdt, 16)
                for piece in range(4):
                    if piece >= 2:
                        sp.wait_ge(m_wo_lo, piece - 1)
                    sp.dma_start(w_raw[:, piece % 2].rearrange("p (k a) n -> p k (a n)", k=2), w_out[piece])\
                        .then_inc(m_wo_raw[piece], 16)
                sp.wait_ge(m_wo_lo, 4)
                for j in range(2):
                    sp.dma_start(w_raw[:, j], w_in[j]).then_inc(m_raw[j], 16)
                with sp.Fori(0, BPB * NWU - 1) as i:
                    for q in range(2):
                        w = i * 2 + 2 + q
                        sp.wait_ge(m_wlo, w - 1)
                        u = sp.snap(w % NWU)
                        sp.dma_start(w_raw[:, q], w_in[bass.ds(u, 1), :, :, :].rearrange("o p c n -> p (o c) n"))\
                            .then_inc(m_raw[q], 16)

            for k, what in enumerate(PLAN):
                (ffn if what == "ffn" else mixer)(k)
            nf, nm = phase_counts(len(PLAN))
            for b in range(NB):
                if PLAN[-1] == "ffn":
                    sp.wait_ge(f_acc, ACC0 + (nf * NX - 1) * NT + (b + 1) * TB)
                else:
                    sp.wait_ge(m_res, (nm - 1) * NT + (b + 1) * TB)
                sp.dma_start(out[:, b * TB:(b + 1) * TB, :], X[:, b * TB:(b + 1) * TB, :]).then_inc(s_out, 16)
            sp.wait_ge(s_out, NB * 16)

        @block.gpsimd
        def _(pool):
            own = Chain(pool, c_pool)
            pool.memset(mhalf[:], -0.5).then_inc(s_ready, 1)
            pool.memset(comb[:], ROUTE).then_inc(s_ready, 1)
            pool.memset(spare[:], 0.0).then_inc(f_h, H0)
            pool.memset(spare2[:, 0:1], 0.0).then_inc(f_hlo, LO0)
            pool.memset(spare2[:, 1:2], 0.0).then_inc(f_dn, DN0)
            pool.memset(spare2[:, 2:3], 0.0).then_inc(f_acc, ACC0)
            own.mark(pool.memset(zero[:], 0.0))
            own.mark(pool.memset(eps[:], EPS))
            own.mark(pool.memset(by_di[:], 1.0 / DI))
            for e in range(NE):
                own.mark(pool.memset(iota8[:, e:e + 1], float(e)))
            own.mark(pool.memset(ident[:], 0.0))
            own.mark(pool.memset(tri[:], 1.0))
            own.join()
            pool.affine_select(out=ident[:], in_=ident[:], compare_op=ALU.not_equal, fill=1.0, base=0,
                               pattern=[[-1, P]], channel_multiplier=1).then_inc(s_ready, 1)
            pool.affine_select(out=tri[:], in_=tri[:], compare_op=ALU.is_ge, fill=0.0, base=0,
                               pattern=[[1, P]], channel_multiplier=-1).then_inc(s_ready, 1)
            pool.wait_ge(s_ready, 4)

            def rsqrt_ln(tiles):
                own.step(pool.tensor_tensor(rstd[:, tiles], rstd[:, tiles], eps[:].broadcast_to([P, TB]), ALU.add))
                pool.tensor_tensor(rstd[:, tiles], rstd[:, tiles], mhalf[:, 0:TB], ALU.pow).then_inc(l_rstd, 1)

            def ffn(k):
                for b in range(NB):
                    pool.wait_ge(l_var, k * NB + b + 1)
                    rsqrt_ln(slice(b * TB, (b + 1) * TB))

            def mixer(k):
                _, nm = phase_counts(k)
                wait_residual(pool, k, NT)
                zeros3 = zero[:].broadcast_to([P, TAPS - 1])

                def turn(i):
                    after, settle = loop_waits(pool, i)
                    pool.tensor_tensor(S[:], zero[:].broadcast_to([P, DI]), zero[:].broadcast_to([P, DI]), ALU.add)\
                        .then_inc(m_zero, 1)
                    for j in range(BPB):
                        after(l_var, k * NB + j + 1, BPB)
                        rsqrt_ln(slice(0, TB))
                        for u in range(NWU):
                            w = j * NWU + u
                            after(m_whi, w + 1, BPB * NWU)
                            pool.tensor_tensor(w_hl[:, w % 2, 1], w_raw[:, w % 2], w_hl[:, w % 2, 0].bitcast(F),
                                               ALU.subtract).then_inc(m_wlo, 1)
                            if u < 5:
                                for c in (2 * u, 2 * u + 1):
                                    n = j * NCH + c
                                    after(m_conv, n - 1, BPB * NCH)
                                    head = pre[:, c % 2, 0:TAPS - 1]
                                    if j == 0:
                                        pool.tensor_tensor(head, zeros3, zeros3, ALU.add).then_inc(m_hin, 1)
                                    else:
                                        after(m_hout, c + 1, NCH * (BPB - 1))
                                        pool.tensor_tensor(head, halo[:, c], zeros3, ALU.add).then_inc(m_hin, 1)
                                    if j < BPB - 1:
                                        after(m_pre, n + 1, BPB * NCH)
                                        pool.tensor_tensor(halo[:, c], pre[:, c % 2, D:D + TAPS - 1], zeros3, ALU.add)\
                                            .then_inc(m_hout, 1)
                        for q in range(TB + 1):
                            n = j * TB + q
                            if q < TB:
                                hq = slice(q * HEADS, (q + 1) * HEADS)
                                after(m_xev, n + 1, TPB)
                                after(m_dec, j + 1, BPB)
                                after(m_D, n, TPB)
                                pool.tensor_tensor(xw[:].rearrange("p (h d) -> p h d", d=HD),
                                                   xdt[:].rearrange("p (h d) -> p h d", d=HD),
                                                   each(wd[:, hq], HD), ALU.mult).then_inc(m_xw, 1)
                                after(m_C, n + 1, TPB)
                                after(m_S, n, TPB)
                                pool.wait_ge(m_zero, i + 1)
                                pool.tensor_tensor(S[:].rearrange("p (h d) -> p h d", d=HD),
                                                   S[:].rearrange("p (h d) -> p h d", d=HD),
                                                   each(dec[:, hq], HD), ALU.mult).then_inc(m_Sd, 1)
                                after(m_yc, n + 1, TPB)
                                pool.tensor_tensor(y[:, n % 2], y[:, n % 2], xD[:], ALU.add).then_inc(m_yd, 1)
                            if q >= 1:
                                after(m_sq, n, TPB)
                                last = slice((n - 1) % 2, (n - 1) % 2 + 1)
                                own.step(pool.tensor_tensor(rs[:, last], ssq[:, last], by_di[:], ALU.mult))
                                own.step(pool.tensor_tensor(rs[:, last], rs[:, last], eps[:], ALU.add))
                                pool.tensor_tensor(rs[:, (n - 1) % 2:(n - 1) % 2 + 1],
                                                   rs[:, (n - 1) % 2:(n - 1) % 2 + 1], mhalf[:, 0:1],
                                                   ALU.pow).then_inc(m_rs, 1)
                            if q < TB:
                                after(m_yi, n + 1, TPB)
                                after(m_z, 8 * (j + 1), 8 * BPB)
                                pool.tensor_tensor(y[:, n % 2], y[:, n % 2], zs[:, q], ALU.mult).then_inc(m_yg, 1)
                    settle((m_C, TPB), (m_S, TPB), (m_conv, BPB * NCH), (m_D, TPB))

                with pool.Fori(0, BATCH) as i:
                    own.enter(i, BPB * (1 + 2 * TB))
                    turn(i)
                own.leave(BATCH)

            for k, what in enumerate(PLAN):
                (ffn if what == "ffn" else mixer)(k)

        @block.scalar
        def _(act):
            act.wait_ge(s_const, 4 * 16)
            own = Chain(act, c_act)
            own.step(act.activation(negA[:], hp[:, HEADS:2 * HEADS], ACT.Exp))

            def split_hi(dst, src, signal):
                act.activation(dst, src, ACT.Copy).then_inc(signal, 1)

            def ffn(k):
                nf, nm = phase_counts(k)
                g0 = nf * NX
                wait_residual(act, k, NT)

                def weights(piece, g, parity):
                    raw, hl, arrived, n = ((g_raw, g_hl, f_graw, 16), (u_raw, u_hl, f_uraw, 16),
                                           (d_raw, d_hl, f_draw, 32))[piece]
                    act.wait_ge(arrived, (g + 1) * n)
                    if piece < 2:
                        split_hi(hl[:, parity, 0], raw[:], f_whi)
                    else:
                        act.activation(hl[:, parity, 0, 0:2], raw[:, 0:2], ACT.Copy)
                        split_hi(hl[0:FE - 2 * P, parity, 0, 2], raw[0:FE - 2 * P, 2], f_whi)

                for piece in range(3):
                    weights(piece, g0, 0)
                for t in range(NT):
                    n = k * NT + t
                    act.wait_ge(l_tp, n + 1)
                    split_hi(xT[:, 0, :, t * P:(t + 1) * P], bank[t % 4][:].rearrange("p (c t) -> p c t", c=KD), l_hi)
                act.wait_ge(r_sh, nf + 1)
                act.activation(r_b[:], r_a[:], ACT.Exp).then_inc(r_ex, 1)

                def pair(i, last):
                    for q in range(2):
                        for b in range(NB):
                            u = i * PAIR_U + (nf * NX * UPE + q * UPE + b)
                            for c, (_, fw) in enumerate(FCH):
                                v = u * NF + c
                                par = ((q * UPE + b) * NF + c) % 2
                                act.wait_ge(f_gu, v + 1)
                                act.wait_ge(f_hlo, v - 1 + LO0)
                                act.activation(gate[0:fw, par], bank[par][0:fw], ACT.Silu).then_inc(f_silu, 1)
                                act.wait_ge(f_h, v + 1 + H0)
                                act.wait_ge(f_dn, u * TB + DN0)
                                split_hi(hT[0:fw, 0, c], gate[0:fw, par], f_hhi)
                            if b < 3 and not (last and q == 1):
                                weights(b, i * 2 + (g0 + q + 1), (q + 1) % 2)

                with act.Fori(0, PAIRS - 1) as i:
                    pair(i, False)
                pair(PAIRS - 1, True)

            def mixer(k):
                _, nm = phase_counts(k)
                wait_residual(act, k, NT)
                for piece in range(4):
                    act.wait_ge(m_wo_n, piece + 1)
                    split_hi(wo[:, 0, 2 * piece:2 * piece + 2],
                             w_raw[:, piece % 2].rearrange("p (k a) n -> p k (a n)", k=2), m_wo_hi)

                def turn(i):
                    after, settle = loop_waits(act, i)

                    def unit_hi(w):
                        after(m_raw[w % 2], w // 2 + 1, BPB * NWU // 2, unit=16)
                        if w >= 2:
                            jj, u = divmod(w - 2, NWU)
                            if u < 5:
                                after(m_cp, jj * NCH + 2 * u + 2, BPB * NCH)
                            else:
                                after(m_zp, jj * 8 + (u - 5) * 2 + 2, 8 * BPB)
                        split_hi(w_hl[:, w % 2, 0], w_raw[:, w % 2], m_whi)

                    def conv_in(n, c):
                        b = bank[c % 2]
                        after(m_cp, n + 1, BPB * NCH)
                        after(m_conv, n - 1, BPB * NCH)
                        after(m_hout, min(n - 1, NCH), NCH * (BPB - 1))
                        act.activation(pre[:, c % 2, TAPS - 1:], b[:], ACT.Copy).then_inc(m_pre, 1)
                        after(m_xc, n - 1, BPB * NCH)
                        act.activation(acc[:, c % 2], b[:], ACT.Identity, bias=cw[:, c, TAPS:TAPS + 1],
                                       scale=cw[:, c, TAPS - 1:TAPS]).then_inc(m_pre2, 1)

                    def conv_out(n, c):
                        after(m_conv, n + 1, BPB * NCH)
                        act.activation(xc[:, c], acc[:, c % 2], ACT.Silu).then_inc(m_xc, 1)

                    unit_hi(0)
                    for j in range(BPB):
                        for q in range(TB):
                            n = k * NT + j * TB + q
                            after(l_tp, n + 1, TPB)
                            split_hi(xb[:, 0, :, q * P:(q + 1) * P],
                                     bank[4 + q % 2][:].rearrange("p (c t) -> p c t", c=KD), l_hi)
                        if j:
                            after(m_yg, j * TB, TPB)
                            after(m_D, j * TB, TPB)
                        for u in range(NWU):
                            w = j * NWU + u
                            if w + 1 < BPB * NWU:
                                unit_hi(w + 1)
                            if u < 5:
                                for c in (2 * u, 2 * u + 1):
                                    n = j * NCH + c
                                    conv_in(n, c)
                                    if c >= 1:
                                        conv_out(n - 1, c - 1)
                                if u == 1:
                                    after(m_dx, j + 1, BPB)
                                    act.activation(d_e[:], d_z[:], ACT.Exp).then_inc(m_de, 1)
                            else:
                                if u == 5:
                                    conv_out(j * NCH + NCH - 1, NCH - 1)
                                for half in range(2):
                                    n = j * 8 + (u - 5) * 2 + half
                                    after(m_zp, n + 1, 8 * BPB)
                                    act.activation(zs[:, 2 * half:2 * half + 2, (u - 5) * WU:(u - 4) * WU],
                                                   bank[6 + half][:].rearrange("p (q n) -> p q n", q=2),
                                                   ACT.Silu).then_inc(m_z, 1)
                        after(m_cs, j + 1, BPB)
                        after(m_ncs, j + 1, BPB)
                        cs, tot = bank[2][:, NQ:2 * NQ], bank[2][:, 2 * NQ:3 * NQ]
                        act.activation(ecs[:], cs, ACT.Exp)
                        act.activation(dec[:], tot, ACT.Exp)
                        act.activation(wd[:], d_p[:], ACT.Exp).then_inc(m_dec, 1)
                        for q in range(TB + 1):
                            n = j * TB + q
                            for g in range(HG if q < TB else 0):
                                after(m_B, HG * n + g + 1, HG * TPB)
                                after(m_E, n, TPB)
                                for h in range(g * GH, (g + 1) * GH):
                                    ins = act.activation(L[:, h], bank[g % 2][:, (h % GH) * P:(h % GH + 1) * P], ACT.Exp,
                                                         bias=ncs[:, q * HEADS + h:q * HEADS + h + 1])
                                ins.then_inc(m_L, 1)
                                if g == 0:
                                    after(m_G, n + 1, TPB)
                                    after(m_D, n, TPB)
                                    after(m_M, HG * n, HG * TPB)
                                    act.activation(GB[:], bank[3][:, 0:2 * P], ACT.Copy).then_inc(m_Bt, 1)
                            if q >= 1:
                                after(m_yg, n, TPB)
                                after(m_rs, n - 2, TPB)
                                after(m_sq, n - 1, TPB)
                                act.activation(ysq[:], y[:, (n - 1) % 2], ACT.Square,
                                               accum_out=ssq[:, (n - 1) % 2:(n - 1) % 2 + 1]).then_inc(m_sq, 1)
                                for half in range(2):
                                    after(m_F, 2 * (n - 1) + half + 1, 2 * TPB)
                                    after(m_out, n - 1, TPB)
                                    split_hi(yT[:, 0, 4 * half:4 * half + 4],
                                             bank[6 + half][:].rearrange("p (c t) -> p c t", c=4), m_yhi)
                    settle((m_zp, 8 * BPB), (m_conv, BPB * NCH), (m_hout, NCH * (BPB - 1)), (m_xc, BPB * NCH),
                           (m_yg, TPB), (m_D, TPB), (m_E, TPB), (m_M, HG * TPB), (m_rs, TPB), (m_sq, TPB),
                           (m_out, TPB))

                with act.Fori(0, BATCH) as i:
                    turn(i)

            for k, what in enumerate(PLAN):
                (ffn if what == "ffn" else mixer)(k)

        @block.vector
        def _(dve):
            own = Chain(dve, c_dve)

            def ln_stats(tiles, slots):
                for xt, s in zip(tiles, slots):
                    own.mark(dve.bn_stats(stats[:, s, :], xt))
                own.join()
                dve.tensor_copy(spare[:], mhalf[:, 0:1])
                for s in slots:
                    own.mark(dve.bn_aggr(mv[:, s, :], stats[:, s, :]))
                own.join()
                dve.tensor_copy(rstd[:, slots[0]:slots[-1] + 1],
                                mv[:, slots[0]:slots[-1] + 1, 1:2].rearrange("p t o -> p (t o)")).then_inc(l_var, 1)

            def ln_scale(dst, xt, s):
                return dve.tensor_scalar(dst, xt, mv[:, s, 0:1], rstd[:, s:s + 1], ALU.subtract, ALU.mult)

            def lo_half(hl_lo, value, hl_hi, signal):
                dve.tensor_tensor(hl_lo, value, hl_hi.bitcast(F), ALU.subtract).then_inc(signal, 1)

            def ffn(k):
                nf, nm = phase_counts(k)
                g0 = nf * NX
                wait_residual(dve, k, NT)

                def weights(piece, g, parity):
                    raw, hl = ((g_raw, g_hl), (u_raw, u_hl), (d_raw, d_hl))[piece]
                    dve.wait_ge(f_whi, 3 * g + (piece + 1))
                    if piece < 2:
                        lo_half(hl[:, parity, 1], raw[:], hl[:, parity, 0], f_wlo)
                    else:
                        dve.tensor_tensor(hl[:, parity, 1, 0:2], raw[:, 0:2], hl[:, parity, 0, 0:2].bitcast(F),
                                          ALU.subtract)
                        lo_half(hl[0:FE - 2 * P, parity, 1, 2], raw[0:FE - 2 * P, 2],
                                hl[0:FE - 2 * P, parity, 0, 2], f_wlo)

                def x_lo(t):
                    dve.wait_ge(l_hi, k * NT + t + 1)
                    lo_half(xT[:, 1, :, t * P:(t + 1) * P], bank[t % 4][:].rearrange("p (c t) -> p c t", c=KD),
                            xT[:, 0, :, t * P:(t + 1) * P], l_lo)

                def block_stats(b):
                    if k == 0:
                        dve.wait_ge(s_x[b], 16)
                    ln_stats([X[:, t, :] for t in range(b * TB, (b + 1) * TB)], range(b * TB, (b + 1) * TB))

                block_stats(0)
                for b in range(NB):
                    if b + 1 < NB:
                        block_stats(b + 1)
                    dve.wait_ge(l_rstd, k * NB + b + 1)
                    for t in range(b * TB, (b + 1) * TB):
                        dve.wait_ge(l_tp, k * NT + max(t - 1, 0))
                        ln_scale(xn_f[:, t % 2], X[:, t, :], t).then_inc(l_xn, 1)
                        if t >= 1:
                            x_lo(t - 1)
                x_lo(NT - 1)
                for piece in range(3):
                    weights(piece, g0, 0)

                logits = bank[4][:, 0:NT * NE].rearrange("p (t e) -> p t e", e=NE)
                dve.wait_ge(r_lg, nf + 1)
                own.step(dve.tensor_reduce(r_1[:], logits, AX.X, ALU.max))
                dve.tensor_tensor(r_a[:], logits, each(r_1[:], NE), ALU.subtract).then_inc(r_sh, 1)
                dve.wait_ge(r_ex, nf + 1)
                own.step(dve.tensor_reduce(r_1[:], r_b[:], AX.X, ALU.add))
                own.step(dve.reciprocal(r_2[:], r_1[:]))
                own.step(dve.tensor_tensor(r_a[:], r_b[:], each(r_2[:], NE), ALU.mult))
                for t in range(NT):
                    own.mark(dve.max(r_top[:, t], r_a[:, t]))
                own.join()
                for t in range(NT):
                    own.mark(dve.max_index(r_idx[:, t], r_top[:, t], r_a[:, t]))
                own.join()
                own.step(dve.tensor_scalar(r_top[:, :, 0:2], r_top[:, :, 0:2], ROUTE, None, ALU.mult))
                for slot in range(2):
                    own.step(dve.tensor_copy(r_1[:], r_idx[:, :, slot]))
                    own.step(dve.tensor_copy(r_2[:], r_top[:, :, slot]))
                    own.step(dve.tensor_tensor(r_a[:] if slot else comb[:, :, 0:NE], some(iota8[:], NT), each(r_1[:], NE),
                                               ALU.is_equal))
                    own.step(dve.tensor_tensor(r_a[:] if slot else comb[:, :, 0:NE], r_a[:] if slot else comb[:, :, 0:NE],
                                               each(r_2[:], NE), ALU.mult))
                own.step(dve.tensor_tensor(comb[:, :, 0:NE], comb[:, :, 0:NE], r_a[:], ALU.add))

                def pair(i, last):
                    for q in range(2):
                        for b in range(NB):
                            u = i * PAIR_U + (nf * NX * UPE + q * UPE + b)
                            for c, (_, fw) in enumerate(FCH):
                                v = u * NF + c
                                par = ((q * UPE + b) * NF + c) % 2
                                dve.wait_ge(f_silu, v + 1)
                                dve.tensor_tensor(gate[0:fw, par], gate[0:fw, par], bank[2 + par][0:fw], ALU.mult)\
                                    .then_inc(f_h, 1)
                                dve.wait_ge(f_hhi, v + 1)
                                lo_half(hT[0:fw, 1, c], gate[0:fw, par], hT[0:fw, 0, c], f_hlo)
                            if b < 3 and not (last and q == 1):
                                weights(b, i * 2 + (g0 + q + 1), (q + 1) % 2)
                            for s in range(TB):
                                t = b * TB + s
                                e = i * 2 + q
                                dve.wait_ge(f_dn, u * TB + (s + 1) + DN0)
                                if isinstance(e, int):
                                    w = comb[:, t, e:e + 1]
                                else:
                                    w = comb[:, t, bass.ds(e, 1)]
                                dve.wait_ge(f_acc, (u - UPE) * TB + (s + 1) + ACC0)
                                dve.scalar_tensor_tensor(X[:, t, :], bank[4 + s][:], w, X[:, t, :], ALU.mult, ALU.add)\
                                    .then_inc(f_acc, 1)

                with dve.Fori(0, PAIRS - 1) as i:
                    pair(i, False)
                pair(PAIRS - 1, True)

            def mixer(k):
                nf, nm = phase_counts(k)
                wait_residual(dve, k, NT)
                for piece in range(4):
                    raw = w_raw[:, piece % 2].rearrange("p (k a) n -> p k (a n)", k=2)
                    dve.wait_ge(m_wo_raw[piece], 16)
                    own.mark(dve.tensor_scalar(raw[:, 0], raw[:, 0], nw[:, 2 * piece:2 * piece + 1], None, ALU.mult))
                    own.join()
                    dve.tensor_scalar(raw[:, 1], raw[:, 1], nw[:, 2 * piece + 1:2 * piece + 2], None, ALU.mult)\
                        .then_inc(m_wo_n, 1)
                    dve.wait_ge(m_wo_hi, piece + 1)
                    lo_half(wo[:, 1, 2 * piece:2 * piece + 2], raw, wo[:, 0, 2 * piece:2 * piece + 2], m_wo_lo)

                def turn(i):
                    after, settle = loop_waits(dve, i)

                    for j in range(BPB):
                        tiles = [X[:, bass.ds(i * TPB + (j * TB + q), 1), :].rearrange("p o n -> p (o n)")
                                 for q in range(TB)]
                        ln_stats(tiles, range(TB))
                        after(l_rstd, k * NB + j + 1, BPB)

                        def x_lo(q):
                            after(l_hi, k * NT + j * TB + q + 1, TPB)
                            lo_half(xb[:, 1, :, q * P:(q + 1) * P],
                                    bank[4 + q % 2][:].rearrange("p (c t) -> p c t", c=KD),
                                    xb[:, 0, :, q * P:(q + 1) * P], l_lo)

                        for q in range(TB):
                            n = k * NT + j * TB + q
                            after(l_tp, n - 1, TPB)
                            ln_scale(xn_m[:, q % 2], tiles[q], q).then_inc(l_xn, 1)
                            if q >= 1:
                                x_lo(q - 1)
                        x_lo(TB - 1)

                        def conv(c):
                            n = j * NCH + c
                            after(m_pre2, n + 1, BPB * NCH)
                            after(m_hin, n + 1, BPB * NCH)
                            for tap in range(TAPS - 1):
                                ins = dve.scalar_tensor_tensor(acc[:, c % 2], pre[:, c % 2, tap:tap + D],
                                                               cw[:, c, tap:tap + 1], acc[:, c % 2], ALU.mult, ALU.add)
                                if tap < TAPS - 2:
                                    own.step(ins)
                            ins.then_inc(m_conv, 1)

                        def softplus():
                            three = lambda t: t[:].rearrange("p (q h) -> p q h", h=HEADS)
                            after(m_dtp, j + 1, BPB)
                            own.step(dve.tensor_tensor(three(d_x), bank[2][:, 0:NQ].rearrange("p (q h) -> p q h", h=HEADS),
                                                       some(hp[:, 0:HEADS], TB), ALU.add))
                            own.step(dve.tensor_scalar(d_q[:], d_x[:], -1.0, None, ALU.mult))
                            dve.tensor_tensor(d_z[:], d_x[:], d_q[:], ALU.min).then_inc(m_dx, 1)

                        def log1p():
                            three = lambda t: t[:].rearrange("p (q h) -> p q h", h=HEADS)
                            after(m_de, j + 1, BPB)
                            own.step(dve.tensor_scalar(d_q[:], d_e[:], 2.0, None, ALU.add))
                            own.step(dve.reciprocal(d_p[:], d_q[:]))
                            own.step(dve.tensor_tensor(d_z[:], d_e[:], d_p[:], ALU.mult))
                            own.step(dve.tensor_tensor(d_q[:], d_z[:], d_z[:], ALU.mult))
                            own.step(dve.tensor_scalar(d_p[:], d_q[:], LOG1P[-1], None, ALU.mult))
                            for c in reversed(LOG1P[:-1]):
                                own.step(dve.scalar_tensor_tensor(d_p[:], d_p[:], c, d_q[:], ALU.add, ALU.mult))
                            own.step(dve.scalar_tensor_tensor(d_p[:], d_p[:], 1.0, d_z[:], ALU.add, ALU.mult))
                            own.step(dve.tensor_scalar(d_x[:], d_x[:], 0.0, None, ALU.max))
                            own.step(dve.scalar_tensor_tensor(dts[:], d_p[:], 2.0, d_x[:], ALU.mult, ALU.add))
                            own.step(dve.tensor_tensor(three(d_a), three(dts), some(negA[:], TB), ALU.mult))
                            own.step(dve.tensor_scalar(d_a[:], d_a[:], -1.0, DECAY_FLOOR, ALU.mult, ALU.max))
                            own.step(dve.tensor_copy(aparts[:, 0], d_a[:]))
                            own.step(dve.tensor_tensor(d_q[:], d_a[:], aparts[:, 0], ALU.subtract))
                            own.step(dve.tensor_copy(aparts[:, 1], d_q[:]))
                            own.step(dve.tensor_tensor(d_a[:], d_q[:], aparts[:, 1], ALU.subtract))
                            dve.tensor_copy(aparts[:, 2], d_a[:]).then_inc(m_ap, 1)

                        for c in range(NCH):
                            conv(c)
                            if c == 1:
                                softplus()
                            if c == 4:
                                log1p()
                        after(m_cs, j + 1, BPB)
                        own.step(dve.tensor_scalar(ncs[:], bank[2][:, NQ:2 * NQ], -1.0, None, ALU.mult))
                        dve.tensor_tensor(d_p[:], bank[2][:, 2 * NQ:3 * NQ], ncs[:], ALU.add).then_inc(m_ncs, 1)

                        def heads_of(ap):
                            return ap.rearrange("p (h d) -> p h d", d=HD)

                        for q in range(TB + 1):
                            n = j * TB + q
                            if q < TB:
                                hq = slice(q * HEADS, (q + 1) * HEADS)
                                HB = HEADS // 2
                                for half in range(2):
                                    hs = slice(half * DI // 2, (half + 1) * DI // 2)
                                    after(m_xt, 2 * n + half + 1, 2 * TPB)
                                    if half == 0:
                                        after(m_xw, n, TPB)
                                        after(m_yd, n, TPB)
                                        after(m_E, n, TPB)
                                    own.mark(dve.tensor_tensor(heads_of(xdt[:, hs]), heads_of(bank[4 + half][:]),
                                                               each(dts[:, q * HEADS + half * HB:q * HEADS + (half + 1) * HB], HD),
                                                               ALU.mult))
                                    ins = dve.tensor_tensor(heads_of(xD[:, hs]), heads_of(bank[4 + half][:]),
                                                            each(hp[:, 2 * HEADS + half * HB:2 * HEADS + (half + 1) * HB], HD),
                                                            ALU.mult)
                                    if half == 0:
                                        own.mark(ins)
                                ins.then_inc(m_xev, 1)
                                after(m_C, n + 1, TPB)
                                after(m_dec, j + 1, BPB)
                                after(m_F, 2 * (n - 1), 2 * TPB)
                                after(m_sq, n - 1, TPB)
                                for half in range(2):
                                    hs = slice(half * DI // 2, (half + 1) * DI // 2)
                                    ins = dve.tensor_tensor(heads_of(y[:, n % 2, hs]), heads_of(bank[6 + half][:]),
                                                            each(ecs[:, q * HEADS + half * HB:q * HEADS + (half + 1) * HB], HD),
                                                            ALU.mult)
                                    if half == 0:
                                        own.mark(ins)
                                ins.then_inc(m_yc, 1)
                                after(m_Bt, n + 1, TPB)
                                for g in range(HG):
                                    after(m_L, HG * n + g + 1, HG * TPB)
                                    dve.tensor_tensor(L[:, g * GH:(g + 1) * GH], L[:, g * GH:(g + 1) * GH],
                                                      some(GB[:, 0:P], GH), ALU.mult).then_inc(m_M, 1)
                                after(m_D, n + 1, TPB)
                                after(m_Sd, n + 1, TPB)
                                own.mark(dve.tensor_tensor(S[:, 0:DI // 2], S[:, 0:DI // 2], bank[4][:], ALU.add))
                                dve.tensor_tensor(S[:, DI // 2:DI], S[:, DI // 2:DI], bank[5][:], ALU.add)\
                                    .then_inc(m_S, 1)
                            if q >= 1:
                                for half in range(2):
                                    after(m_yhi, 2 * (n - 1) + half + 1, 2 * TPB)
                                    lo_half(yT[:, 1, 4 * half:4 * half + 4],
                                            bank[6 + half][:].rearrange("p (c t) -> p c t", c=4),
                                            yT[:, 0, 4 * half:4 * half + 4], m_ylo)
                                t = bass.ds(i * TPB + (n - 1), 1)
                                xt = X[:, t, :].rearrange("p o n -> p (o n)")
                                after(m_out, n, TPB)
                                after(m_rs, n, TPB)
                                dve.scalar_tensor_tensor(xt, bank[2][:], rs[:, (n - 1) % 2:(n - 1) % 2 + 1], xt,
                                                         ALU.mult, ALU.add).then_inc(m_res, 1)
                            if q < TB:
                                after(m_E, n + 1, TPB)
                                after(m_yd, n + 1, TPB)
                                own.mark(dve.tensor_tensor(y[:, n % 2, 0:DI // 2], y[:, n % 2, 0:DI // 2], bank[6][:],
                                                           ALU.add))
                                dve.tensor_tensor(y[:, n % 2, DI // 2:DI], y[:, n % 2, DI // 2:DI], bank[7][:], ALU.add)\
                                    .then_inc(m_yi, 1)
                    settle((m_xw, TPB), (m_yd, TPB), (m_E, TPB), (m_F, 2 * TPB), (m_sq, TPB), (m_out, TPB),
                           (m_yg, TPB))

                own_steps = 2 * TB + NCH * (TAPS - 2) + 2 + 21 + 1 + TB * 6
                with dve.Fori(0, BATCH) as i:
                    own.enter(i, BPB * own_steps)
                    turn(i)
                own.leave(BATCH)

            dve.wait_ge(s_ready, 4)
            own.mark(dve.tensor_copy(tri_b[:], tri[:]))
            own.mark(dve.tensor_copy(ident_b[:], ident[:]))
            own.mark(dve.memset(ones_b[:], 1.0))
            dve.tensor_scalar(mask_b[:], tri[:], 1.0, -MASKED, ALU.subtract, ALU.mult).then_inc(s_bf, 1)
            for k, what in enumerate(PLAN):
                (ffn if what == "ffn" else mixer)(k)

        @block.tensor
        def _(pe):
            pe.wait_ge(s_ready, 4)
            pe.wait_ge(s_bf, 1)
            pe.wait_ge(s_const, 64)

            def ffn(k):
                nf, nm = phase_counts(k)
                g0 = nf * NX
                if k:
                    wait_residual(pe, k, NT)
                for t in range(NT):
                    n = k * NT + t
                    pe.wait_ge(l_xn, n + 1)
                    pe.wait_ge(l_lo, k * NT + max(t - 3, 0))
                    for c in range(KD):
                        ins = pe.transpose(bank[t % 4][:, c * P:(c + 1) * P], xn_f[:, t % 2, c * P:(c + 1) * P], ident[:])
                    ins.then_inc(l_tp, 1)
                for t in range(NT):
                    pe.wait_ge(l_lo, k * NT + t + 1)
                    for m, (half, c) in enumerate([(a, c) for a in range(2) for c in range(KD)]):
                        ins = pe.matmul(bank[4][:, t * NE:(t + 1) * NE],
                                        xT[:, half, c, t * P:(t + 1) * P].bitcast(F), wr[:, c],
                                        start=(m == 0), stop=(m == 2 * KD - 1))
                ins.then_inc(r_lg, 1)

                def pair(i, last):
                    for q in range(2):
                        for b in range(NB):
                            u = i * PAIR_U + (nf * NX * UPE + q * UPE + b)
                            if b == 0:
                                pe.wait_ge(f_wlo, (i * 2 + (g0 + q + 1)) * 3)
                            for c, (f0, fw) in enumerate(FCH):
                                v = u * NF + c
                                par = ((q * UPE + b) * NF + c) % 2
                                pe.wait_ge(f_h, v - 1 + H0)
                                for w, dst in ((g_hl, bank[par]), (u_hl, bank[2 + par])):
                                    n = 0
                                    for kc in range(KD):
                                        for hw, hx in HALVES:
                                            ins = pe.matmul(dst[0:fw], w[:, q, hw, kc, f0:f0 + fw],
                                                            xT[:, hx, kc, b * D:(b + 1) * D],
                                                            start=(n == 0), stop=(n == 3 * KD - 1))
                                            n += 1
                                ins.then_inc(f_gu, 1)
                            for c, (f0, fw) in enumerate(FCH):
                                v = u * NF + c
                                pe.wait_ge(f_hlo, v + 1 + LO0)
                                for s in range(TB):
                                    if c == 0:
                                        pe.wait_ge(f_acc, (u - 1) * TB + (s + 1) + ACC0)
                                    for m, (hh, hw) in enumerate(HALVES):
                                        ins = pe.matmul(bank[4 + s][:], hT[0:fw, hh, c, s * P:(s + 1) * P],
                                                        d_hl[0:fw, q, hw, c],
                                                        start=(c == 0 and m == 0), stop=(c == NF - 1 and m == 2))
                                    if c == NF - 1:
                                        ins.then_inc(f_dn, 1)

                pe.wait_ge(r_sh, nf + 1)
                with pe.Fori(0, PAIRS - 1) as i:
                    pair(i, False)
                pair(PAIRS - 1, True)

            def mixer(k):
                wait_residual(pe, k, NT)
                pe.wait_ge(m_wo_lo, 4)
                pe.wait_ge(m_wdt, 16)

                def turn(i):
                    after, settle = loop_waits(pe, i)

                    for j in range(BPB):
                        for q in range(TB):
                            n = k * NT + j * TB + q
                            after(l_xn, n + 1, TPB)
                            if q < 2:
                                after(m_S, j * TB, TPB)
                                after(l_lo, k * NT + j * TB, TPB)
                            else:
                                after(l_lo, n - 1, TPB)
                            for c in range(KD):
                                ins = pe.transpose(bank[4 + q % 2][:, c * P:(c + 1) * P],
                                                   xn_m[:, q % 2, c * P:(c + 1) * P], ident[:])
                            ins.then_inc(l_tp, 1)
                        after(l_lo, k * NT + (j + 1) * TB, TPB)
                        for u in range(NWU):
                            w = j * NWU + u
                            after(m_wlo, w + 1, BPB * NWU)
                            wt = w_hl[:, w % 2]
                            if u < 5:
                                for c in (2 * u, 2 * u + 1):
                                    n = j * NCH + c
                                    if c < 2:
                                        after(m_L, HG * j * TB, HG * TPB)
                                        after(m_pre2, j * NCH, BPB * NCH)
                                    else:
                                        after(m_pre2, n - 1, BPB * NCH)
                                    m = 0
                                    for kc in range(KD):
                                        for hw, hx in HALVES:
                                            ins = pe.matmul(bank[c % 2][:], wt[:, hw, kc, (c % 2) * P:(c % 2 + 1) * P],
                                                            xb[:, hx, kc], start=(m == 0), stop=(m == 3 * KD - 1))
                                            m += 1
                                    ins.then_inc(m_cp, 1)
                                if u == 0:
                                    after(m_res, j * TB, TPB)
                                    for q in range(TB):
                                        for m, (half, kc) in enumerate([(a, c) for a in range(2) for c in range(KD)]):
                                            ins = pe.matmul(bank[2][:, q * HEADS:(q + 1) * HEADS],
                                                            xb[:, half, kc, q * P:(q + 1) * P].bitcast(F), wdt[:, kc],
                                                            start=(m == 0), stop=(m == 2 * KD - 1))
                                    ins.then_inc(m_dtp, 1)
                            else:
                                for half in range(2):
                                    n = j * 8 + (u - 5) * 2 + half
                                    if u == 5:
                                        after(m_ylo, 2 * j * TB, 2 * TPB)
                                        after(m_yi, j * TB, TPB)
                                    else:
                                        after(m_z, n - 1, 8 * BPB)
                                    for q in (2 * half, 2 * half + 1):
                                        m = 0
                                        for kc in range(KD):
                                            for hx, hw in HALVES:
                                                ins = pe.matmul(bank[6 + half][:, (q % 2) * WU:(q % 2 + 1) * WU],
                                                                xb[:, hx, kc, q * P:(q + 1) * P], wt[:, hw, kc],
                                                                start=(m == 0), stop=(m == 3 * KD - 1))
                                                m += 1
                                    ins.then_inc(m_zp, 1)
                        after(m_ap, j + 1, BPB)
                        for dst, mat in ((1, tri_b), (2, ones_b)):
                            for p in range(3):
                                ins = pe.matmul(bank[2][:, dst * NQ:(dst + 1) * NQ], mat[:], aparts[:, p],
                                                start=(p == 0), stop=(p == 2))
                        ins.then_inc(m_cs, 1)

                        def decays(n, q, g):
                            if q == 0 and g < 2:
                                after(m_pre2, (j + 1) * NCH, BPB * NCH)
                            else:
                                after(m_L, HG * n + g - 1, HG * TPB)
                            dst = bank[g % 2]
                            pe.matmul(dst[:].rearrange("p (h t) -> p h t", h=GH), ident_b[:], some(mask_b[:], GH),
                                      start=True, stop=False)
                            for h in range(GH):
                                col = q * HEADS + g * GH + h
                                for p in range(3):
                                    ins = pe.matmul(dst[:, h * P:(h + 1) * P],
                                                    aparts[:, p, col:col + 1].broadcast_to([P, P]), tri_b[:],
                                                    start=False, stop=(h == GH - 1 and p == 2))
                            ins.then_inc(m_B, 1)

                        def project(n):
                            after(m_yg, n + 1, TPB)
                            for half in range(2):
                                for c in range(4):
                                    ins = pe.transpose(bank[6 + half][:, c * P:(c + 1) * P],
                                                       y[:, n % 2, (4 * half + c) * P:(4 * half + c + 1) * P], ident[:])
                                ins.then_inc(m_F, 1)
                            if n % TB == 0:
                                after(m_dec, j + 1, BPB)
                            after(m_res, n, TPB)
                            m = 0
                            for half in range(2):
                                after(m_ylo, 2 * n + half + 1, 2 * TPB)
                                for c in range(4 * half, 4 * half + 4):
                                    for hy, hw in HALVES:
                                        ins = pe.matmul(bank[2][:], yT[:, hy, c], wo[:, hw, c],
                                                        start=(m == 0), stop=(m == 3 * KI - 1))
                                        m += 1
                            ins.then_inc(m_out, 1)

                        for q in range(TB):
                            n = j * TB + q
                            tt = slice(q * P, (q + 1) * P)
                            decays(n, q, 0)
                            decays(n, q, 1)
                            if q == 0:
                                after(m_xc, (j + 1) * NCH, BPB * NCH)
                            after(m_Bt, n, TPB)
                            pe.matmul(bank[3][:, 0:P], xc[:, 0, tt], xc[:, 1, tt], start=True, stop=True)
                            pe.transpose(bank[3][:, P:2 * P], xc[:, 0, tt], ident[:]).then_inc(m_G, 1)
                            after(m_S, n, TPB)
                            for half in range(2):
                                for c in range(4):
                                    ins = pe.transpose(bank[4 + half][:, c * P:(c + 1) * P],
                                                       xc[:, 2 + 4 * half + c, tt], ident[:])
                                ins.then_inc(m_xt, 1)
                            decays(n, q, 2)
                            pe.wait_ge(m_zero, i + 1)
                            after(m_yi, n, TPB)
                            if q == 0:
                                after(m_z, 8 * (j + 1), 8 * BPB)
                                after(m_ylo, 2 * n, 2 * TPB)
                            for half in range(2):
                                ins = pe.matmul(bank[6 + half][:], xc[:, 1, tt], S[:, half * 512:(half + 1) * 512],
                                                start=True, stop=True)
                            ins.then_inc(m_C, 1)
                            decays(n, q, 3)
                            after(m_xw, n + 1, TPB)
                            after(m_Bt, n + 1, TPB)
                            for half in range(2):
                                ins = pe.matmul(bank[4 + half][:], Bt, xw[:, half * 512:(half + 1) * 512],
                                                start=True, stop=True)
                            ins.then_inc(m_D, 1)
                            after(m_yc, n + 1, TPB)
                            if q >= 1:
                                project(n - 1)
                                after(m_ylo, 2 * n, 2 * TPB)
                            for g in range(HG):
                                after(m_M, HG * n + g + 1, HG * TPB)
                                for h in range(g * GH, (g + 1) * GH):
                                    ins = pe.matmul(bank[6 + h // 8][:, (h % 8) * HD:(h % 8 + 1) * HD], L[:, h],
                                                    xdt[:, h * HD:(h + 1) * HD], start=True, stop=True)
                            ins.then_inc(m_E, 1)
                        after(m_yi, (j + 1) * TB, TPB)
                        project(j * TB + TB - 1)
                    settle((m_S, TPB), (m_L, HG * TPB), (m_pre2, BPB * NCH), (m_res, TPB), (m_ylo, 2 * TPB),
                           (m_yi, TPB), (m_Bt, TPB), (m_z, 8 * BPB), (m_dec, BPB))

                with pe.Fori(0, BATCH) as i:
                    turn(i)

            for k, what in enumerate(PLAN):
                (ffn if what == "ffn" else mixer)(k)


def arrange(inputs):
    import numpy as np
    a = {k: np.asarray(v) for k, v in inputs.items()}

    def by_rows(w, rows=P):
        k = w.shape[-2] // rows
        return np.moveaxis(w.reshape(*w.shape[:-2], k, rows, w.shape[-1]), -3, -2)

    def experts(routed, shared):
        half = shared.shape[1] // NS
        return np.concatenate([routed, shared.reshape(D, NS, half).transpose(1, 0, 2)])

    x = a["L0_attn_u"].reshape(NT, P, D).transpose(1, 0, 2)
    w_in = a["L0_attn_W_in"].T
    units = np.concatenate([w_in[:, 2 * DI:2 * DI + 2 * P], w_in[:, DI:2 * DI], w_in[:, :DI]], axis=1)
    units = by_rows(units.reshape(D, NWU, WU).transpose(1, 0, 2))
    taps = np.concatenate([a["L0_attn_conv_w"].reshape(-1, TAPS), a["L0_attn_conv_b"][:, None]], axis=1)
    taps = np.concatenate([taps[DI:], taps[:DI]]).reshape(NCH, P, TAPS + 1).transpose(1, 0, 2)
    heads = np.concatenate([a["L0_attn_dt_bias"], a["L0_attn_A_log"], a["L0_attn_D"]])
    w_out = by_rows(a["L0_attn_W_out"].T)
    return {
        "x": x,
        "w_router": by_rows(a["L0_ffn_W_router"]),
        "w_gate": by_rows(experts(a["L0_ffn_We_gate"], a["L0_ffn_Ws_gate"])),
        "w_up": by_rows(experts(a["L0_ffn_We_up"], a["L0_ffn_Ws_up"])),
        "w_down": np.concatenate([a["L0_ffn_We_down"], a["L0_ffn_Ws_down"].reshape(NS, FE, D)]),
        "w_in": units,
        "w_dt": by_rows(w_in[:, 2 * DI + 2 * P:]),
        "conv": taps,
        "heads": np.broadcast_to(heads, (P, heads.size)),
        "norm_w": a["L0_attn_norm_w"].reshape(KI, P).T,
        "w_out": w_out.reshape(P, 4, 2, D).transpose(1, 0, 2, 3),
    }


def kernel(**inputs):
    import numpy as np
    import concourse.bacc as bacc
    from concourse.bass_utils import run_bass_kernel_spmd
    nc = bacc.Bacc("TRN2", target_bir_lowering=False, num_devices=1)
    arrays, args = {}, []
    for name, a in arrange(inputs).items():
        a = np.ascontiguousarray(a)
        arrays[f"in_{name}"] = a
        args.append(nc.dram_tensor(f"in_{name}", a.shape, mybir.dt.from_np(a.dtype), kind="ExternalInput").ap())
    out = nc.dram_tensor("out", (P, NT, D), mybir.dt.float32, kind="ExternalOutput").ap()
    program(nc, *args, out)
    got = run_bass_kernel_spmd(nc, [arrays], core_ids=[0]).results[0]["out"]
    return got.transpose(1, 0, 2).reshape(BATCH, TOK // BATCH, D)
```

```python
import concourse.bass as bass
from concourse import mybir


P = 128
D = 512
KD = D // P
TOK = 2048
NT = TOK // P
NB = 4
TB = NT // NB
BATCH = 2
BPB = NB // BATCH
TPB = NT // BATCH
NE = 8
FE = 352
NS = 2
NX = NE + NS
TOPK = 2
TS = 2 * P
NTL = (TOPK * TOK + NE * (TS - 1)) // TS
SJ = NS * NB // 2
JOBS = SJ + NTL + SJ
SETS = NS + NTL + NS
FCH = [(0, 128), (128, 128), (256, 96)]
NF = len(FCH)
HEADS = 16
HD = 64
DI = HEADS * HD
KI = DI // P
NCH = 10
TAPS = 4
WU = 256
NWU = 9
HG = 4
GH = HEADS // HG
EPS = 1e-5
ROUTE = 0.5
DECAY_FLOOR = -120.0
MASKED = -30000.0
HALVES = [(0, 0), (0, 1), (1, 0)]
LOG1P = [1.0 / (2 * k + 1) for k in range(1, 9)]
PLAN = ("ffn", "mixer", "ffn")


class Chain:

    def __init__(self, eng, sem):
        self.eng, self.sem, self.count, self.turn = eng, sem, 0, 0

    def mark(self, ins):
        ins.then_inc(self.sem, 1)
        self.count += 1

    def join(self):
        self.eng.wait_ge(self.sem, self.turn + self.count)

    def step(self, ins):
        self.mark(ins)
        self.join()

    def enter(self, i, per_turn):
        self.turn, self.start, self.per_turn = i * per_turn, self.count, per_turn

    def leave(self, turns):
        assert self.count - self.start == self.per_turn, self.count - self.start
        self.count += (turns - 1) * self.per_turn
        self.turn = 0


def program(nc, x, w_router, w_gate, w_up, w_down, w_in, w_dt, conv, heads, norm_w, w_out, out):
    routed_x = nc.dram_tensor("routed_x", (NTL * TS, D), mybir.dt.float32, kind="Internal").ap()
    routed_y = nc.dram_tensor("routed_y", (NTL * TS, D), mybir.dt.float32, kind="Internal").ap()
    F, R, B16, U32 = mybir.dt.float32, mybir.dt.float32r, mybir.dt.bfloat16, mybir.dt.uint32
    ACT, ALU, AX = mybir.ActivationFunctionType, mybir.AluOpType, mybir.AxisListType

    def sb(name, shape, dt=F):
        return nc.alloc_sbuf_tensor(name, shape, dt)

    def sem(name):
        return nc.alloc_semaphore(name)

    def each(ap, n):
        return ap.rearrange("p (a o) -> p a o", o=1).broadcast_to([P, ap.shape[1], n])

    def some(ap, n):
        return ap.rearrange("p (o a) -> p o a", o=1).broadcast_to([P, n, ap.shape[1]])

    X = sb("X", [P, NT, D])
    ident = sb("ident", [P, P])
    iota = sb("iota", [P, 24])
    stats = sb("stats", [P, NT, 6])
    mv = sb("mv", [P, NT, 2])
    rstd = sb("rstd", [P, NT])
    mhalf = sb("mhalf", [P, NT])
    spare = sb("spare", [P, 1])
    spare2 = sb("spare2", [P, 5])
    zero = sb("zero", [P, 1])
    eps = sb("eps", [P, 1])
    by_di = sb("by_di", [P, 1])
    wr = sb("wr", [P, KD, NE])
    r_1 = sb("r_1", [P, NT])
    r_2 = sb("r_2", [P, NT])
    r_val = sb("r_val", [P, TOPK, NT])
    r_exp = sb("r_exp", [P, TOPK, NT])
    r_sum = sb("r_sum", [P, NT, NE], B16)
    r_cnt = sb("r_cnt", [P, NE])
    r_end = sb("r_end", [P, 2, 4 + NE])
    r_til = sb("r_til", [P, 4 + NE])
    r_pos = sb("r_pos", [P, TOPK * NT])
    slots = sb("slots", [P, TOPK * NT], U32)
    r_te = sb("r_te", [P, NTL])
    tile_e = sb("tile_e", [P, NTL], U32)
    stri_b = sb("stri_b", [P, P], B16)
    cw = sb("cw", [P, NCH, TAPS + 1])
    hp = sb("hp", [P, 3 * HEADS])
    nw = sb("nw", [P, KI])
    negA = sb("negA", [P, HEADS])
    tri = sb("tri", [P, P])
    tri_b = sb("tri_b", [P, P], B16)
    ones_b = sb("ones_b", [P, P], B16)
    ident_b = sb("ident_b", [P, P], B16)
    mask_b = sb("mask_b", [P, P], B16)

    arena = nc.sbuf_base

    def placer():
        at = [(arena + 63) // 64 * 64]

        def place(name, shape, dt=F):
            size = {F: 4, R: 4, U32: 4, B16: 2}[dt]
            for n in shape[1:]:
                size *= n
            t = nc.alloc_sbuf_tensor_at(name, shape, dt, offset=at[0])
            at[0] += (size + 63) // 64 * 64
            return t
        return place

    ff = placer()
    g_raw = ff("g_raw", [P, KD, FE])
    u_raw = ff("u_raw", [P, KD, FE])
    d_raw = ff("d_raw", [P, NF, D])
    g_hl = ff("g_hl", [P, 2, 2, KD, FE], R)
    u_hl = ff("u_hl", [P, 2, 2, KD, FE], R)
    d_hl = ff("d_hl", [P, 2, 2, NF, D], R)
    gate = ff("gate", [P, 2, D])
    hT = ff("hT", [P, 2, NF, D], R)
    tmpT = gate
    xn = ff("xn", [P, NT, D])
    XS = 2 * KD * D * 4
    xs0 = ff("xs0", [P, 2, KD, D], R)
    xs1 = ff("xs1", [P, 2, KD, D], R)
    xs = [xs0, xs1]
    xn_at, xs0_at, xs1_at = (t[:].tensor.manual_sbuf_range[0] for t in (xn, xs0, xs1))
    r_a = ff("r_a", [P, NT, NE])
    r_b = ff("r_b", [P, NT, NE])
    r_top = ff("r_top", [P, NT, NE])
    r_idx = ff("r_idx", [P, NT, NE], U32)
    r_msk = ff("r_msk", [P, TOPK * NT, NE])
    r_cmp = ff("r_cmp", [P, NTL, NE])
    zero_row = ff("zero_row", [P, D])
    xg = nc.alloc_sbuf_tensor_at("xg", [P, 2, 2, D], F, offset=xn_at)
    yg = nc.alloc_sbuf_tensor_at("yg", [P, 2, TOPK, D], F, offset=xn_at + 8 * D * 2)
    ys = nc.alloc_sbuf_tensor_at("ys", [P, 2, 2, D], F, offset=xs0_at)
    xgT = nc.alloc_sbuf_tensor_at("xgT", [P, 2, 2, KD, TS], R, offset=xs1_at)
    mx = placer()
    xb = mx("xb", [P, 2, KD, D], R)
    w_raw = mx("w_raw", [P, 2, KD, WU])
    w_hl = mx("w_hl", [P, 2, 2, KD, WU], R)
    wdt_raw = mx("wdt_raw", [P, KD, HEADS])
    wdt = mx("wdt", [P, 2, KD, HEADS], R)
    wo = mx("wo", [P, 2, KI, D], R)
    pre = mx("pre", [P, 2, TAPS - 1 + D])
    halo = mx("halo", [P, NCH, TAPS - 1])
    acc = mx("acc", [P, 2, D])
    xn_m = acc
    xc = mx("xc", [P, NCH, D])
    zs = mx("zs", [P, TB, DI])
    S = mx("S", [P, 2, DI])
    L = mx("L", [P, HEADS, P])
    xdt = mx("xdt", [P, DI])
    xw = mx("xw", [P, DI])
    xD = mx("xD", [P, DI])
    dtT = xD[0:HEADS, 0:D]
    GB = mx("GB", [P, 2 * P])
    Bt = GB[:, P:2 * P]
    y = mx("y", [P, 2, DI])
    ysq = mx("ysq", [P, DI], B16)
    yT = mx("yT", [P, 2, KI, P], R)
    ssq = mx("ssq", [P, 2])
    rs = mx("rs", [P, 2])
    NQ = TB * HEADS
    d_x = mx("d_x", [P, NQ])
    d_e = mx("d_e", [P, NQ])
    d_z = mx("d_z", [P, NQ])
    d_q = mx("d_q", [P, NQ])
    d_p = mx("d_p", [P, NQ])
    dts = mx("dts", [P, NQ])
    d_a = mx("d_a", [P, NQ])
    aparts = mx("aparts", [P, 3, NQ], B16)
    ncs = mx("ncs", [P, NQ])
    ecs = mx("ecs", [P, NQ])
    dec = mx("dec", [P, NQ])
    wd = mx("wd", [P, NQ])

    bank = [nc.alloc_psum_tensor(f"bank{i}", [P, 512], F) for i in range(8)]

    s_x = [sem(f"s_x{b}") for b in range(NB)]
    s_const = sem("s_const")
    c_pool = sem("c_pool")
    c_dve = sem("c_dve")
    c_act = sem("c_act")
    s_ready = sem("s_ready")
    READY = 6
    s_bf = sem("s_bf")
    s_out = sem("s_out")
    l_var = sem("l_var")
    l_rstd = sem("l_rstd")
    l_xn = sem("l_xn")
    l_tp = sem("l_tp")
    l_hi = sem("l_hi")
    l_lo = sem("l_lo")
    n_var = sem("n_var")
    n_rstd = sem("n_rstd")
    n_xn = sem("n_xn")
    n_tp = sem("n_tp")
    n_cp = sem("n_cp")
    n_lg = sem("n_lg")
    n_sh = sem("n_sh")
    n_ex = sem("n_ex")
    n_msk = sem("n_msk")
    n_rank = sem("n_rank")
    n_slot = sem("n_slot")
    d_zero = sem("d_zero")
    d_sc = sem("d_sc")
    b_tp = sem("b_tp")
    b_hi = sem("b_hi")
    b_lo0 = sem("b_lo0")
    b_lo1 = sem("b_lo1")
    f_graw, f_uraw, f_draw = sem("f_graw"), sem("f_uraw"), sem("f_draw")
    f_whi = sem("f_whi")
    f_wlo = sem("f_wlo")
    f_gu = sem("f_gu")
    f_silu = sem("f_silu")
    f_h = sem("f_h")
    f_hhi = sem("f_hhi")
    f_hlo = sem("f_hlo")
    f_dn = sem("f_dn")
    f_acc = sem("f_acc")
    t_xg = [sem(f"t_xg{q}") for q in range(2)]
    t_tp = sem("t_tp")
    t_hi = sem("t_hi")
    t_lo = sem("t_lo")
    t_dn = sem("t_dn")
    t_y = sem("t_y")
    t_st = [sem(f"t_st{q}") for q in range(2)]
    g_y = [sem(f"g_y{q}") for q in range(2)]
    g_add = sem("g_add")
    m_wo_raw = [sem(f"m_wo_raw{p}") for p in range(4)]
    m_wdt = sem("m_wdt")
    m_wdt_hi = sem("m_wdt_hi")
    m_wdt_lo = sem("m_wdt_lo")
    m_wo_n = sem("m_wo_n")
    m_wo_hi = sem("m_wo_hi")
    m_wo_lo = sem("m_wo_lo")
    m_raw = [sem(f"m_raw{q}") for q in range(2)]
    m_whi = sem("m_whi")
    m_wlo = sem("m_wlo")
    m_cp = sem("m_cp")
    m_pre = sem("m_pre")
    m_pre2 = sem("m_pre2")
    m_hin = sem("m_hin")
    m_hout = sem("m_hout")
    m_conv = sem("m_conv")
    m_xc = sem("m_xc")
    m_dtT = sem("m_dtT")
    m_dtc = sem("m_dtc")
    m_dtp = sem("m_dtp")
    m_dx = sem("m_dx")
    m_de = sem("m_de")
    m_ap = sem("m_ap")
    m_cs = sem("m_cs")
    m_ncs = sem("m_ncs")
    m_dec = sem("m_dec")
    m_zp = sem("m_zp")
    m_z = sem("m_z")
    m_B = sem("m_B")
    m_L = sem("m_L")
    m_G = sem("m_G")
    m_xt = sem("m_xt")
    m_Bt = sem("m_Bt")
    m_xdt = sem("m_xdt")
    m_xD = sem("m_xD")
    m_xw = sem("m_xw")
    m_C = sem("m_C")
    m_yc = sem("m_yc")
    m_yd = sem("m_yd")
    m_M = sem("m_M")
    m_D = sem("m_D")
    m_Sd = sem("m_Sd")
    m_S = sem("m_S")
    m_E = sem("m_E")
    m_yi = sem("m_yi")
    m_yg = sem("m_yg")
    m_sq = sem("m_sq")
    m_rs = sem("m_rs")
    m_F = sem("m_F")
    m_yhi = sem("m_yhi")
    m_ylo = sem("m_ylo")
    m_out = sem("m_out")
    m_res = sem("m_res")
    m_zero = sem("m_zero")

    H0, LO0, DN0, Y0, ST0 = 2, 2, 2, 2, 1
    EVEN, ODD = (NTL + 1) // 2, NTL // 2

    def phase_counts(k):
        return PLAN[:k].count("ffn"), PLAN[:k].count("mixer")

    def wait_residual(eng, k):
        nf, nm = phase_counts(k)
        if k and PLAN[k - 1] == "ffn":
            eng.wait_ge(f_acc, nf * 2 * SJ * TB)
            eng.wait_ge(g_add, nf * TOPK * NT)
        elif k:
            eng.wait_ge(m_res, nm * NT)

    def loop_waits(eng, i):
        def after(s, n, each_turn, unit=1):
            if isinstance(n, int) and n <= 0:
                return
            eng.wait_ge(s, (i * each_turn + n) * unit)

        def settle(*sems):
            for s, each_turn in sems:
                eng.wait_ge(s, i * each_turn + each_turn)
        return after, settle

    block = nc.Block()
    with block:

        @block.sync
        def _(sp):
            for b in range(NB):
                sp.dma_start(X[:, b * TB:(b + 1) * TB, :], x[:, b * TB:(b + 1) * TB, :]).then_inc(s_x[b], 16)
                if b == 0:
                    sp.dma_start(wr[:], w_router).then_inc(s_const, 16)
                    sp.dma_start(cw[:], conv).then_inc(s_const, 16)
                    sp.dma_start(hp[:], heads).then_inc(s_const, 16)
                    sp.dma_start(nw[:], norm_w).then_inc(s_const, 16)

            def ffn(k):
                nf, nm = phase_counts(k)
                g0 = nf * SETS
                wait_residual(sp, k)

                def load(e, g):
                    ds = bass.ds(e, 1)
                    if not isinstance(g, int) or g > 0:
                        sp.wait_ge(f_wlo, g * 3 - 2)
                    sp.dma_start(g_raw[:], w_gate[ds].rearrange("o p c n -> p (o c) n")).then_inc(f_graw, 16)
                    if not isinstance(g, int) or g > 0:
                        sp.wait_ge(f_wlo, g * 3 - 1)
                    sp.dma_start(u_raw[:], w_up[ds].rearrange("o p c n -> p (o c) n")).then_inc(f_uraw, 16)
                    if not isinstance(g, int) or g > 0:
                        sp.wait_ge(f_wlo, g * 3)
                    sp.dma_start(d_raw[:, 0:2, :], w_down[ds, 0:2 * P, :].rearrange("o (c p) n -> p (o c) n", p=P))\
                        .then_inc(f_draw, 16)
                    sp.dma_start(d_raw[0:FE - 2 * P, 2, :], w_down[ds, 2 * P:FE, :].rearrange("o p n -> p (o n)"))\
                        .then_inc(f_draw, 16)

                def rows(j, q):
                    sp.dma_start(xg[:, q], routed_x[bass.ds(j * TS, TS), :].rearrange("(a p) n -> p a n", p=P))\
                        .then_inc(t_xg[q], 16)

                load(NE, g0)
                load(NE + 1, g0 + 1)
                if nf == 0:
                    sp.wait_ge(s_ready, READY)
                    sp.dma_start(routed_x.rearrange("(a p) n -> p a n", p=P), some(zero_row[:], NTL * TS // P))\
                        .then_inc(d_zero, 16)
                sp.wait_ge(n_slot, 2 * (nf + 1))
                sp.wait_ge(d_sc, (nf + 1) * TOPK * NT * 16)
                rows(0, 0)
                rows(1, 1)
                load(sp.value_load(tile_e[0:1, 0:1], min_val=0, max_val=NE - 1), g0 + NS)
                load(sp.value_load(tile_e[0:1, 1:2], min_val=0, max_val=NE - 1), g0 + NS + 1)
                with sp.Fori(1, NTL // 2) as i:
                    for q in range(2):
                        j = i * 2 + q
                        sp.wait_ge(t_tp, (i * 2 + (nf * NTL + q - 1)) * 2)
                        rows(j, q)
                        load(sp.value_load(tile_e[0:1, bass.ds(j, 1)], min_val=0, max_val=NE - 1), i * 2 + (g0 + NS + q))
                sp.wait_ge(t_tp, (nf * NTL + NTL - 2) * 2)
                rows(NTL - 1, 0)
                load(sp.value_load(tile_e[0:1, NTL - 1:NTL], min_val=0, max_val=NE - 1), g0 + NS + NTL - 1)
                load(NE, g0 + NS + NTL)
                load(NE + 1, g0 + NS + NTL + 1)

            def mixer(k):
                wait_residual(sp, k)
                sp.dma_start(wdt_raw[:], w_dt).then_inc(m_wdt, 16)
                for piece in range(4):
                    if piece >= 2:
                        sp.wait_ge(m_wo_lo, piece - 1)
                    sp.dma_start(w_raw[:, piece % 2].rearrange("p (k a) n -> p k (a n)", k=2), w_out[piece])\
                        .then_inc(m_wo_raw[piece], 16)
                sp.wait_ge(m_wo_lo, 4)
                for j in range(2):
                    sp.dma_start(w_raw[:, j], w_in[j]).then_inc(m_raw[j], 16)
                with sp.Fori(0, BPB * NWU - 1) as i:
                    for q in range(2):
                        w = i * 2 + 2 + q
                        sp.wait_ge(m_wlo, w - 1)
                        u = sp.snap(w % NWU)
                        sp.dma_start(w_raw[:, q], w_in[bass.ds(u, 1), :, :, :].rearrange("o p c n -> p (o c) n"))\
                            .then_inc(m_raw[q], 16)

            for k, what in enumerate(PLAN):
                (ffn if what == "ffn" else mixer)(k)
            for b in range(NB):
                wait_residual(sp, len(PLAN))
                sp.dma_start(out[:, b * TB:(b + 1) * TB, :], X[:, b * TB:(b + 1) * TB, :]).then_inc(s_out, 16)
            sp.wait_ge(s_out, NB * 16)

        @block.gpsimd
        def _(pool):
            own = Chain(pool, c_pool)
            slot_rows = lambda c: bass.IndirectOffsetOnAxis(ap=slots[:, c:c + 1], axis=0)
            pool.memset(mhalf[:], -0.5).then_inc(s_ready, 1)
            pool.memset(zero_row[:], 0.0).then_inc(s_ready, 1)
            pool.memset(r_end[:], 0.0).then_inc(s_ready, 1)
            pool.memset(r_til[:], 0.0).then_inc(s_ready, 1)
            pool.memset(spare[:], 0.0).then_inc(f_h, H0)
            pool.memset(spare2[:, 0:1], 0.0).then_inc(f_hlo, LO0)
            pool.memset(spare2[:, 1:2], 0.0).then_inc(t_dn, DN0)
            pool.memset(spare2[:, 2:3], 0.0).then_inc(t_y, Y0)
            for q in range(2):
                pool.memset(spare2[:, 3 + q:4 + q], 0.0).then_inc(t_st[q], ST0)
            own.mark(pool.memset(zero[:], 0.0))
            own.mark(pool.memset(eps[:], EPS))
            own.mark(pool.memset(by_di[:], 1.0 / DI))
            for e in range(24):
                own.mark(pool.memset(iota[:, e:e + 1], float(e)))
            own.mark(pool.memset(ident[:], 0.0))
            own.mark(pool.memset(tri[:], 1.0))
            own.join()
            pool.affine_select(out=ident[:], in_=ident[:], compare_op=ALU.not_equal, fill=1.0, base=0,
                               pattern=[[-1, P]], channel_multiplier=1).then_inc(s_ready, 1)
            pool.affine_select(out=tri[:], in_=tri[:], compare_op=ALU.is_ge, fill=0.0, base=0,
                               pattern=[[1, P]], channel_multiplier=-1).then_inc(s_ready, 1)
            pool.wait_ge(s_ready, READY)

            def rsqrt_ln(tiles, signal):
                n = tiles.stop - tiles.start
                own.step(pool.tensor_tensor(rstd[:, tiles], rstd[:, tiles], eps[:].broadcast_to([P, n]), ALU.add))
                pool.tensor_tensor(rstd[:, tiles], rstd[:, tiles], mhalf[:, 0:n], ALU.pow).then_inc(signal, 1)

            def ffn(k):
                nf, nm = phase_counts(k)
                g0 = nf * SETS

                def weights(piece, g, parity):
                    raw, hl = ((g_raw, g_hl), (u_raw, u_hl), (d_raw, d_hl))[piece]
                    pool.wait_ge(f_whi, g * 3 + (piece + 1))
                    if piece < 2:
                        pool.tensor_tensor(hl[:, parity, 1], raw[:], hl[:, parity, 0].bitcast(F), ALU.subtract)\
                            .then_inc(f_wlo, 1)
                    else:
                        fw = FE - 2 * P
                        pool.tensor_tensor(hl[:, parity, 1, 0:2], raw[:, 0:2], hl[:, parity, 0, 0:2].bitcast(F),
                                           ALU.subtract)
                        pool.tensor_tensor(hl[0:fw, parity, 1, 2], raw[0:fw, 2], hl[0:fw, parity, 0, 2].bitcast(F),
                                           ALU.subtract).then_inc(f_wlo, 1)

                for b in range(NB):
                    pool.wait_ge(n_var, nf * NB + b + 1)
                    rsqrt_ln(slice(b * TB, (b + 1) * TB), n_rstd)
                    if b < 2:
                        for t in range(b * TB, (b + 1) * TB):
                            pool.wait_ge(b_hi, nf * NT + t + 1)
                            pool.tensor_tensor(xs[b][:, 1, :, t % TB * P:(t % TB + 1) * P],
                                               tmpT[:, t % 2].rearrange("p (c t) -> p c t", c=KD),
                                               xs[b][:, 0, :, t % TB * P:(t % TB + 1) * P].bitcast(F),
                                               ALU.subtract).then_inc(b_lo0, 1)
                for piece in range(3):
                    weights(piece, g0, 0)
                for piece in range(3):
                    weights(piece, g0 + 1, 1)
                pool.wait_ge(n_slot, 2 * (nf + 1))
                pool.wait_ge(n_xn, (nf + 1) * NT)
                pool.wait_ge(d_zero, 16)
                for c in range(TOPK * NT):
                    pool.indirect_dma_start(routed_x, slot_rows(c), xn[:, c % NT], None).then_inc(d_sc, 16)
                for piece in range(3):
                    weights(piece, g0 + NS, 0)
                with pool.Fori(0, NTL // 2) as i:
                    for q in range(2):
                        for piece in range(3):
                            weights(piece, i * 2 + (g0 + NS + q + 1), (q + 1) % 2)
                for piece in range(3):
                    weights(piece, g0 + NS + NTL, 1)
                pool.wait_ge(t_st[0], (nf + 1) * EVEN * 16 + ST0)
                pool.wait_ge(t_st[1], (nf + 1) * ODD * 16 + ST0)
                pool.wait_ge(t_tp, (nf + 1) * NTL * 2)
                for t in range(NT):
                    if t == 2:
                        for piece in range(3):
                            weights(piece, g0 + NS + NTL + 1, 0)
                    if t >= 2:
                        pool.wait_ge(g_add, (nf * NT + t - 1) * TOPK)
                    for slot in range(TOPK):
                        pool.indirect_dma_start(yg[:, t % 2, slot], None, routed_y, slot_rows(slot * NT + t))\
                            .then_inc(g_y[t % 2], 16)

            def mixer(k):
                _, nm = phase_counts(k)
                wait_residual(pool, k)
                zeros3 = zero[:].broadcast_to([P, TAPS - 1])

                def turn(i):
                    after, settle = loop_waits(pool, i)
                    pool.tensor_tensor(S[:, 0], zero[:].broadcast_to([P, DI]), zero[:].broadcast_to([P, DI]), ALU.add)\
                        .then_inc(m_zero, 1)

                    def unit_lo(w):
                        after(m_whi, w + 1, BPB * NWU)
                        pool.tensor_tensor(w_hl[:, w % 2, 1], w_raw[:, w % 2], w_hl[:, w % 2, 0].bitcast(F),
                                           ALU.subtract).then_inc(m_wlo, 1)

                    def halos(n, c):
                        after(m_conv, n - 1, BPB * NCH)
                        head = pre[:, c % 2, 0:TAPS - 1]
                        if j == 0:
                            pool.tensor_tensor(head, zeros3, zeros3, ALU.add).then_inc(m_hin, 1)
                        else:
                            after(m_hout, c + 1, NCH * (BPB - 1))
                            pool.tensor_tensor(head, halo[:, c], zeros3, ALU.add).then_inc(m_hin, 1)
                        if j < BPB - 1:
                            after(m_pre, n + 1, BPB * NCH)
                            pool.tensor_tensor(halo[:, c], pre[:, c % 2, D:D + TAPS - 1], zeros3, ALU.add)\
                                .then_inc(m_hout, 1)

                    def rms(n):
                        after(m_sq, n + 1, TPB)
                        it = slice(n % 2, n % 2 + 1)
                        own.step(pool.tensor_tensor(rs[:, it], ssq[:, it], by_di[:], ALU.mult))
                        own.step(pool.tensor_tensor(rs[:, it], rs[:, it], eps[:], ALU.add))
                        pool.tensor_tensor(rs[:, it], rs[:, it], mhalf[:, 0:1], ALU.pow).then_inc(m_rs, 1)

                    unit_lo(0)
                    for j in range(BPB):
                        for u in range(NWU):
                            w = j * NWU + u
                            if w + 1 < BPB * NWU:
                                unit_lo(w + 1)
                            if u < 5:
                                halos(j * NCH + 2 * u, 2 * u)
                                halos(j * NCH + 2 * u + 1, 2 * u + 1)
                            if u == 0 and j:
                                rms(j * TB - 1)
                        for q in range(TB):
                            n = j * TB + q
                            hq = slice(q * HEADS, (q + 1) * HEADS)
                            pool.wait_ge(l_var, i * TPB + (n + TB + 1))
                            rsqrt_ln(slice(q, q + 1), l_rstd)
                            after(m_dec, j + 1, BPB)
                            after(m_C, n, TPB)
                            after(m_S, n, TPB)
                            pool.wait_ge(m_zero, i + 1)
                            pool.tensor_tensor(S[:, (n + 1) % 2].rearrange("p (h d) -> p h d", d=HD),
                                               S[:, n % 2].rearrange("p (h d) -> p h d", d=HD),
                                               each(dec[:, hq], HD), ALU.mult).then_inc(m_Sd, 1)
                            after(m_xdt, n + 1, TPB)
                            after(m_D, n, TPB)
                            pool.tensor_tensor(xw[:].rearrange("p (h d) -> p h d", d=HD),
                                               xdt[:].rearrange("p (h d) -> p h d", d=HD),
                                               each(wd[:, hq], HD), ALU.mult).then_inc(m_xw, 1)
                            if q >= 1:
                                rms(n - 1)
                            after(m_yc, n + 1, TPB)
                            after(m_xD, n + 1, TPB)
                            pool.tensor_tensor(y[:, n % 2], y[:, n % 2], xD[:], ALU.add).then_inc(m_yd, 1)
                            after(m_yi, n + 1, TPB)
                            after(m_z, 8 * (j + 1), 8 * BPB)
                            pool.tensor_tensor(y[:, n % 2], y[:, n % 2], zs[:, q], ALU.mult).then_inc(m_yg, 1)
                    rms(TPB - 1)
                    settle((m_C, TPB), (m_S, TPB), (m_conv, BPB * NCH), (m_D, TPB))

                for q in range(TB):
                    pool.wait_ge(l_var, q + 1)
                    rsqrt_ln(slice(q, q + 1), l_rstd)
                with pool.Fori(0, BATCH) as i:
                    own.enter(i, TPB * 3)
                    turn(i)
                own.leave(BATCH)

            for k, what in enumerate(PLAN):
                (ffn if what == "ffn" else mixer)(k)

        @block.scalar
        def _(act):
            act.wait_ge(s_const, 4 * 16)
            own = Chain(act, c_act)
            own.step(act.activation(negA[:], hp[:, HEADS:2 * HEADS], ACT.Exp))

            def split_hi(dst, src, signal):
                act.activation(dst, src, ACT.Copy).then_inc(signal, 1)

            def ffn(k):
                nf, nm = phase_counts(k)
                g0, j0 = nf * SETS, nf * JOBS
                wait_residual(act, k)

                def weights(piece, g, parity):
                    raw, hl, arrived, n = ((g_raw, g_hl, f_graw, 16), (u_raw, u_hl, f_uraw, 16),
                                           (d_raw, d_hl, f_draw, 32))[piece]
                    act.wait_ge(arrived, (g + 1) * n)
                    if piece < 2:
                        split_hi(hl[:, parity, 0], raw[:], f_whi)
                    else:
                        act.activation(hl[:, parity, 0, 0:2], raw[:, 0:2], ACT.Copy)
                        split_hi(hl[0:FE - 2 * P, parity, 0, 2], raw[0:FE - 2 * P, 2], f_whi)

                for t in range(NT):
                    n = nf * NT + t
                    act.wait_ge(n_tp, n + 1)
                    if t >= 2:
                        act.wait_ge(n_lg, n - 1)
                        act.wait_ge(b_lo0, nf * 2 * TB + min(t - 1, 2 * TB))
                    act.activation(tmpT[:, t % 2], bank[t % 4][:], ACT.Copy).then_inc(n_cp, 1)
                    if t < 2 * TB:
                        split_hi(xs[t // TB][:, 0, :, t % TB * P:(t % TB + 1) * P],
                                 bank[t % 4][:].rearrange("p (c t) -> p c t", c=KD), b_hi)
                    if t in (1, 3, 5):
                        weights(t // 2, g0, 0)
                act.wait_ge(n_sh, nf + 1)
                act.activation(r_b[:], r_a[:], ACT.Exp).then_inc(n_ex, 1)

                def chunk(job, c, par, width, before):
                    fw = FCH[c][1]
                    v = job * NF + c
                    act.wait_ge(f_gu, v + 1)
                    act.wait_ge(f_hlo, v - 1 + LO0)
                    act.activation(gate[0:fw, par, 0:width], bank[par][0:fw, 0:width], ACT.Silu).then_inc(f_silu, 1)
                    act.wait_ge(f_h, v + 1 + H0)
                    if c == 0 and before:
                        act.wait_ge(*before)
                    split_hi(hT[0:fw, 0, c, 0:width], gate[0:fw, par, 0:width], f_hhi)

                def x_hi(t, bk):
                    act.wait_ge(b_tp, nf * 2 * TB + t - 2 * TB + 1)
                    split_hi(xs[(t // TB + 1) % 2][:, 0, :, t % TB * P:(t % TB + 1) * P],
                             bank[bk][:].rearrange("p (c t) -> p c t", c=KD), b_hi)

                def rows_hi(j, q, banks):
                    for a in range(2):
                        act.wait_ge(t_tp, (j + nf * NTL) * 2 + (a + 1))
                        split_hi(xgT[:, q, 0, :, a * P:(a + 1) * P],
                                 bank[banks[a]][:].rearrange("p (c t) -> p c t", c=KD), t_hi)

                def results(j, q, before):
                    for a in range(2):
                        act.wait_ge(t_dn, (j + nf * NTL) * 2 + (a + 1 + DN0))
                        if a == 0:
                            act.wait_ge(t_st[q], before * 16 + ST0)
                        act.activation(ys[:, q, a], bank[4 + a][:], ACT.Copy).then_inc(t_y, 1)
                    act.wait_ge(t_y, (j + nf * NTL + 1) * 2 + Y0)
                    act.dma_start(routed_y[bass.ds(j * TS, TS), :].rearrange("(a p) n -> p a n", p=P), ys[:, q])\
                        .then_inc(t_st[q], 16)

                for job in range(SJ):
                    for c in range(NF):
                        chunk(j0 + job, c, (job * NF + c) % 2, D, (f_dn, (nf * 2 * SJ + job) * TB) if job else None)
                        if job == 0:
                            weights(c, g0 + 1, 1)
                        if job == SJ // 2:
                            weights(c, g0 + NS, 0)
                weights(0, g0 + NS + 1, 1)
                par = (SJ * NF) % 2
                rows_hi(0, 0, (par, 2 + par))
                act.wait_ge(f_dn, (nf * 2 + 1) * SJ * TB)

                def tile(j, q, half, last):
                    job = j + (j0 + SJ)
                    for c in range(NF):
                        chunk(job, c, (q * NF + c) % 2, TS, (t_dn, (j + nf * NTL) * 2 + DN0))
                        if c == 0 and not last:
                            rows_hi(j + 1, (q + 1) % 2, (6, 7))
                        if c < 2:
                            weights(c + 1, j + (g0 + NS + 1), (q + 1) % 2)
                        else:
                            weights(0, j + (g0 + NS + 2), q)
                    if last:
                        for t, bk in zip(range(2 * TB, 3 * TB), late_banks):
                            x_hi(t, bk)
                    results(j, q, half + nf * (EVEN, ODD)[q])

                late_banks = ((NTL * NF) % 2, 2 + (NTL * NF) % 2, 6, 7)
                with act.Fori(0, NTL // 2) as i:
                    for q in range(2):
                        tile(i * 2 + q, q, i, False)
                tile(NTL - 1, 0, NTL // 2, True)

                for job in range(SJ):
                    v = (SJ + NTL + job) * NF
                    for c in range(NF):
                        chunk(j0 + SJ + NTL + job, c, (v + c) % 2, D,
                              (f_dn, ((nf * 2 + 1) * SJ + job) * TB) if job else (t_dn, (nf + 1) * NTL * 2 + DN0))
                        if job == 0 and c < 2:
                            weights(c + 1, g0 + NS + NTL + 1, 0)
                    if job == 0:
                        act.wait_ge(t_st[0], (nf + 1) * EVEN * 16 + ST0)
                        act.wait_ge(t_st[1], (nf + 1) * ODD * 16 + ST0)
                        for a in range(TB):
                            x_hi(3 * TB + a, (v + 1) % 2 + 2 * (a % 2))

            def mixer(k):
                _, nm = phase_counts(k)
                wait_residual(act, k)
                for piece in range(4):
                    act.wait_ge(m_wo_n, piece + 1)
                    split_hi(wo[:, 0, 2 * piece:2 * piece + 2],
                             w_raw[:, piece % 2].rearrange("p (k a) n -> p k (a n)", k=2), m_wo_hi)

                def turn(i):
                    after, settle = loop_waits(act, i)

                    def unit_hi(w):
                        after(m_raw[w % 2], w // 2 + 1, BPB * NWU // 2, unit=16)
                        if w >= 2:
                            jj, u = divmod(w - 2, NWU)
                            if u < 5:
                                after(m_cp, jj * NCH + 2 * u + 2, BPB * NCH)
                            else:
                                after(m_zp, jj * 8 + (u - 5) * 2 + 2, 8 * BPB)
                        split_hi(w_hl[:, w % 2, 0], w_raw[:, w % 2], m_whi)

                    def conv_in(n, c):
                        b = bank[c % 2]
                        after(m_cp, n + 1, BPB * NCH)
                        after(m_conv, n - 1, BPB * NCH)
                        after(m_hout, min(n - 1, NCH), NCH * (BPB - 1))
                        act.activation(pre[:, c % 2, TAPS - 1:], b[:], ACT.Copy).then_inc(m_pre, 1)
                        after(m_xc, n - 1, BPB * NCH)
                        act.activation(acc[:, c % 2], b[:], ACT.Identity, bias=cw[:, c, TAPS:TAPS + 1],
                                       scale=cw[:, c, TAPS - 1:TAPS]).then_inc(m_pre2, 1)

                    def conv_out(n, c):
                        after(m_conv, n + 1, BPB * NCH)
                        act.activation(xc[:, c], acc[:, c % 2], ACT.Silu).then_inc(m_xc, 1)

                    def y_hi(n):
                        for half in range(2):
                            after(m_F, 2 * n + half + 1, 2 * TPB)
                            after(m_out, n, TPB)
                            split_hi(yT[:, 0, 4 * half:4 * half + 4],
                                     bank[6 + half][:].rearrange("p (c t) -> p c t", c=4), m_yhi)

                    def squares(n):
                        after(m_yg, n + 1, TPB)
                        after(m_rs, n - 1, TPB)
                        after(m_sq, n, TPB)
                        act.activation(ysq[:], y[:, n % 2], ACT.Square, accum_out=ssq[:, n % 2:n % 2 + 1]).then_inc(m_sq, 1)

                    unit_hi(0)
                    for j in range(BPB):
                        for u in range(NWU):
                            w = j * NWU + u
                            if w + 1 < BPB * NWU:
                                unit_hi(w + 1)
                            if u < 5:
                                for c in (2 * u, 2 * u + 1):
                                    n = j * NCH + c
                                    conv_in(n, c)
                                    if c == 1:
                                        after(m_D, j * TB, TPB)
                                    if c >= 1:
                                        conv_out(n - 1, c - 1)
                                if u == 0 and j:
                                    y_hi(j * TB - 1)
                                    squares(j * TB - 1)
                                if u == 1:
                                    after(m_dtT, j + 1, BPB)
                                    after(m_yd, j * TB, TPB)
                                    act.activation(dtT, bank[3][0:HEADS, :], ACT.Copy).then_inc(m_dtc, 1)
                                if u == 4:
                                    after(m_dx, j + 1, BPB)
                                    act.activation(d_e[:], d_z[:], ACT.Exp).then_inc(m_de, 1)
                            else:
                                if u == 5:
                                    conv_out(j * NCH + NCH - 1, NCH - 1)
                                    after(m_yg, j * TB, TPB)
                                for half in range(2):
                                    n = j * 8 + (u - 5) * 2 + half
                                    after(m_zp, n + 1, 8 * BPB)
                                    act.activation(zs[:, 2 * half:2 * half + 2, (u - 5) * WU:(u - 4) * WU],
                                                   bank[6 + half][:].rearrange("p (q n) -> p q n", q=2),
                                                   ACT.Silu).then_inc(m_z, 1)
                        after(m_cs, j + 1, BPB)
                        after(m_ncs, j + 1, BPB)
                        cs, tot = bank[2][:, NQ:2 * NQ], bank[2][:, 2 * NQ:3 * NQ]
                        act.activation(ecs[:], cs, ACT.Exp)
                        act.activation(dec[:], tot, ACT.Exp)
                        act.activation(wd[:], d_p[:], ACT.Exp).then_inc(m_dec, 1)
                        for q in range(TB):
                            n = j * TB + q
                            for g in range(HG):
                                after(m_B, HG * n + g + 1, HG * TPB)
                                after(m_E, n, TPB)
                                for h in range(g * GH, (g + 1) * GH):
                                    ins = act.activation(L[:, h], bank[g % 2][:, (h % GH) * P:(h % GH + 1) * P], ACT.Exp,
                                                         bias=ncs[:, q * HEADS + h:q * HEADS + h + 1])
                                ins.then_inc(m_L, 1)
                                if g == 0:
                                    after(m_G, n + 1, TPB)
                                    after(m_D, n, TPB)
                                    after(m_M, HG * n, HG * TPB)
                                    act.activation(GB[:], bank[3][:, 0:2 * P], ACT.Copy).then_inc(m_Bt, 1)
                                if g == 1 and q >= 1:
                                    y_hi(n - 1)
                            if q >= 1:
                                squares(n - 1)
                            act.wait_ge(l_tp, i * TPB + (n + TB + 1))
                            split_hi(xb[:, 0, :, q * P:(q + 1) * P], bank[3][:].rearrange("p (c t) -> p c t", c=KD), l_hi)
                    y_hi(TPB - 1)
                    squares(TPB - 1)
                    settle((m_zp, 8 * BPB), (m_conv, BPB * NCH), (m_hout, NCH * (BPB - 1)), (m_xc, BPB * NCH),
                           (m_yg, TPB), (m_D, TPB), (m_E, TPB), (m_M, HG * TPB), (m_rs, TPB), (m_sq, TPB),
                           (m_out, TPB), (m_yd, TPB))

                act.wait_ge(m_wdt, 16)
                split_hi(wdt[:, 0], wdt_raw[:], m_wdt_hi)
                for q in range(TB):
                    act.wait_ge(l_tp, q + 1)
                    split_hi(xb[:, 0, :, q * P:(q + 1) * P], bank[4 + q % 2][:].rearrange("p (c t) -> p c t", c=KD), l_hi)
                with act.Fori(0, BATCH) as i:
                    turn(i)

            for k, what in enumerate(PLAN):
                (ffn if what == "ffn" else mixer)(k)

        @block.vector
        def _(dve):
            own = Chain(dve, c_dve)

            def ln_stats(tiles, places, signal):
                for xt, s in zip(tiles, places):
                    own.mark(dve.bn_stats(stats[:, s, :], xt))
                own.join()
                dve.tensor_copy(spare[:], mhalf[:, 0:1])
                for s in places:
                    own.mark(dve.bn_aggr(mv[:, s, :], stats[:, s, :]))
                own.join()
                dve.tensor_copy(rstd[:, places[0]:places[-1] + 1],
                                mv[:, places[0]:places[-1] + 1, 1:2].rearrange("p t o -> p (t o)")).then_inc(signal, 1)

            def ln_scale(dst, xt, s):
                return dve.tensor_scalar(dst, xt, mv[:, s, 0:1], rstd[:, s:s + 1], ALU.subtract, ALU.mult)

            def lo_half(hl_lo, value, hl_hi, signal):
                dve.tensor_tensor(hl_lo, value, hl_hi.bitcast(F), ALU.subtract).then_inc(signal, 1)

            def ffn(k):
                nf, nm = phase_counts(k)
                j0 = nf * JOBS
                wait_residual(dve, k)

                def block_stats(b):
                    if k == 0:
                        dve.wait_ge(s_x[b], 16)
                    tiles = range(b * TB, (b + 1) * TB)
                    ln_stats([X[:, t, :] for t in tiles], tiles, n_var)

                block_stats(0)
                for b in range(NB):
                    if b + 1 < NB:
                        block_stats(b + 1)
                    dve.wait_ge(n_rstd, nf * NB + b + 1)
                    for t in range(b * TB, (b + 1) * TB):
                        ln_scale(xn[:, t], X[:, t, :], t).then_inc(n_xn, 1)

                def choose():
                    logits = bank[4][:, 0:NT * NE].rearrange("p (t e) -> p t e", e=NE)
                    dve.wait_ge(n_lg, (nf + 1) * NT)
                    own.step(dve.tensor_reduce(r_1[:], logits, AX.X, ALU.max))
                    dve.tensor_tensor(r_a[:], logits, each(r_1[:], NE), ALU.subtract).then_inc(n_sh, 1)
                    dve.wait_ge(n_ex, nf + 1)
                    own.step(dve.tensor_reduce(r_1[:], r_b[:], AX.X, ALU.add))
                    own.step(dve.reciprocal(r_2[:], r_1[:]))
                    own.step(dve.tensor_tensor(r_a[:], r_b[:], each(r_2[:], NE), ALU.mult))
                    for t in range(NT):
                        own.mark(dve.max(r_top[:, t], r_a[:, t]))
                    own.join()
                    for t in range(NT):
                        own.mark(dve.max_index(r_idx[:, t], r_top[:, t], r_a[:, t]))
                    own.join()
                    for slot in range(TOPK):
                        own.mark(dve.tensor_scalar(r_val[:, slot], r_top[:, :, slot], ROUTE, None, ALU.mult))
                        own.mark(dve.tensor_copy(r_exp[:, slot], r_idx[:, :, slot]))
                    own.join()
                    own.step(dve.tensor_tensor(r_msk[:], some(iota[:, 0:NE], TOPK * NT),
                                               each(r_exp[:].rearrange("p s t -> p (s t)"), NE), ALU.is_equal))
                    dve.tensor_tensor(r_sum[:], r_msk[:, 0:NT], r_msk[:, NT:2 * NT], ALU.add).then_inc(n_msk, 1)

                def place_rows():
                    rank = bank[7][:, 0:NT * NE].rearrange("p (t e) -> p t e", e=NE)
                    dve.wait_ge(n_rank, nf + 1)
                    own.step(dve.tensor_copy(r_cnt[:], bank[7][:, NT * NE:NT * NE + NE]))
                    own.step(dve.tensor_scalar(r_1[:, 0:NE], iota[:, 0:NE], float(TS), None, ALU.mult))
                    own.step(dve.tensor_tensor(r_cmp[:, 0:NE], each(r_cnt[:], NE), some(r_1[:, 0:NE], NE), ALU.is_gt))
                    own.step(dve.tensor_reduce(r_til[:, 4:], r_cmp[:, 0:NE], AX.X, ALU.add))
                    own.step(dve.tensor_tensor(r_end[:, 0, 4:], r_til[:, 4:], r_til[:, 3:3 + NE], ALU.add))
                    own.step(dve.tensor_tensor(r_end[:, 1, 4:], r_end[:, 0, 4:], r_end[:, 0, 2:2 + NE], ALU.add))
                    own.step(dve.tensor_tensor(r_end[:, 0, 4:], r_end[:, 1, 4:], r_end[:, 1, 0:NE], ALU.add))
                    own.step(dve.tensor_tensor(r_1[:, 0:NE], r_end[:, 0, 4:], r_til[:, 4:], ALU.subtract))
                    own.step(dve.tensor_scalar(r_1[:, 0:NE], r_1[:, 0:NE], float(TS), None, ALU.mult))
                    own.step(dve.tensor_tensor(r_b[:], rank, some(r_1[:, 0:NE], NT), ALU.add))
                    for slot in range(TOPK):
                        own.mark(dve.tensor_tensor(r_msk[:, slot * NT:(slot + 1) * NT], r_msk[:, slot * NT:(slot + 1) * NT],
                                                   r_b[:], ALU.mult))
                    own.join()
                    own.step(dve.tensor_reduce(r_pos[:], r_msk[:], AX.X, ALU.add))
                    dve.tensor_copy(slots[:], r_pos[:]).then_inc(n_slot, 1)
                    own.step(dve.tensor_tensor(r_cmp[:], each(iota[:, 0:NTL], NE), some(r_end[:, 0, 4:], NTL), ALU.is_ge))
                    own.step(dve.tensor_reduce(r_te[:], r_cmp[:], AX.X, ALU.add))
                    own.step(dve.tensor_scalar(r_te[:], r_te[:], float(NE - 1), None, ALU.min))
                    dve.tensor_copy(tile_e[:], r_te[:]).then_inc(n_slot, 1)

                def chunk(job, c, par, width):
                    fw = FCH[c][1]
                    v = job * NF + c
                    dve.wait_ge(f_silu, v + 1)
                    dve.tensor_tensor(gate[0:fw, par, 0:width], gate[0:fw, par, 0:width], bank[2 + par][0:fw, 0:width],
                                      ALU.mult).then_inc(f_h, 1)
                    dve.wait_ge(f_hhi, v + 1)
                    lo_half(hT[0:fw, 1, c, 0:width], gate[0:fw, par, 0:width], hT[0:fw, 0, c, 0:width], f_hlo)

                n_acc, n_add = [nf * 2 * SJ * TB], [nf * TOPK * NT]

                def residual_written():
                    dve.wait_ge(f_acc, n_acc[0])
                    dve.wait_ge(g_add, n_add[0])

                def add_shared(b):
                    for a in range(TB):
                        t = b * TB + a
                        dve.wait_ge(f_dn, n_acc[0] + 1)
                        residual_written()
                        dve.scalar_tensor_tensor(X[:, t, :], bank[4 + a][:], ROUTE, X[:, t, :], ALU.mult, ALU.add)\
                            .then_inc(f_acc, 1)
                        n_acc[0] += 1

                def add_routed(t):
                    dve.wait_ge(g_y[t % 2], (nf * NT // 2 + t // 2 + 1) * TOPK * 16)
                    for slot in range(TOPK):
                        residual_written()
                        dve.scalar_tensor_tensor(X[:, t, :], yg[:, t % 2, slot], r_val[:, slot, t:t + 1], X[:, t, :],
                                                 ALU.mult, ALU.add).then_inc(g_add, 1)
                        n_add[0] += 1

                def x_lo(t, bk):
                    dve.wait_ge(b_hi, nf * NT + t + 1)
                    lo_half(xs[(t // TB + 1) % 2][:, 1, :, t % TB * P:(t % TB + 1) * P],
                            bank[bk][:].rearrange("p (c t) -> p c t", c=KD),
                            xs[(t // TB + 1) % 2][:, 0, :, t % TB * P:(t % TB + 1) * P], b_lo1)

                def rows_lo(j, q, banks):
                    for a in range(2):
                        dve.wait_ge(t_hi, (j + nf * NTL) * 2 + (a + 1))
                        lo_half(xgT[:, q, 1, :, a * P:(a + 1) * P],
                                bank[banks[a]][:].rearrange("p (c t) -> p c t", c=KD),
                                xgT[:, q, 0, :, a * P:(a + 1) * P], t_lo)

                choose()
                for job in range(SJ):
                    for c in range(NF):
                        chunk(j0 + job, c, (job * NF + c) % 2, D)
                    if job == 0:
                        place_rows()
                    if job < SJ - 1:
                        add_shared(job % 2)
                par = (SJ * NF) % 2
                rows_lo(0, 0, (par, 2 + par))
                add_shared((SJ - 1) % 2)

                def tile(j, q, last):
                    job = j + (j0 + SJ)
                    for c in range(NF):
                        chunk(job, c, (q * NF + c) % 2, TS)
                        if c == 0 and not last:
                            rows_lo(j + 1, (q + 1) % 2, (6, 7))

                with dve.Fori(0, NTL // 2) as i:
                    for q in range(2):
                        tile(i * 2 + q, q, False)
                tile(NTL - 1, 0, True)
                for t, bk in zip(range(2 * TB, 3 * TB), ((NTL * NF) % 2, 2 + (NTL * NF) % 2, 6, 7)):
                    x_lo(t, bk)
                for job in range(SJ):
                    v = (SJ + NTL + job) * NF
                    for c in range(NF):
                        chunk(j0 + SJ + NTL + job, c, (v + c) % 2, D)
                        first = ((job - 1) * NF + c) * TOPK
                        for t in range(max(first, 0), min(first + TOPK, NT)):
                            add_routed(t)
                    if job == 0:
                        for a in range(TB):
                            x_lo(3 * TB + a, (v + 1) % 2 + 2 * (a % 2))
                    add_shared(2 + job % 2)

            def mixer(k):
                nf, nm = phase_counts(k)
                wait_residual(dve, k)
                for piece in range(4):
                    raw = w_raw[:, piece % 2].rearrange("p (k a) n -> p k (a n)", k=2)
                    dve.wait_ge(m_wo_raw[piece], 16)
                    own.mark(dve.tensor_scalar(raw[:, 0], raw[:, 0], nw[:, 2 * piece:2 * piece + 1], None, ALU.mult))
                    own.join()
                    dve.tensor_scalar(raw[:, 1], raw[:, 1], nw[:, 2 * piece + 1:2 * piece + 2], None, ALU.mult)\
                        .then_inc(m_wo_n, 1)
                    dve.wait_ge(m_wo_hi, piece + 1)
                    lo_half(wo[:, 1, 2 * piece:2 * piece + 2], raw, wo[:, 0, 2 * piece:2 * piece + 2], m_wo_lo)

                def turn(i):
                    after, settle = loop_waits(dve, i)

                    def heads_of(ap):
                        return ap.rearrange("p (h d) -> p h d", d=HD)

                    def y_lo(n):
                        for half in range(2):
                            after(m_yhi, 2 * n + half + 1, 2 * TPB)
                            lo_half(yT[:, 1, 4 * half:4 * half + 4],
                                    bank[6 + half][:].rearrange("p (c t) -> p c t", c=4),
                                    yT[:, 0, 4 * half:4 * half + 4], m_ylo)

                    def residual(n):
                        xt = X[:, bass.ds(i * TPB + n, 1), :].rearrange("p o n -> p (o n)")
                        after(m_out, n + 1, TPB)
                        after(m_rs, n + 1, TPB)
                        dve.scalar_tensor_tensor(xt, bank[2][:], rs[:, n % 2:n % 2 + 1], xt,
                                                 ALU.mult, ALU.add).then_inc(m_res, 1)

                    for j in range(BPB):
                        def conv(c):
                            n = j * NCH + c
                            after(m_pre2, n + 1, BPB * NCH)
                            after(m_hin, n + 1, BPB * NCH)
                            for tap in range(TAPS - 1):
                                ins = dve.scalar_tensor_tensor(acc[:, c % 2], pre[:, c % 2, tap:tap + D],
                                                               cw[:, c, tap:tap + 1], acc[:, c % 2], ALU.mult, ALU.add)
                                if tap < TAPS - 2:
                                    own.step(ins)
                            ins.then_inc(m_conv, 1)

                        def softplus():
                            three = lambda t: t[:].rearrange("p (q h) -> p q h", h=HEADS)
                            after(m_dtp, j + 1, BPB)
                            own.step(dve.tensor_tensor(three(d_x), bank[2][:, 0:NQ].rearrange("p (q h) -> p q h", h=HEADS),
                                                       some(hp[:, 0:HEADS], TB), ALU.add))
                            own.step(dve.tensor_scalar(d_q[:], d_x[:], -1.0, None, ALU.mult))
                            dve.tensor_tensor(d_z[:], d_x[:], d_q[:], ALU.min).then_inc(m_dx, 1)

                        def log1p():
                            three = lambda t: t[:].rearrange("p (q h) -> p q h", h=HEADS)
                            after(m_de, j + 1, BPB)
                            own.step(dve.tensor_scalar(d_q[:], d_e[:], 2.0, None, ALU.add))
                            own.step(dve.reciprocal(d_p[:], d_q[:]))
                            own.step(dve.tensor_tensor(d_z[:], d_e[:], d_p[:], ALU.mult))
                            own.step(dve.tensor_tensor(d_q[:], d_z[:], d_z[:], ALU.mult))
                            own.step(dve.tensor_scalar(d_p[:], d_q[:], LOG1P[-1], None, ALU.mult))
                            for c in reversed(LOG1P[:-1]):
                                own.step(dve.scalar_tensor_tensor(d_p[:], d_p[:], c, d_q[:], ALU.add, ALU.mult))
                            own.step(dve.scalar_tensor_tensor(d_p[:], d_p[:], 1.0, d_z[:], ALU.add, ALU.mult))
                            own.step(dve.tensor_scalar(d_x[:], d_x[:], 0.0, None, ALU.max))
                            own.step(dve.scalar_tensor_tensor(dts[:], d_p[:], 2.0, d_x[:], ALU.mult, ALU.add))
                            own.step(dve.tensor_tensor(three(d_a), three(dts), some(negA[:], TB), ALU.mult))
                            own.step(dve.tensor_scalar(d_a[:], d_a[:], -1.0, DECAY_FLOOR, ALU.mult, ALU.max))
                            own.step(dve.tensor_copy(aparts[:, 0], d_a[:]))
                            own.step(dve.tensor_tensor(d_q[:], d_a[:], aparts[:, 0], ALU.subtract))
                            own.step(dve.tensor_copy(aparts[:, 1], d_q[:]))
                            own.step(dve.tensor_tensor(d_a[:], d_q[:], aparts[:, 1], ALU.subtract))
                            dve.tensor_copy(aparts[:, 2], d_a[:]).then_inc(m_ap, 1)

                        for c in range(NCH):
                            conv(c)
                            if j and c == 0:
                                y_lo(j * TB - 1)
                            if j and c == 3:
                                residual(j * TB - 1)
                            if c == NCH - 3:
                                softplus()
                        log1p()
                        after(m_cs, j + 1, BPB)
                        own.step(dve.tensor_scalar(ncs[:], bank[2][:, NQ:2 * NQ], -1.0, None, ALU.mult))
                        dve.tensor_tensor(d_p[:], bank[2][:, 2 * NQ:3 * NQ], ncs[:], ALU.add).then_inc(m_ncs, 1)

                        for q in range(TB):
                            n = j * TB + q
                            hq = slice(q * HEADS, (q + 1) * HEADS)
                            HB = HEADS // 2
                            nxt = i * TPB + (n + TB)
                            if j == BPB - 1:
                                nxt = dve.snap(nxt % NT)
                            x_next = X[:, bass.ds(nxt, 1), :].rearrange("p o n -> p (o n)")
                            ln_stats([x_next], [q], l_var)
                            for half in range(2):
                                hs = slice(half * DI // 2, (half + 1) * DI // 2)
                                after(m_xt, 2 * n + half + 1, 2 * TPB)
                                if half == 0:
                                    after(m_xw, n, TPB)
                                    after(m_E, n, TPB)
                                ins = dve.tensor_tensor(heads_of(xdt[:, hs]), heads_of(bank[4 + half][:]),
                                                        each(dts[:, q * HEADS + half * HB:q * HEADS + (half + 1) * HB], HD),
                                                        ALU.mult)
                                if half == 0:
                                    own.mark(ins)
                            ins.then_inc(m_xdt, 1)
                            if q >= 1:
                                y_lo(n - 1)
                            after(m_yd, n, TPB)
                            for half in range(2):
                                hs = slice(half * DI // 2, (half + 1) * DI // 2)
                                ins = dve.tensor_tensor(heads_of(xD[:, hs]), heads_of(bank[4 + half][:]),
                                                        each(hp[:, 2 * HEADS + half * HB:2 * HEADS + (half + 1) * HB], HD),
                                                        ALU.mult)
                                if half == 0:
                                    own.mark(ins)
                            ins.then_inc(m_xD, 1)
                            dve.wait_ge(l_rstd, i * TPB + (n + TB + 1))
                            dve.wait_ge(l_tp, i * TPB + (n + TB - 1))
                            ln_scale(xn_m[:, q % 2], x_next, q).then_inc(l_xn, 1)
                            after(m_Bt, n + 1, TPB)
                            for g in range(HG):
                                after(m_L, HG * n + g + 1, HG * TPB)
                                dve.tensor_tensor(L[:, g * GH:(g + 1) * GH], L[:, g * GH:(g + 1) * GH],
                                                  some(GB[:, 0:P], GH), ALU.mult).then_inc(m_M, 1)
                            if q >= 1:
                                residual(n - 1)
                            after(m_C, n + 1, TPB)
                            after(m_dec, j + 1, BPB)
                            after(m_F, 2 * (n - 1), 2 * TPB)
                            after(m_sq, n - 1, TPB)
                            for half in range(2):
                                hs = slice(half * DI // 2, (half + 1) * DI // 2)
                                ins = dve.tensor_tensor(heads_of(y[:, n % 2, hs]), heads_of(bank[6 + half][:]),
                                                        each(ecs[:, q * HEADS + half * HB:q * HEADS + (half + 1) * HB], HD),
                                                        ALU.mult)
                                if half == 0:
                                    own.mark(ins)
                            ins.then_inc(m_yc, 1)
                            dve.wait_ge(l_hi, i * TPB + (n + TB + 1))
                            lo_half(xb[:, 1, :, q * P:(q + 1) * P], bank[3][:].rearrange("p (c t) -> p c t", c=KD),
                                    xb[:, 0, :, q * P:(q + 1) * P], l_lo)
                            after(m_D, n + 1, TPB)
                            after(m_Sd, n + 1, TPB)
                            new = S[:, (n + 1) % 2]
                            own.mark(dve.tensor_tensor(new[:, 0:DI // 2], new[:, 0:DI // 2], bank[4][:], ALU.add))
                            dve.tensor_tensor(new[:, DI // 2:DI], new[:, DI // 2:DI], bank[5][:], ALU.add).then_inc(m_S, 1)
                            after(m_E, n + 1, TPB)
                            after(m_yd, n + 1, TPB)
                            own.mark(dve.tensor_tensor(y[:, n % 2, 0:DI // 2], y[:, n % 2, 0:DI // 2], bank[6][:],
                                                       ALU.add))
                            dve.tensor_tensor(y[:, n % 2, DI // 2:DI], y[:, n % 2, DI // 2:DI], bank[7][:], ALU.add)\
                                .then_inc(m_yi, 1)
                    y_lo(TPB - 1)
                    residual(TPB - 1)
                    settle((m_xw, TPB), (m_yd, TPB), (m_E, TPB), (m_F, 2 * TPB), (m_sq, TPB), (m_out, TPB),
                           (m_yg, TPB), (l_tp, TPB))

                for q in range(TB):
                    ln_stats([X[:, q, :]], [q], l_var)
                for q in range(TB + 1):
                    if q < TB:
                        dve.wait_ge(l_rstd, q + 1)
                        if q >= 2:
                            dve.wait_ge(l_tp, q - 1)
                        ln_scale(xn_m[:, q % 2], X[:, q, :], q).then_inc(l_xn, 1)
                    if q >= 1:
                        dve.wait_ge(l_hi, q)
                        lo_half(xb[:, 1, :, (q - 1) * P:q * P], bank[4 + (q - 1) % 2][:].rearrange("p (c t) -> p c t", c=KD),
                                xb[:, 0, :, (q - 1) * P:q * P], l_lo)
                dve.wait_ge(m_wdt_hi, 1)
                lo_half(wdt[:, 1], wdt_raw[:], wdt[:, 0], m_wdt_lo)
                own_steps = 2 * TB + NCH * (TAPS - 2) + 2 + 21 + 1 + TB * 5
                with dve.Fori(0, BATCH) as i:
                    own.enter(i, BPB * own_steps)
                    turn(i)
                own.leave(BATCH)

            dve.wait_ge(s_ready, READY)
            own.mark(dve.tensor_copy(tri_b[:], tri[:]))
            own.mark(dve.tensor_copy(ident_b[:], ident[:]))
            own.mark(dve.memset(ones_b[:], 1.0))
            own.mark(dve.tensor_tensor(stri_b[:], tri[:], ident[:], ALU.subtract))
            dve.tensor_scalar(mask_b[:], tri[:], 1.0, -MASKED, ALU.subtract, ALU.mult).then_inc(s_bf, 1)
            for k, what in enumerate(PLAN):
                (ffn if what == "ffn" else mixer)(k)

        @block.tensor
        def _(pe):
            pe.wait_ge(s_ready, READY)
            pe.wait_ge(s_bf, 1)
            pe.wait_ge(s_const, 64)

            def ffn(k):
                nf, nm = phase_counts(k)
                g0, j0 = nf * SETS, nf * JOBS
                wait_residual(pe, k)

                def transpose(bk, src, signal):
                    for c in range(KD):
                        ins = pe.transpose(bank[bk][:, c * P:(c + 1) * P], src[:, c * P:(c + 1) * P], ident[:])
                    ins.then_inc(signal, 1)

                def logits(t):
                    pe.wait_ge(n_cp, nf * NT + t + 1)
                    for c in range(KD):
                        ins = pe.matmul(bank[4][:, t * NE:(t + 1) * NE], tmpT[:, t % 2, c * P:(c + 1) * P], wr[:, c],
                                        start=(c == 0), stop=(c == KD - 1))
                    ins.then_inc(n_lg, 1)

                for t in range(NT):
                    pe.wait_ge(n_xn, nf * NT + t + 1)
                    if t >= 4:
                        pe.wait_ge(n_cp, nf * NT + t - 3)
                        pe.wait_ge(b_hi, nf * NT + min(t - 3, 2 * TB))
                    transpose(t % 4, xn[:, t], n_tp)
                    if t >= 1:
                        logits(t - 1)
                logits(NT - 1)

                def ranks():
                    pe.wait_ge(n_msk, nf + 1)
                    rank = bank[7][:, 0:NT * NE]
                    pe.matmul(rank, stri_b[:], r_sum[:].rearrange("p t e -> p (t e)"), start=True, stop=False)
                    for t in range(NT - 1):
                        pe.matmul(bank[7][:, (t + 1) * NE:NT * NE].rearrange("p (t e) -> p t e", e=NE), ones_b[:],
                                  some(r_sum[:, t], NT - 1 - t), start=False, stop=(t == NT - 2))
                    for t in range(NT):
                        ins = pe.matmul(bank[7][:, NT * NE:NT * NE + NE], ones_b[:], r_sum[:, t],
                                        start=(t == 0), stop=(t == NT - 1))
                    ins.then_inc(n_rank, 1)

                def gate_up(job, c, par, wpar, x_of, width):
                    f0, fw = FCH[c]
                    v = job * NF + c
                    pe.wait_ge(f_h, v - 1 + H0)
                    for w, dst in ((g_hl, bank[par]), (u_hl, bank[2 + par])):
                        n = 0
                        for kc in range(KD):
                            for hw, hx in HALVES:
                                ins = pe.matmul(dst[0:fw, 0:width], w[:, wpar, hw, kc, f0:f0 + fw], x_of(hx, kc),
                                                start=(n == 0), stop=(n == 3 * KD - 1))
                                n += 1
                    ins.then_inc(f_gu, 1)

                def down(job, c, wpar, tiles, free, signal):
                    fw = FCH[c][1]
                    pe.wait_ge(f_hlo, job * NF + (c + 1) + LO0)
                    for a in range(tiles):
                        if c == 0:
                            free(a)
                        for m, (hh, hw) in enumerate(HALVES):
                            ins = pe.matmul(bank[4 + a][:], hT[0:fw, hh, c, a * P:(a + 1) * P], d_hl[0:fw, wpar, hw, c],
                                            start=(c == 0 and m == 0), stop=(c == NF - 1 and m == 2))
                        if c == NF - 1:
                            ins.then_inc(signal, 1)

                n_acc = nf * 2 * SJ * TB
                pe.wait_ge(n_sh, nf + 1)
                for job in range(SJ):
                    b, wpar = job % 2, job // 2
                    x_of = lambda h, kc: xs[b][:, h, kc]
                    pe.wait_ge(b_lo0, nf * 2 * TB + (b + 1) * TB)
                    pe.wait_ge(f_wlo, (g0 + wpar) * 3 + 2)
                    for c in range(NF):
                        gate_up(j0 + job, c, (job * NF + c) % 2, wpar, x_of, D)
                    if job == 0:
                        ranks()
                    if job == SJ - 1:
                        par = (SJ * NF) % 2
                        pe.wait_ge(t_xg[0], (nf * EVEN + 1) * 16)
                        pe.wait_ge(f_h, (j0 + job) * NF + 2 + H0)
                        transpose(par, xg[:, 0, 0], t_tp)
                        transpose(2 + par, xg[:, 0, 1], t_tp)

                    def free(a):
                        if job == 0 and a == 3:
                            pe.wait_ge(n_slot, 2 * nf + 2)
                        if job:
                            pe.wait_ge(f_acc, n_acc + (job - 1) * TB + a + 1)
                    pe.wait_ge(f_wlo, (g0 + wpar) * 3 + 3)
                    for c in range(NF):
                        down(j0 + job, c, wpar, TB, free, f_dn)

                def tile(j, q, last):
                    job = j + (j0 + SJ)
                    x_of = lambda h, kc: xgT[:, q, h, kc]
                    pe.wait_ge(t_lo, (j + (nf * NTL + 1)) * 2)
                    pe.wait_ge(f_wlo, j * 3 + ((g0 + NS) * 3 + 2))
                    gate_up(job, 0, (q * NF) % 2, q, x_of, TS)
                    if not last:
                        if q == 0:
                            pe.wait_ge(t_xg[1], (i + (nf * ODD + 1)) * 16)
                        else:
                            pe.wait_ge(t_xg[0], (i + (nf * EVEN + 2)) * 16)
                        pe.wait_ge(t_lo, (j + (nf * NTL + 1)) * 2)
                        if q == 0:
                            pe.wait_ge(f_acc, n_acc + SJ * TB)
                        for a in range(2):
                            transpose(6 + a, xg[:, (q + 1) % 2, a], t_tp)
                    for c in (1, 2):
                        gate_up(job, c, (q * NF + c) % 2, q, x_of, TS)
                    if last:
                        pe.wait_ge(f_h, job * NF + 2 + H0)
                        late = ((NTL * NF) % 2, 2 + (NTL * NF) % 2, 6, 7)
                        for t, bk in zip(range(2 * TB, 3 * TB), late):
                            transpose(bk, xn[:, t], b_tp)

                    def free(a):
                        pe.wait_ge(t_y, (j + nf * NTL - 1) * 2 + (a + 1 + Y0))
                    pe.wait_ge(f_wlo, j * 3 + ((g0 + NS) * 3 + 3))
                    for c in range(NF):
                        down(job, c, q, 2, free, t_dn)

                with pe.Fori(0, NTL // 2) as i:
                    for q in range(2):
                        tile(i * 2 + q, q, False)
                tile(NTL - 1, 0, True)

                for job in range(SJ):
                    b, wpar = job % 2, (1, 0)[job // 2]
                    v = (SJ + NTL + job) * NF
                    x_of = lambda h, kc: xs[(b + 1) % 2][:, h, kc]
                    pe.wait_ge(b_lo1, nf * 2 * TB + (b + 1) * TB)
                    pe.wait_ge(f_wlo, (g0 + NS + NTL + job // 2) * 3 + 2)
                    for c in range(NF):
                        gate_up(j0 + SJ + NTL + job, c, (v + c) % 2, wpar, x_of, D)
                    if job == 0:
                        pe.wait_ge(f_h, (j0 + SJ + NTL) * NF + 2 + H0)
                        for a in range(2):
                            transpose((v + 1) % 2 + 2 * a, xn[:, 3 * TB + a], b_tp)

                    def free(a):
                        if job:
                            pe.wait_ge(f_acc, n_acc + (SJ + job - 1) * TB + a + 1)
                        elif a < 2:
                            pe.wait_ge(t_y, (nf + 1) * NTL * 2 + Y0)
                        else:
                            pe.wait_ge(b_lo1, nf * 2 * TB + TB)
                    pe.wait_ge(f_wlo, (g0 + NS + NTL + job // 2) * 3 + 3)
                    for c in range(NF):
                        if job == 0 and c == 2:
                            for a in range(2, 4):
                                pe.wait_ge(b_lo1, nf * 2 * TB + TB + a - 1)
                                transpose((v + 1) % 2 + 2 * (a % 2), xn[:, 3 * TB + a], b_tp)
                        down(j0 + SJ + NTL + job, c, wpar, TB, free, f_dn)

            def mixer(k):
                wait_residual(pe, k)
                pe.wait_ge(m_wo_lo, 4)

                def turn(i):
                    after, settle = loop_waits(pe, i)

                    def y_features(n):
                        after(m_yg, n + 1, TPB)
                        for half in range(2):
                            for c in range(4):
                                ins = pe.transpose(bank[6 + half][:, c * P:(c + 1) * P],
                                                   y[:, n % 2, (4 * half + c) * P:(4 * half + c + 1) * P], ident[:])
                            ins.then_inc(m_F, 1)

                    def project(n):
                        if n % TB == 0:
                            after(m_dec, n // TB + 1, BPB)
                        after(m_res, n, TPB)
                        m = 0
                        for half in range(2):
                            after(m_ylo, 2 * n + half + 1, 2 * TPB)
                            for c in range(4 * half, 4 * half + 4):
                                for hy, hw in HALVES:
                                    ins = pe.matmul(bank[2][:], yT[:, hy, c], wo[:, hw, c],
                                                    start=(m == 0), stop=(m == 3 * KI - 1))
                                    m += 1
                        ins.then_inc(m_out, 1)

                    for j in range(BPB):
                        pe.wait_ge(l_lo, i * TPB + (j + 1) * TB)
                        for u in range(NWU):
                            w = j * NWU + u
                            after(m_wlo, w + 1, BPB * NWU)
                            wt = w_hl[:, w % 2]
                            if u < 5:
                                for c in (2 * u, 2 * u + 1):
                                    n = j * NCH + c
                                    if c < 2:
                                        after(m_L, HG * j * TB, HG * TPB)
                                        after(m_pre2, j * NCH, BPB * NCH)
                                    else:
                                        after(m_pre2, n - 1, BPB * NCH)
                                    m = 0
                                    for kc in range(KD):
                                        for hw, hx in HALVES:
                                            ins = pe.matmul(bank[c % 2][:], wt[:, hw, kc, (c % 2) * P:(c % 2 + 1) * P],
                                                            xb[:, hx, kc], start=(m == 0), stop=(m == 3 * KD - 1))
                                            m += 1
                                    ins.then_inc(m_cp, 1)
                                if u == 0 and j:
                                    y_features(j * TB - 1)
                                if u == 1 and j:
                                    project(j * TB - 1)
                                if u == 1:
                                    pe.wait_ge(m_wdt_lo, 1)
                                    for m, (kc, (hw, hx)) in enumerate([(c, h) for c in range(KD) for h in HALVES]):
                                        ins = pe.matmul(bank[3][0:HEADS, :], wdt[:, hw, kc], xb[:, hx, kc],
                                                        start=(m == 0), stop=(m == 3 * KD - 1))
                                    ins.then_inc(m_dtT, 1)
                                if u == 2:
                                    after(m_dtc, j + 1, BPB)
                                    after(m_res, j * TB, TPB)
                                    for q in range(TB):
                                        ins = pe.matmul(bank[2][:, q * HEADS:(q + 1) * HEADS], dtT[:, q * P:(q + 1) * P],
                                                        ident[0:HEADS, 0:HEADS], start=True, stop=True)
                                    ins.then_inc(m_dtp, 1)
                            else:
                                for half in range(2):
                                    n = j * 8 + (u - 5) * 2 + half
                                    if u == 5:
                                        after(m_ylo, 2 * j * TB, 2 * TPB)
                                        after(m_yi, j * TB, TPB)
                                    else:
                                        after(m_z, n - 1, 8 * BPB)
                                    for q in (2 * half, 2 * half + 1):
                                        m = 0
                                        for kc in range(KD):
                                            for hx, hw in HALVES:
                                                ins = pe.matmul(bank[6 + half][:, (q % 2) * WU:(q % 2 + 1) * WU],
                                                                xb[:, hx, kc, q * P:(q + 1) * P], wt[:, hw, kc],
                                                                start=(m == 0), stop=(m == 3 * KD - 1))
                                                m += 1
                                    ins.then_inc(m_zp, 1)
                        after(m_ap, j + 1, BPB)
                        for dst, mat in ((1, tri_b), (2, ones_b)):
                            for p in range(3):
                                ins = pe.matmul(bank[2][:, dst * NQ:(dst + 1) * NQ], mat[:], aparts[:, p],
                                                start=(p == 0), stop=(p == 2))
                        ins.then_inc(m_cs, 1)

                        def decays(n, q, g):
                            if q == 0 and g < 2:
                                after(m_pre2, (j + 1) * NCH, BPB * NCH)
                            else:
                                after(m_L, HG * n + g - 1, HG * TPB)
                            dst = bank[g % 2]
                            pe.matmul(dst[:].rearrange("p (h t) -> p h t", h=GH), ident_b[:], some(mask_b[:], GH),
                                      start=True, stop=False)
                            for h in range(GH):
                                col = q * HEADS + g * GH + h
                                for p in range(3):
                                    ins = pe.matmul(dst[:, h * P:(h + 1) * P],
                                                    aparts[:, p, col:col + 1].broadcast_to([P, P]), tri_b[:],
                                                    start=False, stop=(h == GH - 1 and p == 2))
                            ins.then_inc(m_B, 1)

                        for q in range(TB):
                            n = j * TB + q
                            tt = slice(q * P, (q + 1) * P)
                            decays(n, q, 0)
                            decays(n, q, 1)
                            if q == 0:
                                after(m_xc, (j + 1) * NCH, BPB * NCH)
                            after(m_Bt, n, TPB)
                            after(m_dtc, j + 1, BPB)
                            pe.wait_ge(l_lo, i * TPB + (n + TB))
                            pe.matmul(bank[3][:, 0:P], xc[:, 0, tt], xc[:, 1, tt], start=True, stop=True)
                            pe.transpose(bank[3][:, P:2 * P], xc[:, 0, tt], ident[:]).then_inc(m_G, 1)
                            after(m_S, n, TPB)
                            for half in range(2):
                                for c in range(4):
                                    ins = pe.transpose(bank[4 + half][:, c * P:(c + 1) * P],
                                                       xc[:, 2 + 4 * half + c, tt], ident[:])
                                ins.then_inc(m_xt, 1)
                            decays(n, q, 2)
                            if q >= 1:
                                y_features(n - 1)
                            decays(n, q, 3)
                            if q >= 1:
                                project(n - 1)
                            pe.wait_ge(m_zero, i + 1)
                            after(m_yi, n, TPB)
                            after(m_ylo, 2 * n, 2 * TPB)
                            if q == 0:
                                after(m_z, 8 * (j + 1), 8 * BPB)
                            for half in range(2):
                                ins = pe.matmul(bank[6 + half][:], xc[:, 1, tt], S[:, n % 2, half * 512:(half + 1) * 512],
                                                start=True, stop=True)
                            ins.then_inc(m_C, 1)
                            pe.wait_ge(l_xn, i * TPB + (n + TB + 1))
                            after(m_Bt, n + 1, TPB)
                            for c in range(KD):
                                ins = pe.transpose(bank[3][:, c * P:(c + 1) * P], xn_m[:, q % 2, c * P:(c + 1) * P],
                                                   ident[:])
                            ins.then_inc(l_tp, 1)
                            after(m_xw, n + 1, TPB)
                            after(m_xD, n + 1, TPB)
                            for half in range(2):
                                ins = pe.matmul(bank[4 + half][:], Bt, xw[:, half * 512:(half + 1) * 512],
                                                start=True, stop=True)
                            ins.then_inc(m_D, 1)
                            after(m_yc, n + 1, TPB)
                            for g in range(HG):
                                after(m_M, HG * n + g + 1, HG * TPB)
                                for h in range(g * GH, (g + 1) * GH):
                                    ins = pe.matmul(bank[6 + h // 8][:, (h % 8) * HD:(h % 8 + 1) * HD], L[:, h],
                                                    xdt[:, h * HD:(h + 1) * HD], start=True, stop=True)
                            ins.then_inc(m_E, 1)
                    y_features(TPB - 1)
                    project(TPB - 1)
                    settle((m_S, TPB), (m_L, HG * TPB), (m_pre2, BPB * NCH), (m_res, TPB), (m_ylo, 2 * TPB),
                           (m_yi, TPB), (m_Bt, TPB), (m_z, 8 * BPB), (m_dec, BPB), (l_lo, TPB))

                for q in range(TB):
                    pe.wait_ge(l_xn, q + 1)
                    if q >= 2:
                        pe.wait_ge(l_lo, q - 1)
                    for c in range(KD):
                        ins = pe.transpose(bank[4 + q % 2][:, c * P:(c + 1) * P], xn_m[:, q % 2, c * P:(c + 1) * P],
                                           ident[:])
                    ins.then_inc(l_tp, 1)
                with pe.Fori(0, BATCH) as i:
                    turn(i)

            for k, what in enumerate(PLAN):
                (ffn if what == "ffn" else mixer)(k)


def arrange(inputs):
    import numpy as np
    a = {k: np.asarray(v) for k, v in inputs.items()}

    def by_rows(w, rows=P):
        k = w.shape[-2] // rows
        return np.moveaxis(w.reshape(*w.shape[:-2], k, rows, w.shape[-1]), -3, -2)

    def experts(routed, shared):
        half = shared.shape[1] // NS
        return np.concatenate([routed, shared.reshape(D, NS, half).transpose(1, 0, 2)])

    x = a["L0_attn_u"].reshape(NT, P, D).transpose(1, 0, 2)
    w_in = a["L0_attn_W_in"].T
    units = np.concatenate([w_in[:, 2 * DI:2 * DI + 2 * P], w_in[:, DI:2 * DI], w_in[:, :DI]], axis=1)
    units = by_rows(units.reshape(D, NWU, WU).transpose(1, 0, 2))
    taps = np.concatenate([a["L0_attn_conv_w"].reshape(-1, TAPS), a["L0_attn_conv_b"][:, None]], axis=1)
    taps = np.concatenate([taps[DI:], taps[:DI]]).reshape(NCH, P, TAPS + 1).transpose(1, 0, 2)
    heads = np.concatenate([a["L0_attn_dt_bias"], a["L0_attn_A_log"], a["L0_attn_D"]])
    w_out = by_rows(a["L0_attn_W_out"].T)
    return {
        "x": x,
        "w_router": by_rows(a["L0_ffn_W_router"]),
        "w_gate": by_rows(experts(a["L0_ffn_We_gate"], a["L0_ffn_Ws_gate"])),
        "w_up": by_rows(experts(a["L0_ffn_We_up"], a["L0_ffn_Ws_up"])),
        "w_down": np.concatenate([a["L0_ffn_We_down"], a["L0_ffn_Ws_down"].reshape(NS, FE, D)]),
        "w_in": units,
        "w_dt": by_rows(w_in[:, 2 * DI + 2 * P:]),
        "conv": taps,
        "heads": np.broadcast_to(heads, (P, heads.size)),
        "norm_w": a["L0_attn_norm_w"].reshape(KI, P).T,
        "w_out": w_out.reshape(P, 4, 2, D).transpose(1, 0, 2, 3),
    }


def kernel(**inputs):
    import numpy as np
    import concourse.bacc as bacc
    from concourse.bass_utils import run_bass_kernel_spmd
    nc = bacc.Bacc("TRN2", target_bir_lowering=False, num_devices=1)
    arrays, args = {}, []
    for name, a in arrange(inputs).items():
        a = np.ascontiguousarray(a)
        arrays[f"in_{name}"] = a
        args.append(nc.dram_tensor(f"in_{name}", a.shape, mybir.dt.from_np(a.dtype), kind="ExternalInput").ap())
    out = nc.dram_tensor("out", (P, NT, D), mybir.dt.float32, kind="ExternalOutput").ap()
    program(nc, *args, out)
    got = run_bass_kernel_spmd(nc, [arrays], core_ids=[0]).results[0]["out"]
    return got.transpose(1, 0, 2).reshape(BATCH, TOK // BATCH, D)
```

```python
import concourse.bass as bass
from concourse import mybir


P = 128
D = 512
KD = D // P
TOK = 2048
NT = TOK // P
NB = 4
TB = NT // NB
BATCH = 2
BPB = NB // BATCH
TPB = NT // BATCH
NE = 8
FE = 352
NS = 2
NX = NE + NS
TOPK = 2
TS = 2 * P
NTL = (TOPK * TOK + NE * (TS - 1)) // TS
SJ = NS * NB // 2
JOBS = SJ + NTL + SJ
SETS = NS + NTL + NS
FCH = [(0, 128), (128, 128), (256, 96)]
NF = len(FCH)
HEADS = 16
HD = 64
DI = HEADS * HD
KI = DI // P
NCH = 10
TAPS = 4
WU = 256
NWU = 9
HG = 4
GH = HEADS // HG
EPS = 1e-5
ROUTE = 0.5
DECAY_FLOOR = -120.0
MASKED = -30000.0
HALVES = [(0, 0), (0, 1), (1, 0)]
LOG1P = [1.0 / (2 * k + 1) for k in range(1, 9)]
PLAN = ("ffn", "mixer", "ffn")


class Chain:

    def __init__(self, eng, sem):
        self.eng, self.sem, self.count, self.turn = eng, sem, 0, 0

    def mark(self, ins):
        ins.then_inc(self.sem, 1)
        self.count += 1

    def join(self):
        self.eng.wait_ge(self.sem, self.turn + self.count)

    def step(self, ins):
        self.mark(ins)
        self.join()

    def enter(self, i, per_turn):
        self.turn, self.start, self.per_turn = i * per_turn, self.count, per_turn

    def leave(self, turns):
        assert self.count - self.start == self.per_turn, self.count - self.start
        self.count += (turns - 1) * self.per_turn
        self.turn = 0


def program(nc, x, w_router, w_gate, w_up, w_down, w_in, w_dt, conv, heads, norm_w, w_out, out):
    routed_x = nc.dram_tensor("routed_x", (NTL * TS, D), mybir.dt.float32, kind="Internal").ap()
    routed_y = nc.dram_tensor("routed_y", (NTL * TS, D), mybir.dt.float32, kind="Internal").ap()
    F, R, B16, U32 = mybir.dt.float32, mybir.dt.float32r, mybir.dt.bfloat16, mybir.dt.uint32
    ACT, ALU, AX = mybir.ActivationFunctionType, mybir.AluOpType, mybir.AxisListType

    def sb(name, shape, dt=F):
        return nc.alloc_sbuf_tensor(name, shape, dt)

    def sem(name):
        return nc.alloc_semaphore(name)

    def each(ap, n):
        return ap.rearrange("p (a o) -> p a o", o=1).broadcast_to([P, ap.shape[1], n])

    def some(ap, n):
        return ap.rearrange("p (o a) -> p o a", o=1).broadcast_to([P, n, ap.shape[1]])

    X = sb("X", [P, NT, D])
    ident = sb("ident", [P, P])
    iota = sb("iota", [P, 24])
    stats = sb("stats", [P, NT, 6])
    mv = sb("mv", [P, NT, 2])
    rstd = sb("rstd", [P, NT])
    mhalf = sb("mhalf", [P, NT])
    carrier = sb("carrier", [P, 1])
    starts = sb("starts", [P, 6])
    zero = sb("zero", [P, 1])
    eps = sb("eps", [P, 1])
    by_di = sb("by_di", [P, 1])
    wr = sb("wr", [P, KD, NE])
    r_1 = sb("r_1", [P, NT])
    r_2 = sb("r_2", [P, NT])
    r_val = sb("r_val", [P, TOPK, NT])
    r_exp = sb("r_exp", [P, TOPK, NT])
    r_sum = sb("r_sum", [P, NT, NE], B16)
    r_cnt = sb("r_cnt", [P, NE])
    r_end = sb("r_end", [P, 2, 4 + NE])
    r_til = sb("r_til", [P, 4 + NE])
    r_pos = sb("r_pos", [P, TOPK * NT])
    slots = sb("slots", [P, TOPK * NT], U32)
    r_te = sb("r_te", [P, NTL])
    tile_e = sb("tile_e", [P, NTL], U32)
    stri_b = sb("stri_b", [P, P], B16)
    cw = sb("cw", [P, NCH, TAPS + 1])
    hp = sb("hp", [P, 3 * HEADS])
    nw = sb("nw", [P, KI])
    negA = sb("negA", [P, HEADS])
    tri = sb("tri", [P, P])
    tri_b = sb("tri_b", [P, P], B16)
    ones_b = sb("ones_b", [P, P], B16)
    ident_b = sb("ident_b", [P, P], B16)
    mask_b = sb("mask_b", [P, P], B16)

    arena = nc.sbuf_base

    def placer(start):
        at = [(start + 63) // 64 * 64]

        def place(name, shape, dt=F):
            size = {F: 4, R: 4, U32: 4, B16: 2}[dt]
            for n in shape[1:]:
                size *= n
            t = nc.alloc_sbuf_tensor_at(name, shape, dt, offset=at[0])
            at[0] += (size + 63) // 64 * 64
            return t
        return place

    ff = placer(arena)
    g_raw = ff("g_raw", [P, KD, FE])
    u_raw = ff("u_raw", [P, KD, FE])
    d_raw = ff("d_raw", [P, NF, D])
    g_hl = ff("g_hl", [P, 2, 2, KD, FE], R)
    u_hl = ff("u_hl", [P, 2, 2, KD, FE], R)
    d_hl = ff("d_hl", [P, 2, 2, NF, D], R)
    gate = ff("gate", [P, 2, D])
    hT = ff("hT", [P, 2, NF, D], R)
    xn = ff("xn", [P, NT, D])
    xs0 = ff("xs0", [P, 2, KD, D], R)
    xs1 = ff("xs1", [P, 2, KD, D], R)
    xs = [xs0, xs1]
    xn_at, xs0_at, xs1_at = (t[:].tensor.manual_sbuf_range[0] for t in (xn, xs0, xs1))
    r_a = ff("r_a", [P, NT, NE])
    r_b = ff("r_b", [P, NT, NE])
    r_top = ff("r_top", [P, NT, NE])
    r_idx = ff("r_idx", [P, NT, NE], U32)
    r_msk = ff("r_msk", [P, TOPK * NT, NE])
    r_cmp = ff("r_cmp", [P, NTL, NE])
    zero_row = ff("zero_row", [P, D])
    hT_at = hT[:].tensor.manual_sbuf_range[0]
    tmpT = [nc.alloc_sbuf_tensor_at(f"tmpT{h}", [P, D], F, offset=hT_at + (h * NF + NF - 1) * D * 4) for h in range(2)]
    xg = nc.alloc_sbuf_tensor_at("xg", [P, 2, 2, D], F, offset=xn_at)
    yg = nc.alloc_sbuf_tensor_at("yg", [P, 2, TOPK, D], F, offset=xn_at + 8 * D * 2)
    ys = nc.alloc_sbuf_tensor_at("ys", [P, 2, 2, D], F, offset=xs0_at)
    xgT = nc.alloc_sbuf_tensor_at("xgT", [P, 2, 2, KD, TS], R, offset=xs1_at)
    mx = placer(arena)
    NQ = TB * HEADS
    zs = mx("zs", [P, TB, DI])
    wo = mx("wo", [P, 2, KI, D], R)
    xc = mx("xc", [P, NCH, D])
    y = mx("y", [P, 2, DI])
    L = mx("L", [P, HEADS, P])
    GB = mx("GB", [P, 2 * P])
    Bt = GB[:, P:2 * P]
    xdt = mx("xdt", [P, DI])
    xw = mx("xw", [P, DI])
    xD = mx("xD", [P, DI])
    dtT = xD[0:HEADS, 0:D]
    ysq = mx("ysq", [P, DI], B16)
    d_x = mx("d_x", [P, NQ])
    d_e = mx("d_e", [P, NQ])
    d_z = mx("d_z", [P, NQ])
    d_q = mx("d_q", [P, NQ])
    d_p = mx("d_p", [P, NQ])
    dts = mx("dts", [P, NQ])
    d_a = mx("d_a", [P, NQ])
    ncs = mx("ncs", [P, NQ])
    w_raw = mx("w_raw", [P, 2, KD, WU])
    S = mx("S", [P, 2, DI])
    acc = mx("acc", [P, 2, D])
    xn_m = acc
    yT = mx("yT", [P, 2, KI, P], R)
    wdt_raw = mx("wdt_raw", [P, KD, HEADS])
    wdt = mx("wdt", [P, 2, KD, HEADS], R)
    halo = mx("halo", [P, NCH, TAPS - 1])
    ssq = mx("ssq", [P, 2])
    rs = mx("rs", [P, 2])
    aparts = mx("aparts", [P, 3, NQ], B16)
    ecs = mx("ecs", [P, NQ])
    dec = mx("dec", [P, NQ])
    wd = mx("wd", [P, NQ])
    xb = xs0
    mx_x = placer(xs1_at)
    w_hl = mx_x("w_hl", [P, 2, 2, KD, WU], R)
    pre = mx_x("pre", [P, 2, TAPS - 1 + D])
    place_of = lambda t: t[:].tensor.manual_sbuf_range
    assert place_of(zs)[1] <= place_of(d_raw)[1] and place_of(wo)[1] <= place_of(u_hl)[1]
    assert place_of(w_raw) == place_of(xg) and place_of(acc)[0] >= place_of(yg)[1]
    assert place_of(wdt_raw)[0] >= xn_at + 3 * TB * D * 4 and place_of(wd)[1] <= xs0_at
    assert place_of(g_raw)[1] <= place_of(zs)[0] + 2 * DI * 4 and place_of(u_raw)[1] <= place_of(zs)[0] + 3 * DI * 4
    assert place_of(w_hl) == place_of(xs1)

    bank = [nc.alloc_psum_tensor(f"bank{i}", [P, 512], F) for i in range(8)]

    s_x = [sem(f"s_x{b}") for b in range(NB)]
    s_const = sem("s_const")
    c_pool = sem("c_pool")
    c_dve = sem("c_dve")
    c_act = sem("c_act")
    s_ready = sem("s_ready")
    READY = 6
    s_bf = sem("s_bf")
    s_out = sem("s_out")
    l_var = sem("l_var")
    l_rstd = sem("l_rstd")
    l_xn = sem("l_xn")
    l_tp = sem("l_tp")
    l_hi = sem("l_hi")
    l_lo = sem("l_lo")
    n_var = sem("n_var")
    n_rstd = sem("n_rstd")
    n_xn = sem("n_xn")
    n_tp = sem("n_tp")
    n_cp = sem("n_cp")
    n_lg = sem("n_lg")
    n_sh = sem("n_sh")
    n_ex = sem("n_ex")
    n_msk = sem("n_msk")
    n_rank = sem("n_rank")
    n_rcp = sem("n_rcp")
    n_slot = sem("n_slot")
    d_zero = sem("d_zero")
    d_sc = sem("d_sc")
    b_tp = sem("b_tp")
    b_hi = sem("b_hi")
    b_lo0 = sem("b_lo0")
    b_lo1 = sem("b_lo1")
    f_graw, f_uraw, f_draw = sem("f_graw"), sem("f_uraw"), sem("f_draw")
    f_whi = sem("f_whi")
    f_wlo = sem("f_wlo")
    f_gu = sem("f_gu")
    f_silu = sem("f_silu")
    f_h = sem("f_h")
    f_hhi = sem("f_hhi")
    f_hlo = sem("f_hlo")
    f_dn = sem("f_dn")
    f_acc = sem("f_acc")
    t_xg = [sem(f"t_xg{q}") for q in range(2)]
    t_tp = sem("t_tp")
    t_hi = sem("t_hi")
    t_lo = sem("t_lo")
    t_dn = sem("t_dn")
    t_y = sem("t_y")
    t_st = [sem(f"t_st{q}") for q in range(2)]
    g_y = [sem(f"g_y{q}") for q in range(2)]
    g_add = sem("g_add")
    m_wo_raw = sem("m_wo_raw")
    m_wdt = sem("m_wdt")
    m_wdt_hi = sem("m_wdt_hi")
    m_wdt_lo = sem("m_wdt_lo")
    m_wo_n = sem("m_wo_n")
    m_wo_hi = sem("m_wo_hi")
    m_wo_lo0 = sem("m_wo_lo0")
    m_wo_lo1 = sem("m_wo_lo1")
    m_raw = [sem(f"m_raw{q}") for q in range(2)]
    m_whi = sem("m_whi")
    m_wlo = sem("m_wlo")
    m_cp = sem("m_cp")
    m_pre = sem("m_pre")
    m_conv = sem("m_conv")
    m_xc = sem("m_xc")
    m_dtT = sem("m_dtT")
    m_dtc = sem("m_dtc")
    m_dtp = sem("m_dtp")
    m_dx = sem("m_dx")
    m_de = sem("m_de")
    m_ap = sem("m_ap")
    m_cs = sem("m_cs")
    m_ncs = sem("m_ncs")
    m_dec = sem("m_dec")
    m_zp = sem("m_zp")
    m_z = sem("m_z")
    m_B = sem("m_B")
    m_L = sem("m_L")
    m_G = sem("m_G")
    m_xt = sem("m_xt")
    m_Bt = sem("m_Bt")
    m_xdt = sem("m_xdt")
    m_xD = sem("m_xD")
    m_xw = sem("m_xw")
    m_C = sem("m_C")
    m_yc = sem("m_yc")
    m_yd = sem("m_yd")
    m_M = sem("m_M")
    m_D = sem("m_D")
    m_Sd = sem("m_Sd")
    m_S = sem("m_S")
    m_E = sem("m_E")
    m_yi = sem("m_yi")
    m_yg = sem("m_yg")
    m_sq = sem("m_sq")
    m_rs = sem("m_rs")
    m_F = sem("m_F")
    m_yhi = sem("m_yhi")
    m_ylo = sem("m_ylo")
    m_out = sem("m_out")
    m_res = sem("m_res")
    m_zero = sem("m_zero")

    H0, LO0, DN0, Y0, ST0 = 2, 2, 2, 2, 1
    EVEN, ODD = (NTL + 1) // 2, NTL // 2

    LATE_BANKS = ((NTL * NF) % 2, 2 + (NTL * NF) % 2, 6, 7)
    SECOND = (0, 1, 1, 0)
    PAIRS = [range(t, t + 2) for t in range(TB, NT, 2)]

    def phase_counts(k):
        return PLAN[:k].count("ffn"), PLAN[:k].count("mixer")

    def wait_residual(eng, k):
        nf, nm = phase_counts(k)
        if k and PLAN[k - 1] == "ffn":
            eng.wait_ge(f_acc, nf * 2 * SJ * TB)
            eng.wait_ge(g_add, nf * TOPK * NT)
        elif k:
            eng.wait_ge(m_res, nm * NT)

    def loop_waits(eng, i):
        def after(s, n, each_turn, unit=1):
            if n <= 0:
                return
            eng.wait_ge(s, (i * each_turn + n) * unit)

        def settle(*sems):
            for s, each_turn in sems:
                eng.wait_ge(s, i * each_turn + each_turn)
        return after, settle

    block = nc.Block()
    with block:

        @block.sync
        def _(sp):
            def load_x(b):
                sp.dma_start(X[:, b * TB:(b + 1) * TB, :], x[:, b * TB:(b + 1) * TB, :]).then_inc(s_x[b], 16)

            load_x(0)
            for dst, src in ((wr, w_router), (cw, conv), (hp, heads), (nw, norm_w)):
                sp.dma_start(dst[:], src).then_inc(s_const, 16)

            def ffn(k):
                nf, nm = phase_counts(k)
                g0 = nf * SETS

                def load_piece(piece, e):
                    ds = bass.ds(e, 1)
                    if piece == 0:
                        sp.dma_start(g_raw[:], w_gate[ds].rearrange("o p c n -> p (o c) n")).then_inc(f_graw, 16)
                    elif piece == 1:
                        sp.dma_start(u_raw[:], w_up[ds].rearrange("o p c n -> p (o c) n")).then_inc(f_uraw, 16)
                    else:
                        sp.dma_start(d_raw[:, 0:2, :], w_down[ds, 0:2 * P, :].rearrange("o (c p) n -> p (o c) n", p=P))\
                            .then_inc(f_draw, 16)
                        sp.dma_start(d_raw[0:FE - 2 * P, 2, :], w_down[ds, 2 * P:FE, :].rearrange("o p n -> p (o n)"))\
                            .then_inc(f_draw, 16)

                def load(e, g):
                    for piece in range(3):
                        sp.wait_ge(f_wlo, g * 3 - 2 + piece)
                        load_piece(piece, e)

                def rows(j, q):
                    sp.dma_start(xg[:, q], routed_x[bass.ds(j * TS, TS), :].rearrange("(a p) n -> p a n", p=P))\
                        .then_inc(t_xg[q], 16)

                for piece in range(3):
                    if k and piece < 2:
                        sp.wait_ge(m_yg, nm * NT - 2 + piece)
                    elif k:
                        wait_residual(sp, k)
                    load_piece(piece, NE)
                    if k == 0 and piece == 1:
                        load_x(1)
                if k == 0:
                    load_x(2)
                    load_x(3)
                load(NE + 1, g0 + 1)
                if nf == 0:
                    sp.wait_ge(s_ready, READY)
                    sp.dma_start(routed_x.rearrange("(a p) n -> p a n", p=P), some(zero_row[:], NTL * TS // P))\
                        .then_inc(d_zero, 16)
                sp.wait_ge(n_slot, 2 * (nf + 1))
                load(sp.value_load(tile_e[0:1, 0:1], min_val=0, max_val=NE - 1), g0 + NS)
                sp.wait_ge(d_sc, (nf + 1) * TOPK * NT * 16)
                rows(0, 0)
                rows(1, 1)
                load(sp.value_load(tile_e[0:1, 1:2], min_val=0, max_val=NE - 1), g0 + NS + 1)
                with sp.Fori(1, NTL // 2) as i:
                    for q in range(2):
                        j = i * 2 + q
                        sp.wait_ge(t_tp, (i * 2 + (nf * NTL + q - 1)) * 2)
                        rows(j, q)
                        load(sp.value_load(tile_e[0:1, bass.ds(j, 1)], min_val=0, max_val=NE - 1), i * 2 + (g0 + NS + q))
                sp.wait_ge(t_tp, (nf * NTL + NTL - 2) * 2)
                rows(NTL - 1, 0)
                load(sp.value_load(tile_e[0:1, NTL - 1:NTL], min_val=0, max_val=NE - 1), g0 + NS + NTL - 1)
                load(NE, g0 + NS + NTL)
                load(NE + 1, g0 + NS + NTL + 1)

            def mixer(k):
                nf, _ = phase_counts(k)
                sp.wait_ge(f_wlo, nf * SETS * 3)
                sp.wait_ge(t_tp, nf * NTL * 2)
                sp.wait_ge(b_tp, nf * 2 * TB)
                sp.dma_start(zs[:], w_out.rearrange("a p k n -> p a (k n)")).then_inc(m_wo_raw, 16)
                for j in range(2):
                    sp.dma_start(w_raw[:, j], w_in[j]).then_inc(m_raw[j], 16)
                sp.dma_start(wdt_raw[:], w_dt).then_inc(m_wdt, 16)
                with sp.Fori(0, BPB * NWU - 1) as i:
                    for q in range(2):
                        w = i * 2 + 2 + q
                        sp.wait_ge(m_wlo, w - 1)
                        u = sp.snap(w % NWU)
                        sp.dma_start(w_raw[:, q], w_in[bass.ds(u, 1), :, :, :].rearrange("o p c n -> p (o c) n"))\
                            .then_inc(m_raw[q], 16)
                sp.wait_ge(m_wlo, BATCH * BPB * NWU - 1)
                sp.dma_start(w_raw[:, 0], w_in[0]).then_inc(m_raw[0], 16)

            for k, what in enumerate(PLAN):
                (ffn if what == "ffn" else mixer)(k)
            nf, _ = phase_counts(len(PLAN))
            shared, routed = nf * 2 * SJ * TB, nf * TOPK * NT

            def store(first, tiles):
                sp.dma_start(out[:, first:first + tiles, :], X[:, first:first + tiles, :]).then_inc(s_out, 16)

            sp.wait_ge(f_acc, shared - SJ * TB)
            for b in range(2):
                sp.wait_ge(g_add, routed - TOPK * (NT - (b + 1) * TB))
                store(b * TB, TB)
            sp.wait_ge(g_add, routed)
            sp.wait_ge(f_acc, shared - TB)
            store((2 + SECOND[2]) * TB, TB)
            for a in range(TB):
                sp.wait_ge(f_acc, shared - TB + a + 1)
                store((2 + SECOND[3]) * TB + a, 1)
            sp.wait_ge(s_out, (3 + TB) * 16)

        @block.gpsimd
        def _(pool):
            own = Chain(pool, c_pool)
            slot_rows = lambda c: bass.IndirectOffsetOnAxis(ap=slots[:, c:c + 1], axis=0)
            pool.memset(mhalf[:], -0.5).then_inc(s_ready, 1)
            pool.memset(zero_row[:], 0.0).then_inc(s_ready, 1)
            pool.memset(r_end[:], 0.0).then_inc(s_ready, 1)
            pool.memset(r_til[:], 0.0).then_inc(s_ready, 1)
            pool.memset(starts[:, 5:6], 0.0).then_inc(f_h, H0)
            pool.memset(starts[:, 0:1], 0.0).then_inc(f_hlo, LO0)
            pool.memset(starts[:, 1:2], 0.0).then_inc(t_dn, DN0)
            pool.memset(starts[:, 2:3], 0.0).then_inc(t_y, Y0)
            for q in range(2):
                pool.memset(starts[:, 3 + q:4 + q], 0.0).then_inc(t_st[q], ST0)
            own.mark(pool.memset(zero[:], 0.0))
            own.mark(pool.memset(eps[:], EPS))
            own.mark(pool.memset(by_di[:], 1.0 / DI))
            for e in range(24):
                own.mark(pool.memset(iota[:, e:e + 1], float(e)))
            own.mark(pool.memset(ident[:], 0.0))
            own.mark(pool.memset(tri[:], 1.0))
            own.join()
            pool.affine_select(out=ident[:], in_=ident[:], compare_op=ALU.not_equal, fill=1.0, base=0,
                               pattern=[[-1, P]], channel_multiplier=1).then_inc(s_ready, 1)
            pool.affine_select(out=tri[:], in_=tri[:], compare_op=ALU.is_ge, fill=0.0, base=0,
                               pattern=[[1, P]], channel_multiplier=-1).then_inc(s_ready, 1)
            pool.wait_ge(s_ready, READY)

            def rsqrt_ln(tiles, signal):
                n = tiles.stop - tiles.start
                own.step(pool.tensor_tensor(rstd[:, tiles], rstd[:, tiles], eps[:].broadcast_to([P, n]), ALU.add))
                pool.tensor_tensor(rstd[:, tiles], rstd[:, tiles], mhalf[:, 0:n], ALU.pow).then_inc(signal, 1)

            def ffn(k):
                nf, nm = phase_counts(k)
                g0 = nf * SETS

                def weights(piece, g, parity):
                    raw, hl = ((g_raw, g_hl), (u_raw, u_hl), (d_raw, d_hl))[piece]
                    pool.wait_ge(f_whi, g * 3 + (piece + 1))
                    if piece < 2:
                        pool.tensor_tensor(hl[:, parity, 1], raw[:], hl[:, parity, 0].bitcast(F), ALU.subtract)\
                            .then_inc(f_wlo, 1)
                    else:
                        fw = FE - 2 * P
                        pool.tensor_tensor(hl[:, parity, 1, 0:2], raw[:, 0:2], hl[:, parity, 0, 0:2].bitcast(F),
                                           ALU.subtract)
                        pool.tensor_tensor(hl[0:fw, parity, 1, 2], raw[0:fw, 2], hl[0:fw, parity, 0, 2].bitcast(F),
                                           ALU.subtract).then_inc(f_wlo, 1)

                for b in range(NB):
                    if b or not nm:
                        pool.wait_ge(n_var, nf * NB + b + 1 - nm)
                        rsqrt_ln(slice(b * TB, (b + 1) * TB), n_rstd)
                    for piece in ((0, 1), (2,), (), ())[b]:
                        weights(piece, g0, 0)
                for piece in range(3):
                    weights(piece, g0 + 1, 1)
                pool.wait_ge(n_slot, 2 * (nf + 1))
                pool.wait_ge(n_xn, (nf + 1) * NT)
                pool.wait_ge(d_zero, 16)
                for c in range(TOPK * NT):
                    pool.indirect_dma_start(routed_x, slot_rows(c), xn[:, c % NT], None).then_inc(d_sc, 16)
                for piece in range(3):
                    weights(piece, g0 + NS, 0)
                with pool.Fori(0, NTL // 2) as i:
                    for q in range(2):
                        for piece in range(3):
                            weights(piece, i * 2 + (g0 + NS + q + 1), (q + 1) % 2)
                for piece in range(3):
                    weights(piece, g0 + NS + NTL, 1)
                pool.wait_ge(t_st[0], (nf + 1) * EVEN * 16 + ST0)
                pool.wait_ge(t_st[1], (nf + 1) * ODD * 16 + ST0)
                pool.wait_ge(t_tp, (nf + 1) * NTL * 2)
                for t in range(NT):
                    if t == 2:
                        for piece in range(3):
                            weights(piece, g0 + NS + NTL + 1, 0)
                    if t >= 2:
                        pool.wait_ge(g_add, (nf * NT + t - 1) * TOPK)
                    for slot in range(TOPK):
                        pool.indirect_dma_start(yg[:, t % 2, slot], None, routed_y, slot_rows(slot * NT + t))\
                            .then_inc(g_y[t % 2], 16)

            def mixer(k):
                nf, _ = phase_counts(k)
                for q in range(TB):
                    pool.wait_ge(l_var, q + 1)
                    rsqrt_ln(slice(q, q + 1), l_rstd)
                pool.wait_ge(m_whi, 1)
                pool.tensor_tensor(w_hl[:, 0, 1], w_raw[:, 0], w_hl[:, 0, 0].bitcast(F), ALU.subtract).then_inc(m_wlo, 1)
                for piece in range(2):
                    pool.wait_ge(m_wo_hi, piece + 1)
                    pool.tensor_tensor(wo[:, 1, 2 * piece:2 * piece + 2], zs[:, piece].rearrange("p (k n) -> p k n", k=2),
                                       wo[:, 0, 2 * piece:2 * piece + 2].bitcast(F), ALU.subtract).then_inc(m_wo_lo0, 1)
                pool.wait_ge(g_add, nf * TOPK * NT)

                def turn(i):
                    after, settle = loop_waits(pool, i)
                    pool.tensor_tensor(S[:, 0], zero[:].broadcast_to([P, DI]), zero[:].broadcast_to([P, DI]), ALU.add)\
                        .then_inc(m_zero, 1)

                    def unit_lo(w):
                        after(m_whi, w + 1, BPB * NWU)
                        pool.tensor_tensor(w_hl[:, w % 2, 1], w_raw[:, w % 2], w_hl[:, w % 2, 0].bitcast(F),
                                           ALU.subtract).then_inc(m_wlo, 1)

                    def rms(n):
                        after(m_sq, n + 1, TPB)
                        it = slice(n % 2, n % 2 + 1)
                        own.step(pool.tensor_tensor(rs[:, it], ssq[:, it], by_di[:], ALU.mult))
                        own.step(pool.tensor_tensor(rs[:, it], rs[:, it], eps[:], ALU.add))
                        pool.tensor_tensor(rs[:, it], rs[:, it], mhalf[:, 0:1], ALU.pow).then_inc(m_rs, 1)

                    for j in range(BPB):
                        for u in range(NWU):
                            w = j * NWU + u
                            unit_lo(w + 1)
                            if u == 0 and j:
                                rms(j * TB - 1)
                        for q in range(TB):
                            n = j * TB + q
                            hq = slice(q * HEADS, (q + 1) * HEADS)
                            pool.wait_ge(l_var, i * TPB + (n + TB + 1))
                            rsqrt_ln(slice(q, q + 1), l_rstd)
                            after(m_dec, j + 1, BPB)
                            after(m_C, n, TPB)
                            after(m_S, n, TPB)
                            pool.wait_ge(m_zero, i + 1)
                            pool.tensor_tensor(S[:, (n + 1) % 2].rearrange("p (h d) -> p h d", d=HD),
                                               S[:, n % 2].rearrange("p (h d) -> p h d", d=HD),
                                               each(dec[:, hq], HD), ALU.mult).then_inc(m_Sd, 1)
                            after(m_xdt, n + 1, TPB)
                            after(m_D, n, TPB)
                            pool.tensor_tensor(xw[:].rearrange("p (h d) -> p h d", d=HD),
                                               xdt[:].rearrange("p (h d) -> p h d", d=HD),
                                               each(wd[:, hq], HD), ALU.mult).then_inc(m_xw, 1)
                            if q >= 1:
                                rms(n - 1)
                            after(m_yc, n + 1, TPB)
                            after(m_xD, n + 1, TPB)
                            pool.tensor_tensor(y[:, n % 2], y[:, n % 2], xD[:], ALU.add).then_inc(m_yd, 1)
                            after(m_yi, n + 1, TPB)
                            after(m_z, 8 * (j + 1), 8 * BPB)
                            pool.tensor_tensor(y[:, n % 2], y[:, n % 2], zs[:, q], ALU.mult).then_inc(m_yg, 1)
                    rms(TPB - 1)
                    settle((m_C, TPB), (m_S, TPB), (m_conv, BPB * NCH), (m_D, TPB))

                with pool.Fori(0, BATCH) as i:
                    own.enter(i, TPB * 3)
                    turn(i)
                own.leave(BATCH)

            for k, what in enumerate(PLAN):
                (ffn if what == "ffn" else mixer)(k)

        @block.scalar
        def _(act):
            act.wait_ge(s_const, 4 * 16)
            own = Chain(act, c_act)
            own.step(act.activation(negA[:], hp[:, HEADS:2 * HEADS], ACT.Exp))

            def split_hi(dst, src, signal):
                act.activation(dst, src, ACT.Copy).then_inc(signal, 1)

            def norm_w_out(chunks):
                act.wait_ge(m_wo_raw, 16)
                for c in chunks:
                    w = zs[:, c // 2, c % 2 * D:(c % 2 + 1) * D]
                    act.activation(w, w, ACT.Copy, scale=nw[:, c:c + 1]).then_inc(m_wo_n, 1)

            def first_hi(q):
                act.wait_ge(l_tp, q + 1)
                split_hi(xb[:, 0, :, q * P:(q + 1) * P], bank[4 + q][:].rearrange("p (c t) -> p c t", c=KD), l_hi)

            def ffn(k):
                nf, nm = phase_counts(k)
                g0, j0 = nf * SETS, nf * JOBS
                mixer_next = PLAN[k + 1:k + 2] == ("mixer",)
                wait_residual(act, k)

                def weights(piece, g, parity):
                    raw, hl, arrived, n = ((g_raw, g_hl, f_graw, 16), (u_raw, u_hl, f_uraw, 16),
                                           (d_raw, d_hl, f_draw, 32))[piece]
                    act.wait_ge(arrived, (g + 1) * n)
                    if piece < 2:
                        split_hi(hl[:, parity, 0], raw[:], f_whi)
                    else:
                        act.activation(hl[:, parity, 0, 0:2], raw[:, 0:2], ACT.Copy)
                        split_hi(hl[0:FE - 2 * P, parity, 0, 2], raw[0:FE - 2 * P, 2], f_whi)

                def x_copy(t):
                    n = nf * NT + t
                    act.wait_ge(n_tp, n + 1)
                    if t >= 2:
                        act.wait_ge(n_lg, n - 1)
                    act.activation(tmpT[t % 2][:], bank[5 + t % 3][:], ACT.Copy).then_inc(n_cp, 1)
                    if nm * TB <= t < 2 * TB:
                        split_hi(xs[t // TB][:, 0, :, t % TB * P:(t % TB + 1) * P],
                                 bank[5 + t % 3][:].rearrange("p (c t) -> p c t", c=KD), b_hi)

                def chunk(job, c, par, width, before):
                    fw = FCH[c][1]
                    v = job * NF + c
                    act.wait_ge(f_gu, v + 1)
                    act.wait_ge(f_hlo, v - 1 + LO0)
                    act.activation(gate[0:fw, par, 0:width], bank[par][0:fw, 0:width], ACT.Silu).then_inc(f_silu, 1)
                    act.wait_ge(f_h, v + 1 + H0)
                    if c == 0 and before:
                        act.wait_ge(*before)
                    split_hi(hT[0:fw, 0, c, 0:width], gate[0:fw, par, 0:width], f_hhi)

                def x_hi(t, bk):
                    act.wait_ge(b_tp, nf * 2 * TB + t - 2 * TB + 1)
                    split_hi(xs[(t // TB + 1) % 2][:, 0, :, t % TB * P:(t % TB + 1) * P],
                             bank[bk][:].rearrange("p (c t) -> p c t", c=KD), b_hi)

                def rows_hi(j, q, banks):
                    for a in range(2):
                        act.wait_ge(t_tp, (j + nf * NTL) * 2 + (a + 1))
                        split_hi(xgT[:, q, 0, :, a * P:(a + 1) * P],
                                 bank[banks[a]][:].rearrange("p (c t) -> p c t", c=KD), t_hi)

                def results(j, q, before):
                    for a in range(2):
                        act.wait_ge(t_dn, (j + nf * NTL) * 2 + (a + 1 + DN0))
                        if a == 0:
                            act.wait_ge(t_st[q], before * 16 + ST0)
                        act.activation(ys[:, q, a], bank[4 + a][:], ACT.Copy).then_inc(t_y, 1)
                    act.wait_ge(t_y, (j + nf * NTL + 1) * 2 + Y0)
                    act.dma_start(routed_y[bass.ds(j * TS, TS), :].rearrange("(a p) n -> p a n", p=P), ys[:, q])\
                        .then_inc(t_st[q], 16)

                weights(0, g0, 0)
                weights(1, g0, 0)
                for t in range(TB):
                    x_copy(t)
                weights(2, g0, 0)
                for job in range(SJ):
                    for c in range(NF):
                        if job == 0:
                            for pair in PAIRS[2 * c:2 * c + 2]:
                                for t in pair:
                                    x_copy(t)
                        if job == 0 and c == NF - 1:
                            act.wait_ge(n_lg, (nf + 1) * NT)
                        chunk(j0 + job, c, (job * NF + c) % 2, D, (f_dn, (nf * 2 * SJ + job) * TB) if job else None)
                        if job == 0:
                            weights(c, g0 + 1, 1)
                        if job == SJ // 2:
                            weights(c, g0 + NS, 0)
                    if job == 0:
                        act.wait_ge(n_sh, nf + 1)
                        act.activation(r_b[:], r_a[:], ACT.Exp).then_inc(n_ex, 1)
                weights(0, g0 + NS + 1, 1)
                par = (SJ * NF) % 2
                rows_hi(0, 0, (par, 2 + par))
                act.wait_ge(f_dn, (nf * 2 + 1) * SJ * TB)

                def tile(j, q, half, last):
                    job = j + (j0 + SJ)
                    for c in range(NF):
                        chunk(job, c, (q * NF + c) % 2, TS, (t_dn, (j + nf * NTL) * 2 + DN0))
                        if c == 0 and not last:
                            rows_hi(j + 1, (q + 1) % 2, (6, 7))
                        if c < 2:
                            weights(c + 1, j + (g0 + NS + 1), (q + 1) % 2)
                        else:
                            weights(0, j + (g0 + NS + 2), q)
                    if last:
                        for t, bk in zip(range(2 * TB, 3 * TB), LATE_BANKS):
                            x_hi(t, bk)
                    results(j, q, half + nf * (EVEN, ODD)[q])

                with act.Fori(0, NTL // 2) as i:
                    for q in range(2):
                        tile(i * 2 + q, q, i, False)
                tile(NTL - 1, 0, NTL // 2, True)

                for job in range(SJ):
                    v = (SJ + NTL + job) * NF
                    for c in range(NF):
                        chunk(j0 + SJ + NTL + job, c, (v + c) % 2, D,
                              (f_dn, ((nf * 2 + 1) * SJ + job) * TB) if job else (t_dn, (nf + 1) * NTL * 2 + DN0))
                        if job == 0 and c < 2:
                            weights(c + 1, g0 + NS + NTL + 1, 0)
                        if job == SJ - 1 and c >= 1 and mixer_next:
                            first_hi(2 * c - 2)
                            first_hi(2 * c - 1)
                        if job == SJ - 2 and mixer_next:
                            norm_w_out(range(c * NF, min((c + 1) * NF, KI)))
                    if job == 0:
                        act.wait_ge(t_st[0], (nf + 1) * EVEN * 16 + ST0)
                        act.wait_ge(t_st[1], (nf + 1) * ODD * 16 + ST0)
                        for a in range(TB):
                            x_hi(3 * TB + a, (v + 1) % 2 + 2 * (a % 2))

            def mixer(k):
                nf, nm = phase_counts(k)
                act.wait_ge(m_wo_n, KI)
                act.wait_ge(f_gu, nf * JOBS * NF)
                act.wait_ge(m_raw[0], 16)
                split_hi(w_hl[:, 0, 0], w_raw[:, 0], m_whi)
                for piece in range(4):
                    split_hi(wo[:, 0, 2 * piece:2 * piece + 2], zs[:, piece].rearrange("p (k n) -> p k n", k=2), m_wo_hi)

                def turn(i):
                    after, settle = loop_waits(act, i)

                    def unit_hi(w):
                        after(m_raw[w % 2], w // 2 + 1, BPB * NWU // 2, unit=16)
                        if w >= 2:
                            jj, u = divmod(w - 2, NWU)
                            if u < 5:
                                after(m_cp, jj * NCH + 2 * u + 2, BPB * NCH)
                            else:
                                after(m_zp, jj * 8 + (u - 5) * 2 + 2, 8 * BPB)
                        split_hi(w_hl[:, w % 2, 0], w_raw[:, w % 2], m_whi)

                    def conv_in(n, c):
                        b = bank[c % 2]
                        after(m_cp, n + 1, BPB * NCH)
                        after(m_conv, n - 1, BPB * NCH)
                        act.activation(pre[:, c % 2, TAPS - 1:], b[:], ACT.Copy)
                        after(m_xc, n - 1, BPB * NCH)
                        act.activation(acc[:, c % 2], b[:], ACT.Identity, bias=cw[:, c, TAPS:TAPS + 1],
                                       scale=cw[:, c, TAPS - 1:TAPS]).then_inc(m_pre, 1)

                    def conv_out(n, c):
                        after(m_conv, n + 1, BPB * NCH)
                        act.activation(xc[:, c], acc[:, c % 2], ACT.Silu).then_inc(m_xc, 1)

                    def y_hi(n):
                        for half in range(2):
                            after(m_F, 2 * n + half + 1, 2 * TPB)
                            after(m_out, n, TPB)
                            split_hi(yT[:, 0, 4 * half:4 * half + 4],
                                     bank[6 + half][:].rearrange("p (c t) -> p c t", c=4), m_yhi)

                    def squares(n):
                        after(m_yg, n + 1, TPB)
                        after(m_rs, n - 1, TPB)
                        after(m_sq, n, TPB)
                        act.activation(ysq[:], y[:, n % 2], ACT.Square, accum_out=ssq[:, n % 2:n % 2 + 1]).then_inc(m_sq, 1)

                    for j in range(BPB):
                        for u in range(NWU):
                            w = j * NWU + u
                            unit_hi(w + 1)
                            if u < 5:
                                for c in (2 * u, 2 * u + 1):
                                    n = j * NCH + c
                                    conv_in(n, c)
                                    if c == 1:
                                        after(m_D, j * TB, TPB)
                                    if c >= 1:
                                        conv_out(n - 1, c - 1)
                                if u == 0 and j:
                                    y_hi(j * TB - 1)
                                    squares(j * TB - 1)
                                if u == 1:
                                    after(m_dtT, j + 1, BPB)
                                    after(m_yd, j * TB, TPB)
                                    act.activation(dtT, bank[3][0:HEADS, :], ACT.Copy).then_inc(m_dtc, 1)
                            else:
                                if u == 5:
                                    conv_out(j * NCH + NCH - 1, NCH - 1)
                                    act.wait_ge(m_wo_lo0, 2)
                                    act.wait_ge(m_wo_lo1, 2)
                                    after(m_yg, j * TB, TPB)
                                for half in range(2):
                                    n = j * 8 + (u - 5) * 2 + half
                                    after(m_zp, n + 1, 8 * BPB)
                                    act.activation(zs[:, 2 * half:2 * half + 2, (u - 5) * WU:(u - 4) * WU],
                                                   bank[6 + half][:].rearrange("p (q n) -> p q n", q=2),
                                                   ACT.Silu).then_inc(m_z, 1)
                                if u == 6:
                                    after(m_dx, j + 1, BPB)
                                    act.activation(d_e[:], d_z[:], ACT.Exp).then_inc(m_de, 1)
                        after(m_cs, j + 1, BPB)
                        after(m_ncs, j + 1, BPB)
                        cs, tot = bank[2][:, NQ:2 * NQ], bank[2][:, 2 * NQ:3 * NQ]
                        act.activation(ecs[:], cs, ACT.Exp)
                        act.activation(dec[:], tot, ACT.Exp)
                        act.activation(wd[:], d_p[:], ACT.Exp).then_inc(m_dec, 1)
                        for q in range(TB):
                            n = j * TB + q
                            for g in range(HG):
                                after(m_B, HG * n + g + 1, HG * TPB)
                                after(m_E, n, TPB)
                                for h in range(g * GH, (g + 1) * GH):
                                    ins = act.activation(L[:, h], bank[g % 2][:, (h % GH) * P:(h % GH + 1) * P], ACT.Exp,
                                                         bias=ncs[:, q * HEADS + h:q * HEADS + h + 1])
                                ins.then_inc(m_L, 1)
                                if g == 0:
                                    after(m_G, n + 1, TPB)
                                    after(m_D, n, TPB)
                                    after(m_M, HG * n, HG * TPB)
                                    act.activation(GB[:], bank[3][:, 0:2 * P], ACT.Copy).then_inc(m_Bt, 1)
                                if g == 1 and q >= 1:
                                    y_hi(n - 1)
                            if q >= 1:
                                squares(n - 1)
                            act.wait_ge(l_tp, i * TPB + (n + TB + 1))
                            split_hi(xb[:, 0, :, q * P:(q + 1) * P], bank[3][:].rearrange("p (c t) -> p c t", c=KD), l_hi)
                    y_hi(TPB - 1)
                    squares(TPB - 1)
                    settle((m_zp, 8 * BPB), (m_conv, BPB * NCH), (m_xc, BPB * NCH),
                           (m_yg, TPB), (m_D, TPB), (m_E, TPB), (m_M, HG * TPB), (m_rs, TPB), (m_sq, TPB),
                           (m_out, TPB), (m_yd, TPB))

                act.wait_ge(m_wdt, 16)
                split_hi(wdt[:, 0], wdt_raw[:], m_wdt_hi)
                with act.Fori(0, BATCH) as i:
                    turn(i)

            for k, what in enumerate(PLAN):
                (ffn if what == "ffn" else mixer)(k)

        @block.vector
        def _(dve):
            own = Chain(dve, c_dve)

            def ln_stats(tiles, places, signal):
                for xt, s in zip(tiles, places):
                    own.mark(dve.bn_stats(stats[:, s, :], xt))
                own.join()
                dve.tensor_copy(carrier[:], mhalf[:, 0:1])
                for s in places:
                    own.mark(dve.bn_aggr(mv[:, s, :], stats[:, s, :]))
                own.join()
                dve.tensor_copy(rstd[:, places[0]:places[-1] + 1],
                                mv[:, places[0]:places[-1] + 1, 1:2].rearrange("p t o -> p (t o)")).then_inc(signal, 1)

            def ln_scale(dst, xt, s):
                return dve.tensor_scalar(dst, xt, mv[:, s, 0:1], rstd[:, s:s + 1], ALU.subtract, ALU.mult)

            def lo_half(hl_lo, value, hl_hi, signal):
                dve.tensor_tensor(hl_lo, value, hl_hi.bitcast(F), ALU.subtract).then_inc(signal, 1)

            def ffn(k):
                nf, nm = phase_counts(k)
                j0 = nf * JOBS
                wait_residual(dve, k)

                def block_stats(b):
                    if k == 0:
                        dve.wait_ge(s_x[b], 16)
                    tiles = range(b * TB, (b + 1) * TB)
                    ln_stats([X[:, t, :] for t in tiles], tiles, n_var)

                def block_scale(b):
                    if b or not nm:
                        dve.wait_ge(n_rstd, nf * NB + b + 1 - nm)
                    for t in range(b * TB, (b + 1) * TB):
                        ln_scale(xn[:, t], X[:, t, :], t).then_inc(n_xn, 1)

                def x_lo_first(tiles):
                    for t in tiles:
                        b = t // TB
                        at = slice(t % TB * P, (t % TB + 1) * P)
                        dve.wait_ge(b_hi, nf * NT + t + 1 - nm * TB)
                        lo_half(xs[b][:, 1, :, at], bank[5 + t % 3][:].rearrange("p (c t) -> p c t", c=KD),
                                xs[b][:, 0, :, at], b_lo0)

                def shift_logits():
                    logits = bank[4][:, 0:NT * NE].rearrange("p (t e) -> p t e", e=NE)
                    dve.wait_ge(n_lg, (nf + 1) * NT)
                    own.step(dve.tensor_reduce(r_1[:], logits, AX.X, ALU.max))
                    dve.tensor_tensor(r_a[:], logits, each(r_1[:], NE), ALU.subtract).then_inc(n_sh, 1)

                def choose():
                    dve.wait_ge(n_ex, nf + 1)
                    own.step(dve.tensor_reduce(r_1[:], r_b[:], AX.X, ALU.add))
                    own.step(dve.reciprocal(r_2[:], r_1[:]))
                    own.step(dve.tensor_tensor(r_a[:], r_b[:], each(r_2[:], NE), ALU.mult))
                    for t in range(NT):
                        own.mark(dve.max(r_top[:, t], r_a[:, t]))
                    own.join()
                    for t in range(NT):
                        own.mark(dve.max_index(r_idx[:, t], r_top[:, t], r_a[:, t]))
                    own.join()
                    for slot in range(TOPK):
                        own.mark(dve.tensor_scalar(r_val[:, slot], r_top[:, :, slot], ROUTE, None, ALU.mult))
                        own.mark(dve.tensor_copy(r_exp[:, slot], r_idx[:, :, slot]))
                    own.join()
                    own.step(dve.tensor_tensor(r_msk[:], some(iota[:, 0:NE], TOPK * NT),
                                               each(r_exp[:].rearrange("p s t -> p (s t)"), NE), ALU.is_equal))
                    dve.tensor_tensor(r_sum[:], r_msk[:, 0:NT], r_msk[:, NT:2 * NT], ALU.add).then_inc(n_msk, 1)

                def place_rows():
                    rank = bank[1][:, 0:NT * NE].rearrange("p (t e) -> p t e", e=NE)
                    dve.wait_ge(n_rank, nf + 1)
                    own.mark(dve.tensor_copy(r_cnt[:], bank[1][:, NT * NE:NT * NE + NE]))
                    dve.tensor_copy(r_a[:], rank).then_inc(n_rcp, 1)
                    dve.wait_ge(n_rcp, nf + 1)
                    own.join()
                    own.step(dve.tensor_scalar(r_1[:, 0:NE], iota[:, 0:NE], float(TS), None, ALU.mult))
                    own.step(dve.tensor_tensor(r_cmp[:, 0:NE], each(r_cnt[:], NE), some(r_1[:, 0:NE], NE), ALU.is_gt))
                    own.step(dve.tensor_reduce(r_til[:, 4:], r_cmp[:, 0:NE], AX.X, ALU.add))
                    own.step(dve.tensor_tensor(r_end[:, 0, 4:], r_til[:, 4:], r_til[:, 3:3 + NE], ALU.add))
                    own.step(dve.tensor_tensor(r_end[:, 1, 4:], r_end[:, 0, 4:], r_end[:, 0, 2:2 + NE], ALU.add))
                    own.step(dve.tensor_tensor(r_end[:, 0, 4:], r_end[:, 1, 4:], r_end[:, 1, 0:NE], ALU.add))
                    own.step(dve.tensor_tensor(r_1[:, 0:NE], r_end[:, 0, 4:], r_til[:, 4:], ALU.subtract))
                    own.step(dve.tensor_scalar(r_1[:, 0:NE], r_1[:, 0:NE], float(TS), None, ALU.mult))
                    own.step(dve.tensor_tensor(r_b[:], r_a[:], some(r_1[:, 0:NE], NT), ALU.add))
                    for slot in range(TOPK):
                        own.mark(dve.tensor_tensor(r_msk[:, slot * NT:(slot + 1) * NT], r_msk[:, slot * NT:(slot + 1) * NT],
                                                   r_b[:], ALU.mult))
                    own.join()
                    own.step(dve.tensor_reduce(r_pos[:], r_msk[:], AX.X, ALU.add))
                    dve.tensor_copy(slots[:], r_pos[:]).then_inc(n_slot, 1)
                    own.step(dve.tensor_tensor(r_cmp[:], each(iota[:, 0:NTL], NE), some(r_end[:, 0, 4:], NTL), ALU.is_ge))
                    own.step(dve.tensor_reduce(r_te[:], r_cmp[:], AX.X, ALU.add))
                    own.step(dve.tensor_scalar(r_te[:], r_te[:], float(NE - 1), None, ALU.min))
                    dve.tensor_copy(tile_e[:], r_te[:]).then_inc(n_slot, 1)

                def chunk(job, c, par, width):
                    fw = FCH[c][1]
                    v = job * NF + c
                    dve.wait_ge(f_silu, v + 1)
                    dve.tensor_tensor(gate[0:fw, par, 0:width], gate[0:fw, par, 0:width], bank[2 + par][0:fw, 0:width],
                                      ALU.mult).then_inc(f_h, 1)
                    dve.wait_ge(f_hhi, v + 1)
                    lo_half(hT[0:fw, 1, c, 0:width], gate[0:fw, par, 0:width], hT[0:fw, 0, c, 0:width], f_hlo)

                n_acc, n_add = [nf * 2 * SJ * TB], [nf * TOPK * NT]

                def residual_written():
                    dve.wait_ge(f_acc, n_acc[0])
                    dve.wait_ge(g_add, n_add[0])

                def add_shared(b):
                    for a in range(TB):
                        t = b * TB + a
                        dve.wait_ge(f_dn, n_acc[0] + 1)
                        residual_written()
                        dve.scalar_tensor_tensor(X[:, t, :], bank[4 + a][:], ROUTE, X[:, t, :], ALU.mult, ALU.add)\
                            .then_inc(f_acc, 1)
                        n_acc[0] += 1

                def add_routed(t):
                    dve.wait_ge(g_y[t % 2], (nf * NT // 2 + t // 2 + 1) * TOPK * 16)
                    for slot in range(TOPK):
                        residual_written()
                        dve.scalar_tensor_tensor(X[:, t, :], yg[:, t % 2, slot], r_val[:, slot, t:t + 1], X[:, t, :],
                                                 ALU.mult, ALU.add).then_inc(g_add, 1)
                        n_add[0] += 1

                def x_lo(t, bk):
                    dve.wait_ge(b_hi, nf * NT + t + 1 - nm * TB)
                    lo_half(xs[(t // TB + 1) % 2][:, 1, :, t % TB * P:(t % TB + 1) * P],
                            bank[bk][:].rearrange("p (c t) -> p c t", c=KD),
                            xs[(t // TB + 1) % 2][:, 0, :, t % TB * P:(t % TB + 1) * P], b_lo1)

                def first_lo(q):
                    dve.wait_ge(l_hi, q + 1)
                    lo_half(xb[:, 1, :, q * P:(q + 1) * P], bank[4 + q][:].rearrange("p (c t) -> p c t", c=KD),
                            xb[:, 0, :, q * P:(q + 1) * P], l_lo)

                def rows_lo(j, q, banks):
                    for a in range(2):
                        dve.wait_ge(t_hi, (j + nf * NTL) * 2 + (a + 1))
                        lo_half(xgT[:, q, 1, :, a * P:(a + 1) * P],
                                bank[banks[a]][:].rearrange("p (c t) -> p c t", c=KD),
                                xgT[:, q, 0, :, a * P:(a + 1) * P], t_lo)

                if not nm:
                    block_stats(0)
                block_scale(0)
                block_stats(1)
                if not nm:
                    x_lo_first(range(TB))
                block_scale(1)
                block_stats(2)
                block_scale(2)
                for job in range(SJ):
                    for c in range(NF):
                        if job == 0 and c == 0:
                            x_lo_first(range(TB, 2 * TB))
                        if job == 0 and c == NF - 1:
                            shift_logits()
                        chunk(j0 + job, c, (job * NF + c) % 2, D)
                        if job == 0 and c == 0:
                            block_stats(3)
                            block_scale(3)
                    if job == 0:
                        choose()
                        place_rows()
                    if job < SJ - 1:
                        add_shared(job % 2)
                par = (SJ * NF) % 2
                rows_lo(0, 0, (par, 2 + par))
                add_shared((SJ - 1) % 2)

                def tile(j, q, last):
                    job = j + (j0 + SJ)
                    for c in range(NF):
                        chunk(job, c, (q * NF + c) % 2, TS)
                        if c == 0 and not last:
                            rows_lo(j + 1, (q + 1) % 2, (6, 7))

                with dve.Fori(0, NTL // 2) as i:
                    for q in range(2):
                        tile(i * 2 + q, q, False)
                tile(NTL - 1, 0, True)
                for t, bk in zip(range(2 * TB, 3 * TB), LATE_BANKS):
                    x_lo(t, bk)
                for job in range(SJ):
                    v = (SJ + NTL + job) * NF
                    to_mixer = job == SJ - 1 and PLAN[k + 1:k + 2] == ("mixer",)
                    for c in range(NF):
                        chunk(j0 + SJ + NTL + job, c, (v + c) % 2, D)
                        if to_mixer and c >= 1:
                            first_lo(2 * c - 2)
                            first_lo(2 * c - 1)
                        for q in range(2 * c, 2 * c + 2) if to_mixer and c < 2 else ():
                            dve.wait_ge(l_rstd, q + 1)
                            if q >= 2:
                                dve.wait_ge(l_tp, q - 1)
                            ln_scale(xn_m[:, q % 2], X[:, q, :], q).then_inc(l_xn, 1)
                        first = (job * NF + c - 2) * 2
                        for t in range(max(first, 0), min(first + 2, NT)):
                            add_routed(t)
                        if PLAN[k + 1:k + 2] == ("mixer",) and (job, c) == (SJ - 2, NF - 1):
                            residual_written()
                            for q in range(TB):
                                ln_stats([X[:, q, :]], [q], l_var)
                    if job == 0:
                        for a in range(TB):
                            x_lo(3 * TB + a, (v + 1) % 2 + 2 * (a % 2))
                    add_shared(2 + SECOND[job])

            def mixer(k):
                nf, nm = phase_counts(k)
                wait_residual(dve, k)
                def turn(i):
                    after, settle = loop_waits(dve, i)

                    def heads_of(ap):
                        return ap.rearrange("p (h d) -> p h d", d=HD)

                    def y_lo(n):
                        for half in range(2):
                            after(m_yhi, 2 * n + half + 1, 2 * TPB)
                            lo_half(yT[:, 1, 4 * half:4 * half + 4],
                                    bank[6 + half][:].rearrange("p (c t) -> p c t", c=4),
                                    yT[:, 0, 4 * half:4 * half + 4], m_ylo)

                    def residual(n):
                        xt = X[:, bass.ds(i * TPB + n, 1), :].rearrange("p o n -> p (o n)")
                        after(m_out, n + 1, TPB)
                        after(m_rs, n + 1, TPB)
                        dve.scalar_tensor_tensor(xt, bank[2][:], rs[:, n % 2:n % 2 + 1], xt,
                                                 ALU.mult, ALU.add).then_inc(m_res, 1)

                    for j in range(BPB):
                        def conv(c):
                            n = j * NCH + c
                            after(m_pre, n + 1, BPB * NCH)
                            own.mark(dve.tensor_copy(pre[:, c % 2, 0:TAPS - 1],
                                                     halo[:, c] if j else zero[:].broadcast_to([P, TAPS - 1])))
                            if j < BPB - 1:
                                own.mark(dve.tensor_copy(halo[:, c], pre[:, c % 2, D:D + TAPS - 1]))
                            own.join()
                            for tap in range(TAPS - 1):
                                ins = dve.scalar_tensor_tensor(acc[:, c % 2], pre[:, c % 2, tap:tap + D],
                                                               cw[:, c, tap:tap + 1], acc[:, c % 2], ALU.mult, ALU.add)
                                if tap < TAPS - 2:
                                    own.step(ins)
                            ins.then_inc(m_conv, 1)

                        def softplus():
                            three = lambda t: t[:].rearrange("p (q h) -> p q h", h=HEADS)
                            after(m_dtp, j + 1, BPB)
                            own.step(dve.tensor_tensor(three(d_x), bank[2][:, 0:NQ].rearrange("p (q h) -> p q h", h=HEADS),
                                                       some(hp[:, 0:HEADS], TB), ALU.add))
                            own.step(dve.tensor_scalar(d_q[:], d_x[:], -1.0, None, ALU.mult))
                            dve.tensor_tensor(d_z[:], d_x[:], d_q[:], ALU.min).then_inc(m_dx, 1)

                        def log1p():
                            three = lambda t: t[:].rearrange("p (q h) -> p q h", h=HEADS)
                            after(m_de, j + 1, BPB)
                            own.step(dve.tensor_scalar(d_q[:], d_e[:], 2.0, None, ALU.add))
                            own.step(dve.reciprocal(d_p[:], d_q[:]))
                            own.step(dve.tensor_tensor(d_z[:], d_e[:], d_p[:], ALU.mult))
                            own.step(dve.tensor_tensor(d_q[:], d_z[:], d_z[:], ALU.mult))
                            own.step(dve.tensor_scalar(d_p[:], d_q[:], LOG1P[-1], None, ALU.mult))
                            for c in reversed(LOG1P[:-1]):
                                own.step(dve.scalar_tensor_tensor(d_p[:], d_p[:], c, d_q[:], ALU.add, ALU.mult))
                            own.step(dve.scalar_tensor_tensor(d_p[:], d_p[:], 1.0, d_z[:], ALU.add, ALU.mult))
                            own.step(dve.tensor_scalar(d_x[:], d_x[:], 0.0, None, ALU.max))
                            own.step(dve.scalar_tensor_tensor(dts[:], d_p[:], 2.0, d_x[:], ALU.mult, ALU.add))
                            own.step(dve.tensor_tensor(three(d_a), three(dts), some(negA[:], TB), ALU.mult))
                            own.step(dve.tensor_scalar(d_a[:], d_a[:], -1.0, DECAY_FLOOR, ALU.mult, ALU.max))
                            own.step(dve.tensor_copy(aparts[:, 0], d_a[:]))
                            own.step(dve.tensor_tensor(d_q[:], d_a[:], aparts[:, 0], ALU.subtract))
                            own.step(dve.tensor_copy(aparts[:, 1], d_q[:]))
                            own.step(dve.tensor_tensor(d_a[:], d_q[:], aparts[:, 1], ALU.subtract))
                            dve.tensor_copy(aparts[:, 2], d_a[:]).then_inc(m_ap, 1)

                        for c in range(NCH):
                            conv(c)
                            if j and c == 0:
                                y_lo(j * TB - 1)
                            if j and c == 3:
                                residual(j * TB - 1)
                            if c == NCH - 3:
                                softplus()
                        log1p()
                        after(m_cs, j + 1, BPB)
                        own.step(dve.tensor_scalar(ncs[:], bank[2][:, NQ:2 * NQ], -1.0, None, ALU.mult))
                        dve.tensor_tensor(d_p[:], bank[2][:, 2 * NQ:3 * NQ], ncs[:], ALU.add).then_inc(m_ncs, 1)

                        for q in range(TB):
                            n = j * TB + q
                            hq = slice(q * HEADS, (q + 1) * HEADS)
                            HB = HEADS // 2
                            nxt = i * TPB + (n + TB)
                            if j == BPB - 1:
                                nxt = dve.snap(nxt % NT)
                            x_next = X[:, bass.ds(nxt, 1), :].rearrange("p o n -> p (o n)")
                            ln_stats([x_next], [q], l_var)
                            for half in range(2):
                                hs = slice(half * DI // 2, (half + 1) * DI // 2)
                                after(m_xt, 2 * n + half + 1, 2 * TPB)
                                if half == 0:
                                    after(m_xw, n, TPB)
                                    after(m_E, n, TPB)
                                ins = dve.tensor_tensor(heads_of(xdt[:, hs]), heads_of(bank[4 + half][:]),
                                                        each(dts[:, q * HEADS + half * HB:q * HEADS + (half + 1) * HB], HD),
                                                        ALU.mult)
                                if half == 0:
                                    own.mark(ins)
                            ins.then_inc(m_xdt, 1)
                            if q >= 1:
                                y_lo(n - 1)
                            after(m_yd, n, TPB)
                            for half in range(2):
                                hs = slice(half * DI // 2, (half + 1) * DI // 2)
                                ins = dve.tensor_tensor(heads_of(xD[:, hs]), heads_of(bank[4 + half][:]),
                                                        each(hp[:, 2 * HEADS + half * HB:2 * HEADS + (half + 1) * HB], HD),
                                                        ALU.mult)
                                if half == 0:
                                    own.mark(ins)
                            ins.then_inc(m_xD, 1)
                            dve.wait_ge(l_rstd, i * TPB + (n + TB + 1))
                            dve.wait_ge(l_tp, i * TPB + (n + TB - 1))
                            ln_scale(xn_m[:, q % 2], x_next, q).then_inc(l_xn, 1)
                            after(m_Bt, n + 1, TPB)
                            for g in range(HG):
                                after(m_L, HG * n + g + 1, HG * TPB)
                                dve.tensor_tensor(L[:, g * GH:(g + 1) * GH], L[:, g * GH:(g + 1) * GH],
                                                  some(GB[:, 0:P], GH), ALU.mult).then_inc(m_M, 1)
                            if q >= 1:
                                residual(n - 1)
                            after(m_C, n + 1, TPB)
                            after(m_dec, j + 1, BPB)
                            after(m_F, 2 * (n - 1), 2 * TPB)
                            after(m_sq, n - 1, TPB)
                            for half in range(2):
                                hs = slice(half * DI // 2, (half + 1) * DI // 2)
                                ins = dve.tensor_tensor(heads_of(y[:, n % 2, hs]), heads_of(bank[6 + half][:]),
                                                        each(ecs[:, q * HEADS + half * HB:q * HEADS + (half + 1) * HB], HD),
                                                        ALU.mult)
                                if half == 0:
                                    own.mark(ins)
                            ins.then_inc(m_yc, 1)
                            dve.wait_ge(l_hi, i * TPB + (n + TB + 1))
                            lo_half(xb[:, 1, :, q * P:(q + 1) * P], bank[3][:].rearrange("p (c t) -> p c t", c=KD),
                                    xb[:, 0, :, q * P:(q + 1) * P], l_lo)
                            after(m_D, n + 1, TPB)
                            after(m_Sd, n + 1, TPB)
                            new = S[:, (n + 1) % 2]
                            own.mark(dve.tensor_tensor(new[:, 0:DI // 2], new[:, 0:DI // 2], bank[4][:], ALU.add))
                            dve.tensor_tensor(new[:, DI // 2:DI], new[:, DI // 2:DI], bank[5][:], ALU.add).then_inc(m_S, 1)
                            after(m_E, n + 1, TPB)
                            after(m_yd, n + 1, TPB)
                            own.mark(dve.tensor_tensor(y[:, n % 2, 0:DI // 2], y[:, n % 2, 0:DI // 2], bank[6][:],
                                                       ALU.add))
                            dve.tensor_tensor(y[:, n % 2, DI // 2:DI], y[:, n % 2, DI // 2:DI], bank[7][:], ALU.add)\
                                .then_inc(m_yi, 1)
                    y_lo(TPB - 1)
                    residual(TPB - 1)
                    settle((m_xw, TPB), (m_yd, TPB), (m_E, TPB), (m_F, 2 * TPB), (m_sq, TPB), (m_out, TPB),
                           (m_yg, TPB), (l_tp, TPB))

                for piece in range(2, 4):
                    dve.wait_ge(m_wo_hi, piece + 1)
                    lo_half(wo[:, 1, 2 * piece:2 * piece + 2], zs[:, piece].rearrange("p (k n) -> p k n", k=2),
                            wo[:, 0, 2 * piece:2 * piece + 2], m_wo_lo1)
                dve.wait_ge(m_wdt_hi, 1)
                lo_half(wdt[:, 1], wdt_raw[:], wdt[:, 0], m_wdt_lo)
                own_steps = 2 * TB + NCH * (TAPS - 2) + 2 + 21 + 1 + TB * 5
                with dve.Fori(0, BATCH) as i:
                    own.enter(i, BPB * own_steps + NCH * (2 * BPB - 1))
                    turn(i)
                own.leave(BATCH)

            dve.wait_ge(s_ready, READY)
            own.mark(dve.tensor_copy(tri_b[:], tri[:]))
            own.mark(dve.tensor_copy(ident_b[:], ident[:]))
            own.mark(dve.memset(ones_b[:], 1.0))
            own.mark(dve.tensor_tensor(stri_b[:], tri[:], ident[:], ALU.subtract))
            dve.tensor_scalar(mask_b[:], tri[:], 1.0, -MASKED, ALU.subtract, ALU.mult).then_inc(s_bf, 1)
            for k, what in enumerate(PLAN):
                (ffn if what == "ffn" else mixer)(k)

        @block.tensor
        def _(pe):
            pe.wait_ge(s_ready, READY)
            pe.wait_ge(s_bf, 1)
            pe.wait_ge(s_const, 64)

            def ffn(k):
                nf, nm = phase_counts(k)
                g0, j0 = nf * SETS, nf * JOBS
                wait_residual(pe, k)

                def transpose(bk, src, signal):
                    for c in range(KD):
                        ins = pe.transpose(bank[bk][:, c * P:(c + 1) * P], src[:, c * P:(c + 1) * P], ident[:])
                    ins.then_inc(signal, 1)

                def logits(t):
                    pe.wait_ge(n_cp, nf * NT + t + 1)
                    for c in range(KD):
                        ins = pe.matmul(bank[4][:, t * NE:(t + 1) * NE], tmpT[t % 2][:, c * P:(c + 1) * P], wr[:, c],
                                        start=(c == 0), stop=(c == KD - 1))
                    ins.then_inc(n_lg, 1)

                def transpose_x(tiles):
                    for t in tiles:
                        pe.wait_ge(n_xn, nf * NT + t + 1)
                        if t >= 3:
                            pe.wait_ge(n_cp, nf * NT + t - 2)
                            pe.wait_ge(b_lo0, nf * 2 * TB - nm * TB + min(t - 2, 2 * TB))
                        transpose(5 + t % 3, xn[:, t], n_tp)

                def router(half):
                    for t in PAIRS[half]:
                        logits(t)
                    if half + 1 < len(PAIRS):
                        transpose_x(PAIRS[half + 1])

                def ranks():
                    pe.wait_ge(n_msk, nf + 1)
                    pe.wait_ge(f_h, j0 * NF + 2 + H0)
                    rank = bank[1][:, 0:NT * NE]
                    pe.matmul(rank, stri_b[:], r_sum[:].rearrange("p t e -> p (t e)"), start=True, stop=False)
                    for t in range(NT - 1):
                        pe.matmul(bank[1][:, (t + 1) * NE:NT * NE].rearrange("p (t e) -> p t e", e=NE), ones_b[:],
                                  some(r_sum[:, t], NT - 1 - t), start=False, stop=(t == NT - 2))
                    for t in range(NT):
                        ins = pe.matmul(bank[1][:, NT * NE:NT * NE + NE], ones_b[:], r_sum[:, t],
                                        start=(t == 0), stop=(t == NT - 1))
                    ins.then_inc(n_rank, 1)

                def gate_up(job, c, par, wpar, x_of, width, beside=None):
                    f0, fw = FCH[c]
                    v = job * NF + c
                    pe.wait_ge(f_h, v - 1 + H0)
                    for part, (w, dst) in enumerate(((g_hl, bank[par]), (u_hl, bank[2 + par]))):
                        n = 0
                        for kc in range(KD):
                            for hw, hx in HALVES:
                                ins = pe.matmul(dst[0:fw, 0:width], w[:, wpar, hw, kc, f0:f0 + fw], x_of(hx, kc),
                                                start=(n == 0), stop=(n == 3 * KD - 1))
                                n += 1
                        if part == 1:
                            ins.then_inc(f_gu, 1)
                        if beside:
                            beside(2 * c + part)

                def down(job, c, wpar, tiles, free, signal):
                    fw = FCH[c][1]
                    pe.wait_ge(f_hlo, job * NF + (c + 1) + LO0)
                    for a in range(tiles):
                        if c == 0:
                            free(a)
                        for m, (hh, hw) in enumerate(HALVES):
                            ins = pe.matmul(bank[4 + a][:], hT[0:fw, hh, c, a * P:(a + 1) * P], d_hl[0:fw, wpar, hw, c],
                                            start=(c == 0 and m == 0), stop=(c == NF - 1 and m == 2))
                        if c == NF - 1:
                            ins.then_inc(signal, 1)

                n_acc = nf * 2 * SJ * TB
                transpose_x(range(2))
                for t in range(TB):
                    logits(t)
                    if t + 2 < TB:
                        transpose_x(range(t + 2, t + 3))
                transpose_x(PAIRS[0])
                for job in range(SJ):
                    b, wpar = job % 2, job // 2
                    x_of = lambda h, kc: xs[b][:, h, kc]
                    if job == 1:
                        pe.wait_ge(n_rcp, nf + 1)
                    if nm and b == 0:
                        pe.wait_ge(l_lo, TB + nm * NT)
                    else:
                        pe.wait_ge(b_lo0, nf * 2 * TB - nm * TB + (b + 1) * TB)
                    pe.wait_ge(f_wlo, (g0 + wpar) * 3 + 2)
                    for c in range(NF):
                        gate_up(j0 + job, c, (job * NF + c) % 2, wpar, x_of, D, beside=router if job == 0 else None)
                    if job == SJ - 1:
                        par = (SJ * NF) % 2
                        pe.wait_ge(t_xg[0], (nf * EVEN + 1) * 16)
                        pe.wait_ge(f_h, (j0 + job) * NF + 2 + H0)
                        transpose(par, xg[:, 0, 0], t_tp)
                        transpose(2 + par, xg[:, 0, 1], t_tp)

                    def free(a):
                        if job == 0 and a == 0:
                            pe.wait_ge(n_sh, nf + 1)
                            pe.wait_ge(n_cp, (nf + 1) * NT)
                        if job:
                            pe.wait_ge(f_acc, n_acc + (job - 1) * TB + a + 1)
                    pe.wait_ge(f_wlo, (g0 + wpar) * 3 + 3)
                    for c in range(NF):
                        down(j0 + job, c, wpar, TB, free, f_dn)
                        if job == 0 and c == NF - 1:
                            ranks()

                def tile(j, q, last):
                    job = j + (j0 + SJ)
                    x_of = lambda h, kc: xgT[:, q, h, kc]
                    pe.wait_ge(t_lo, (j + (nf * NTL + 1)) * 2)
                    pe.wait_ge(f_wlo, j * 3 + ((g0 + NS) * 3 + 2))
                    gate_up(job, 0, (q * NF) % 2, q, x_of, TS)
                    if not last:
                        if q == 0:
                            pe.wait_ge(t_xg[1], (i + (nf * ODD + 1)) * 16)
                        else:
                            pe.wait_ge(t_xg[0], (i + (nf * EVEN + 2)) * 16)
                        pe.wait_ge(t_lo, (j + (nf * NTL + 1)) * 2)
                        if q == 0:
                            pe.wait_ge(f_acc, n_acc + SJ * TB)
                        for a in range(2):
                            transpose(6 + a, xg[:, (q + 1) % 2, a], t_tp)
                    for c in (1, 2):
                        gate_up(job, c, (q * NF + c) % 2, q, x_of, TS)
                    if last:
                        pe.wait_ge(f_h, job * NF + 2 + H0)
                        for t, bk in zip(range(2 * TB, 3 * TB), LATE_BANKS):
                            transpose(bk, xn[:, t], b_tp)

                    def free(a):
                        pe.wait_ge(t_y, (j + nf * NTL - 1) * 2 + (a + 1 + Y0))
                    pe.wait_ge(f_wlo, j * 3 + ((g0 + NS) * 3 + 3))
                    for c in range(NF):
                        down(job, c, q, 2, free, t_dn)

                with pe.Fori(0, NTL // 2) as i:
                    for q in range(2):
                        tile(i * 2 + q, q, False)
                tile(NTL - 1, 0, True)

                for job in range(SJ):
                    b, wpar = SECOND[job], (1, 0)[job // 2]
                    to_mixer = job == SJ - 1 and PLAN[k + 1:k + 2] == ("mixer",)
                    v = (SJ + NTL + job) * NF
                    x_of = lambda h, kc: xs[(b + 1) % 2][:, h, kc]
                    pe.wait_ge(b_lo1, nf * 2 * TB + (b + 1) * TB)
                    pe.wait_ge(f_wlo, (g0 + NS + NTL + job // 2) * 3 + 2)

                    def first_block(half):
                        for q in {3: (0, 1), 5: (2, 3)}.get(half, ()):
                            pe.wait_ge(l_xn, q + 1)
                            pe.wait_ge(f_acc, n_acc + (SJ + job - 1) * TB + q + 1)
                            transpose(4 + q, xn_m[:, q % 2], l_tp)
                    for c in range(NF):
                        gate_up(j0 + SJ + NTL + job, c, (v + c) % 2, wpar, x_of, D, beside=first_block if to_mixer else None)
                    if job == 0:
                        pe.wait_ge(f_h, (j0 + SJ + NTL) * NF + 2 + H0)
                        for a in range(2):
                            transpose((v + 1) % 2 + 2 * a, xn[:, 3 * TB + a], b_tp)

                    def free(a):
                        if to_mixer:
                            pe.wait_ge(l_lo, a + 1)
                        elif job:
                            pe.wait_ge(f_acc, n_acc + (SJ + job - 1) * TB + a + 1)
                        elif a < 2:
                            pe.wait_ge(t_y, (nf + 1) * NTL * 2 + Y0)
                        else:
                            pe.wait_ge(b_lo1, nf * 2 * TB + TB)
                    pe.wait_ge(f_wlo, (g0 + NS + NTL + job // 2) * 3 + 3)
                    for c in range(NF):
                        if job == 0 and c == 2:
                            for a in range(2, 4):
                                pe.wait_ge(b_lo1, nf * 2 * TB + TB + a - 1)
                                transpose((v + 1) % 2 + 2 * (a % 2), xn[:, 3 * TB + a], b_tp)
                        down(j0 + SJ + NTL + job, c, wpar, TB, free, f_dn)

            def mixer(k):

                def turn(i):
                    after, settle = loop_waits(pe, i)

                    def y_features(n):
                        after(m_yg, n + 1, TPB)
                        for half in range(2):
                            for c in range(4):
                                ins = pe.transpose(bank[6 + half][:, c * P:(c + 1) * P],
                                                   y[:, n % 2, (4 * half + c) * P:(4 * half + c + 1) * P], ident[:])
                            ins.then_inc(m_F, 1)

                    def project(n):
                        if n % TB == 0:
                            pe.wait_ge(m_wo_lo0, 2)
                            pe.wait_ge(m_wo_lo1, 2)
                            after(m_dec, n // TB + 1, BPB)
                        after(m_res, n, TPB)
                        m = 0
                        for half in range(2):
                            after(m_ylo, 2 * n + half + 1, 2 * TPB)
                            for c in range(4 * half, 4 * half + 4):
                                for hy, hw in HALVES:
                                    ins = pe.matmul(bank[2][:], yT[:, hy, c], wo[:, hw, c],
                                                    start=(m == 0), stop=(m == 3 * KI - 1))
                                    m += 1
                        ins.then_inc(m_out, 1)

                    for j in range(BPB):
                        pe.wait_ge(l_lo, i * TPB + (j + 1) * TB)
                        for u in range(NWU):
                            w = j * NWU + u
                            after(m_wlo, w + 1, BPB * NWU)
                            wt = w_hl[:, w % 2]
                            if u < 5:
                                for c in (2 * u, 2 * u + 1):
                                    n = j * NCH + c
                                    if c < 2:
                                        after(m_L, HG * j * TB, HG * TPB)
                                        after(m_pre, j * NCH, BPB * NCH)
                                    else:
                                        after(m_pre, n - 1, BPB * NCH)
                                    m = 0
                                    for kc in range(KD):
                                        for hw, hx in HALVES:
                                            ins = pe.matmul(bank[c % 2][:], wt[:, hw, kc, (c % 2) * P:(c % 2 + 1) * P],
                                                            xb[:, hx, kc], start=(m == 0), stop=(m == 3 * KD - 1))
                                            m += 1
                                    ins.then_inc(m_cp, 1)
                                if u == 0 and j:
                                    y_features(j * TB - 1)
                                if u == 1 and j:
                                    project(j * TB - 1)
                                if u == 1:
                                    pe.wait_ge(m_wdt_lo, 1)
                                    for m, (kc, (hw, hx)) in enumerate([(c, h) for c in range(KD) for h in HALVES]):
                                        ins = pe.matmul(bank[3][0:HEADS, :], wdt[:, hw, kc], xb[:, hx, kc],
                                                        start=(m == 0), stop=(m == 3 * KD - 1))
                                    ins.then_inc(m_dtT, 1)
                                if u == 2:
                                    after(m_dtc, j + 1, BPB)
                                    after(m_res, j * TB, TPB)
                                    for q in range(TB):
                                        ins = pe.matmul(bank[2][:, q * HEADS:(q + 1) * HEADS], dtT[:, q * P:(q + 1) * P],
                                                        ident[0:HEADS, 0:HEADS], start=True, stop=True)
                                    ins.then_inc(m_dtp, 1)
                            else:
                                for half in range(2):
                                    n = j * 8 + (u - 5) * 2 + half
                                    if u == 5:
                                        wait_residual(pe, k)
                                        after(m_ylo, 2 * j * TB, 2 * TPB)
                                        after(m_yi, j * TB, TPB)
                                    else:
                                        after(m_z, n - 1, 8 * BPB)
                                    for q in (2 * half, 2 * half + 1):
                                        m = 0
                                        for kc in range(KD):
                                            for hx, hw in HALVES:
                                                ins = pe.matmul(bank[6 + half][:, (q % 2) * WU:(q % 2 + 1) * WU],
                                                                xb[:, hx, kc, q * P:(q + 1) * P], wt[:, hw, kc],
                                                                start=(m == 0), stop=(m == 3 * KD - 1))
                                                m += 1
                                    ins.then_inc(m_zp, 1)
                        after(m_ap, j + 1, BPB)
                        for dst, mat in ((1, tri_b), (2, ones_b)):
                            for p in range(3):
                                ins = pe.matmul(bank[2][:, dst * NQ:(dst + 1) * NQ], mat[:], aparts[:, p],
                                                start=(p == 0), stop=(p == 2))
                        ins.then_inc(m_cs, 1)

                        def decays(n, q, g):
                            if q == 0 and g < 2:
                                after(m_pre, (j + 1) * NCH, BPB * NCH)
                            else:
                                after(m_L, HG * n + g - 1, HG * TPB)
                            dst = bank[g % 2]
                            pe.matmul(dst[:].rearrange("p (h t) -> p h t", h=GH), ident_b[:], some(mask_b[:], GH),
                                      start=True, stop=False)
                            for h in range(GH):
                                col = q * HEADS + g * GH + h
                                for p in range(3):
                                    ins = pe.matmul(dst[:, h * P:(h + 1) * P],
                                                    aparts[:, p, col:col + 1].broadcast_to([P, P]), tri_b[:],
                                                    start=False, stop=(h == GH - 1 and p == 2))
                            ins.then_inc(m_B, 1)

                        for q in range(TB):
                            n = j * TB + q
                            tt = slice(q * P, (q + 1) * P)
                            decays(n, q, 0)
                            decays(n, q, 1)
                            if q == 0:
                                after(m_xc, (j + 1) * NCH, BPB * NCH)
                            after(m_Bt, n, TPB)
                            after(m_dtc, j + 1, BPB)
                            pe.wait_ge(l_lo, i * TPB + (n + TB))
                            pe.matmul(bank[3][:, 0:P], xc[:, 0, tt], xc[:, 1, tt], start=True, stop=True)
                            pe.transpose(bank[3][:, P:2 * P], xc[:, 0, tt], ident[:]).then_inc(m_G, 1)
                            after(m_S, n, TPB)
                            for half in range(2):
                                for c in range(4):
                                    ins = pe.transpose(bank[4 + half][:, c * P:(c + 1) * P],
                                                       xc[:, 2 + 4 * half + c, tt], ident[:])
                                ins.then_inc(m_xt, 1)
                            decays(n, q, 2)
                            if q >= 1:
                                y_features(n - 1)
                            decays(n, q, 3)
                            if q >= 1:
                                project(n - 1)
                            pe.wait_ge(m_zero, i + 1)
                            after(m_yi, n, TPB)
                            after(m_ylo, 2 * n, 2 * TPB)
                            if q == 0:
                                after(m_z, 8 * (j + 1), 8 * BPB)
                            for half in range(2):
                                ins = pe.matmul(bank[6 + half][:], xc[:, 1, tt], S[:, n % 2, half * 512:(half + 1) * 512],
                                                start=True, stop=True)
                            ins.then_inc(m_C, 1)
                            pe.wait_ge(l_xn, i * TPB + (n + TB + 1))
                            after(m_Bt, n + 1, TPB)
                            for c in range(KD):
                                ins = pe.transpose(bank[3][:, c * P:(c + 1) * P], xn_m[:, q % 2, c * P:(c + 1) * P],
                                                   ident[:])
                            ins.then_inc(l_tp, 1)
                            after(m_xw, n + 1, TPB)
                            after(m_xD, n + 1, TPB)
                            for half in range(2):
                                ins = pe.matmul(bank[4 + half][:], Bt, xw[:, half * 512:(half + 1) * 512],
                                                start=True, stop=True)
                            ins.then_inc(m_D, 1)
                            after(m_yc, n + 1, TPB)
                            for g in range(HG):
                                after(m_M, HG * n + g + 1, HG * TPB)
                                for h in range(g * GH, (g + 1) * GH):
                                    ins = pe.matmul(bank[6 + h // 8][:, (h % 8) * HD:(h % 8 + 1) * HD], L[:, h],
                                                    xdt[:, h * HD:(h + 1) * HD], start=True, stop=True)
                            ins.then_inc(m_E, 1)
                    y_features(TPB - 1)
                    project(TPB - 1)
                    settle((m_S, TPB), (m_L, HG * TPB), (m_pre, BPB * NCH), (m_res, TPB), (m_ylo, 2 * TPB),
                           (m_yi, TPB), (m_Bt, TPB), (m_z, 8 * BPB), (m_dec, BPB), (l_lo, TPB))

                with pe.Fori(0, BATCH) as i:
                    turn(i)

            for k, what in enumerate(PLAN):
                (ffn if what == "ffn" else mixer)(k)


def arrange(inputs):
    import numpy as np
    a = {k: np.asarray(v) for k, v in inputs.items()}

    def by_rows(w, rows=P):
        k = w.shape[-2] // rows
        return np.moveaxis(w.reshape(*w.shape[:-2], k, rows, w.shape[-1]), -3, -2)

    def experts(routed, shared):
        half = shared.shape[1] // NS
        return np.concatenate([routed, shared.reshape(D, NS, half).transpose(1, 0, 2)])

    x = a["L0_attn_u"].reshape(NT, P, D).transpose(1, 0, 2)
    w_in = a["L0_attn_W_in"].T
    units = np.concatenate([w_in[:, 2 * DI:2 * DI + 2 * P], w_in[:, DI:2 * DI], w_in[:, :DI]], axis=1)
    units = by_rows(units.reshape(D, NWU, WU).transpose(1, 0, 2))
    taps = np.concatenate([a["L0_attn_conv_w"].reshape(-1, TAPS), a["L0_attn_conv_b"][:, None]], axis=1)
    taps = np.concatenate([taps[DI:], taps[:DI]]).reshape(NCH, P, TAPS + 1).transpose(1, 0, 2)
    heads = np.concatenate([a["L0_attn_dt_bias"], a["L0_attn_A_log"], a["L0_attn_D"]])
    w_out = by_rows(a["L0_attn_W_out"].T)
    return {
        "x": x,
        "w_router": by_rows(a["L0_ffn_W_router"]),
        "w_gate": by_rows(experts(a["L0_ffn_We_gate"], a["L0_ffn_Ws_gate"])),
        "w_up": by_rows(experts(a["L0_ffn_We_up"], a["L0_ffn_Ws_up"])),
        "w_down": np.concatenate([a["L0_ffn_We_down"], a["L0_ffn_Ws_down"].reshape(NS, FE, D)]),
        "w_in": units,
        "w_dt": by_rows(w_in[:, 2 * DI + 2 * P:]),
        "conv": taps,
        "heads": np.broadcast_to(heads, (P, heads.size)),
        "norm_w": a["L0_attn_norm_w"].reshape(KI, P).T,
        "w_out": w_out.reshape(P, 4, 2, D).transpose(1, 0, 2, 3),
    }


def kernel(**inputs):
    import numpy as np
    import concourse.bacc as bacc
    from concourse.bass_utils import run_bass_kernel_spmd
    nc = bacc.Bacc("TRN2", target_bir_lowering=False, num_devices=1)
    arrays, args = {}, []
    for name, a in arrange(inputs).items():
        a = np.ascontiguousarray(a)
        arrays[f"in_{name}"] = a
        args.append(nc.dram_tensor(f"in_{name}", a.shape, mybir.dt.from_np(a.dtype), kind="ExternalInput").ap())
    out = nc.dram_tensor("out", (P, NT, D), mybir.dt.float32, kind="ExternalOutput").ap()
    program(nc, *args, out)
    got = run_bass_kernel_spmd(nc, [arrays], core_ids=[0]).results[0]["out"]
    return got.transpose(1, 0, 2).reshape(BATCH, TOK // BATCH, D)
```
